# Optimizing a Trainium2 kernel written in Bass

```python
import numpy as np
import jax
import jax.numpy as jnp

def _softmax(x, axis=-1):
    return jax.nn.softmax(x, axis=axis)

def _gelu(x):
    return jax.nn.gelu(x, approximate=True)

def _silu(x):
    return jax.nn.silu(x)

def _sigmoid(x):
    return jax.nn.sigmoid(x)

def _layernorm(x, axis=-1, eps=1e-05):
    m = jnp.mean(x, axis=axis, keepdims=True)
    v = jnp.var(x, axis=axis, keepdims=True)
    return (x - m) / jnp.sqrt(v + eps)

def _scatter_add(tgt, idx, src, axis=0):
    return tgt.at[idx].add(src)

def _segment_sum(src, seg, n):
    return jax.ops.segment_sum(src, seg, n)
kernel_name = 'mk_gnn_ffn_d1_gnn_r8_1e5756'

def setup_inputs(seed: int=0):
    np.random.seed(seed)
    _w = jnp.asarray

    def _rec_inputs():
        import jax
        import jax.numpy as jnp
        _gk = jax.random.key(seed)
        x = -0.0003713 + 1 * jax.random.normal(jax.random.fold_in(_gk, 1), (6250, 256), jnp.float32)
        src = jax.random.randint(jax.random.fold_in(_gk, 2), (100000,), 0, 6250, jnp.int32)
        dst = jax.random.randint(jax.random.fold_in(_gk, 3), (100000,), 0, 6250, jnp.int32)
        _o = jnp.argsort(dst, stable=True)
        src = src[_o]
        dst = dst[_o]
        return (x, src, dst)
    x, src, dst = _rec_inputs()

    def _L0_gnn_setup():
        import jax, jax.numpy as jnp
        import numpy as np
        ALPHA = 0.2
        LN_EPS = 1e-05

        def _gat_layer(x, src, dst, W, b, a, g, beta, N, concat):
            h = x @ W.T + b
            d = W.shape[0]
            s_src = h @ a[:d]
            s_dst = h @ a[d:]
            score = s_src[src] + s_dst[dst]
            e = jnp.exp(-jax.nn.leaky_relu(score, ALPHA))
            h_prime = jax.ops.segment_sum(e[:, None] * h[dst], src, num_segments=N)
            mu = jnp.mean(h_prime, axis=-1, keepdims=True)
            var = jnp.var(h_prime, axis=-1, keepdims=True)
            h_prime = (h_prime - mu) * jax.lax.rsqrt(var + LN_EPS) * g + beta
            return jax.nn.elu(h_prime) if concat else h_prime
        key = jax.random.key(seed)
        ks = jax.random.split(key, 13)
        N, E, F, D, H = (6250, 100000, 256, 64, 8)
        S = 0.02
        inp = {'embeds': jax.random.normal(ks[0], (N, F), dtype=jnp.float32), 'W_heads': jax.random.normal(ks[1], (H, D, F), dtype=jnp.float32) * S, 'b_heads': jax.random.normal(ks[2], (H, D), dtype=jnp.float32) * S, 'a_heads': jax.random.normal(ks[3], (H, 2 * D), dtype=jnp.float32) * S, 'g_heads': jnp.ones((H, D), dtype=jnp.float32), 'beta_heads': jnp.zeros((H, D), dtype=jnp.float32), 'W_out': jax.random.normal(ks[4], (F, D * H), dtype=jnp.float32) * S, 'b_out': jax.random.normal(ks[5], (F,), dtype=jnp.float32) * S, 'a_out': jax.random.normal(ks[6], (2 * F,), dtype=jnp.float32) * S, 'g_out': jnp.ones((F,), dtype=jnp.float32), 'beta_out': jnp.zeros((F,), dtype=jnp.float32), 'edge_index': jax.random.randint(ks[7], (2, E), 0, N, dtype=jnp.int32)}
        return inp
    _L0_gnn_all = _L0_gnn_setup()
    _L0_gnn_in = {k: v for k, v in _L0_gnn_all.items() if k in ('W_heads', 'b_heads', 'a_heads', 'g_heads', 'beta_heads', 'W_out', 'b_out', 'a_out', 'g_out', 'beta_out')}
    del _L0_gnn_all

    def _L0_ffn_setup():
        import jax, jax.numpy as jnp
        import numpy as np
        C = 256
        HID = 1024
        E = 8
        TEMP = 1.0
        key = jax.random.key(seed)
        ks = jax.random.split(key, 7)
        x = jax.random.normal(ks[0], (8, 2048, C), dtype=jnp.float32)
        W1 = jax.random.normal(ks[1], (C, HID), dtype=jnp.float32) * 0.02
        b1 = jnp.zeros((HID,), dtype=jnp.float32)
        Wg = jax.random.normal(ks[2], (HID, E), dtype=jnp.float32) * 0.02
        bg = jnp.zeros((E,), dtype=jnp.float32)
        Wd = jax.random.normal(ks[3], (E, HID, C), dtype=jnp.float32) * 0.02
        bd = jnp.zeros((E, C), dtype=jnp.float32)
        return {'x': x, 'W1': W1, 'b1': b1, 'Wg': Wg, 'bg': bg, 'Wd': Wd, 'bd': bd}
    _L0_ffn_all = _L0_ffn_setup()
    _L0_ffn_in = {k: v for k, v in _L0_ffn_all.items() if k in ('W1', 'b1', 'Wg', 'bg', 'Wd', 'bd')}
    del _L0_ffn_all
    return {'x': x, 'src': src, 'dst': dst, 'L0_gnn_W_heads': _L0_gnn_in['W_heads'], 'L0_gnn_b_heads': _L0_gnn_in['b_heads'], 'L0_gnn_a_heads': _L0_gnn_in['a_heads'], 'L0_gnn_g_heads': _L0_gnn_in['g_heads'], 'L0_gnn_beta_heads': _L0_gnn_in['beta_heads'], 'L0_gnn_W_out': _L0_gnn_in['W_out'], 'L0_gnn_b_out': _L0_gnn_in['b_out'], 'L0_gnn_a_out': _L0_gnn_in['a_out'], 'L0_gnn_g_out': _L0_gnn_in['g_out'], 'L0_gnn_beta_out': _L0_gnn_in['beta_out'], 'L0_ffn_W1': _L0_ffn_in['W1'], 'L0_ffn_b1': _L0_ffn_in['b1'], 'L0_ffn_Wg': _L0_ffn_in['Wg'], 'L0_ffn_bg': _L0_ffn_in['bg'], 'L0_ffn_Wd': _L0_ffn_in['Wd'], 'L0_ffn_bd': _L0_ffn_in['bd']}

def reference(x, src, dst, L0_gnn_W_heads, L0_gnn_b_heads, L0_gnn_a_heads, L0_gnn_g_heads, L0_gnn_beta_heads, L0_gnn_W_out, L0_gnn_b_out, L0_gnn_a_out, L0_gnn_g_out, L0_gnn_beta_out, L0_ffn_W1, L0_ffn_b1, L0_ffn_Wg, L0_ffn_bg, L0_ffn_Wd, L0_ffn_bd):
    import jax
    import jax.numpy as jnp

    def _L0_gnn_ref(embeds, W_heads, b_heads, a_heads, g_heads, beta_heads, W_out, b_out, a_out, g_out, beta_out, edge_index):
        import jax, jax.numpy as jnp
        import numpy as np
        ALPHA = 0.2
        LN_EPS = 1e-05

        def _gat_layer(x, src, dst, W, b, a, g, beta, N, concat):
            h = x @ W.T + b
            d = W.shape[0]
            s_src = h @ a[:d]
            s_dst = h @ a[d:]
            score = s_src[src] + s_dst[dst]
            e = jnp.exp(-jax.nn.leaky_relu(score, ALPHA))
            h_prime = jax.ops.segment_sum(e[:, None] * h[dst], src, num_segments=N)
            mu = jnp.mean(h_prime, axis=-1, keepdims=True)
            var = jnp.var(h_prime, axis=-1, keepdims=True)
            h_prime = (h_prime - mu) * jax.lax.rsqrt(var + LN_EPS) * g + beta
            return jax.nn.elu(h_prime) if concat else h_prime
        N = embeds.shape[0]
        src, dst = (edge_index[0], edge_index[1])
        H = W_heads.shape[0]
        heads = [_gat_layer(embeds, src, dst, W_heads[i], b_heads[i], a_heads[i], g_heads[i], beta_heads[i], N, concat=True) for i in range(H)]
        x = jnp.concatenate(heads, axis=1)
        out = _gat_layer(x, src, dst, W_out, b_out, a_out, g_out, beta_out, N, concat=False)
        return jax.nn.elu(out)

    def _L0_ffn_ref(x, W1, b1, Wg, bg, Wd, bd):
        import jax, jax.numpy as jnp
        import numpy as np
        C = 256
        HID = 1024
        E = 8
        TEMP = 1.0
        orig_shape = x.shape
        xf = x.reshape(-1, orig_shape[-1])
        H = jax.nn.gelu(xf @ W1 + b1, approximate=False)
        probs = jax.nn.softmax((H @ Wg + bg) / TEMP, axis=-1)
        assign = jnp.argmax(probs, axis=-1)
        out = jnp.zeros_like(xf)
        for e in range(Wd.shape[0]):
            y = H @ Wd[e] + bd[e]
            sel = (assign == e)[:, None]
            out = out + jnp.where(sel, probs[:, e:e + 1] * y, 0.0)
        return out.reshape(orig_shape)
    edge_index = jnp.stack([src, dst])
    x = x + _L0_gnn_ref(_layernorm(x, axis=-1), L0_gnn_W_heads, L0_gnn_b_heads, L0_gnn_a_heads, L0_gnn_g_heads, L0_gnn_beta_heads, L0_gnn_W_out, L0_gnn_b_out, L0_gnn_a_out, L0_gnn_g_out, L0_gnn_beta_out, edge_index)
    x = x + _L0_ffn_ref(_layernorm(x, axis=-1)[None], L0_ffn_W1, L0_ffn_b1, L0_ffn_Wg, L0_ffn_bg, L0_ffn_Wd, L0_ffn_bd)[0]
    return x

_drawn_inputs = setup_inputs


def setup_inputs(seed=0):
    import zlib

    import numpy as np

    out = dict(_drawn_inputs(seed))
    spreads = {'L0_gnn_g_heads': (1.0, 0.2),
     'L0_gnn_beta_heads': (0.0, 0.1),
     'L0_gnn_g_out': (1.0, 0.2),
     'L0_gnn_beta_out': (0.0, 0.1),
     'L0_ffn_b1': (0.0, 0.652),
     'L0_ffn_bg': (0.0, 0.504),
     'L0_ffn_bd': (0.0, 0.752)}
    factors = {'L0_ffn_W1': 3.436, 'L0_ffn_Wg': 3.615, 'L0_ffn_Wd': 4.263}
    for name, (base, spread) in spreads.items():
        noise = np.random.default_rng([zlib.crc32(name.encode()), seed]).standard_normal(out[name].shape)
        drawn = base * np.exp(spread * noise) if base else spread * noise
        out[name] = jnp.asarray(drawn.astype(out[name].dtype))
    for name, factor in factors.items():
        out[name] = (out[name] * factor).astype(out[name].dtype)
    return out
```

```python
from contextlib import ExitStack

import concourse.bass as bass
from concourse import mybir

P = 128
F32 = mybir.dt.float32
I32 = mybir.dt.int32
U32 = mybir.dt.uint32
ALU = mybir.AluOpType
ACT = mybir.ActivationFunctionType
AX = mybir.AxisListType

ONE_TAG = 0x40000000
DST_BITS = 13
PAD_DST = (1 << DST_BITS) - 1
LN_EPS = 1e-5
LEAK = 0.2


def build(nc, x, src, dst, W_heads, b_heads, a_heads, g_heads, beta_heads, W_out, b_out, a_out, g_out, beta_out,
          W1, b1, Wg, bg, Wd, bd, out):
    N, C = x.shape
    E = src.shape[0]
    H, D, _ = W_heads.shape
    HD = H * D
    HID = W1.shape[1]
    NE = Wg.shape[1]
    NT = -(-N // P)
    LASTP = N - (NT - 1) * P
    KF = C // P
    KH = HD // P
    HR = HD + H
    HR2 = C + 4
    MC = HID // P

    EP = 125
    EC = E // EP
    SC = 1024
    PC = SC - EC
    FB = SC.bit_length() - 1
    GT = 2
    UG = 8
    NG = -(-((E + NT * (GT * P - 1)) // (GT * P)) // UG) * UG
    NTL = NG * GT
    US = UG * GT
    SURPLUS = ((NT * P + P - 1) << DST_BITS) | PAD_DST | ONE_TAG
    assert EP * EC == E and P * PC >= NT * (GT * P - 1) and NTL <= SC and N <= NT * P < PAD_DST

    TC = 64
    TFB = TC.bit_length() - 1
    TPC = TC - NT
    BT = 4
    NB1 = -(-NT // BT)
    NB2 = -(-((N + NE * (P - 1)) // P) // BT)
    TT = NB2 * BT
    T_SURPLUS = (NE << DST_BITS) | PAD_DST | ONE_TAG
    assert P * TPC >= NE * (P - 1) and TT <= TC and NB2 % 2 == 0 and NB1 % 2 == 1
    XR = 2 * C + 2

    with ExitStack() as ctx:
        def sb(name, shape, dt=F32):
            return ctx.enter_context(nc.sbuf_tensor(name, shape, dt))

        def ps(name, shape, dt=F32):
            return ctx.enter_context(nc.psum_tensor(name, shape, dt))

        def sem(name):
            return ctx.enter_context(nc.semaphore(name))

        h1_dram = nc.dram_tensor("h1_rows", (NT * P, HR), F32, kind="Internal").ap()
        h2_dram = nc.dram_tensor("h2_rows", (NT * P, HR2), F32, kind="Internal").ap()
        tok_dram = nc.dram_tensor("token_rows", (NT * P, XR), F32, kind="Internal").ap()
        order_dram = nc.dram_tensor("token_order", (P * TC,), F32, kind="Internal").ap()

        WD0 = (NT + 1) * C
        arena = sb("arena", [P, max((NT + 1) * HD, WD0 + NE * MC * C)])
        xn = arena[:, 0:NT * C].rearrange("p (t f) -> p t f", t=NT)
        wraw = arena[:, NT * C:NT * C + KH * C].rearrange("p (c f) -> p c f", c=KH)
        wo0 = NT * C + KH * C
        woraw = arena[:, wo0:wo0 + KF * HD].rearrange("p (m f) -> p m f", m=KF)
        wd_sb = arena[:, WD0:WD0 + NE * MC * C]
        work = sb("work", [P, US * HR])
        got1 = work[:, :].rearrange("p (s r) -> p s r", s=US)
        got2 = work[:, 0:US * HR2].rearrange("p (s r) -> p s r", s=US)
        srcdst = work[:, 0:2 * EC].bitcast(I32).rearrange("p (a c) -> p a c", a=2)
        srcf = work[:, 2 * EC:3 * EC]
        padno = work[:, 3 * EC:3 * EC + PC].bitcast(I32)
        padnof = work[:, 3 * EC + PC:3 * EC + 2 * PC]
        padwin = work[:, 3 * EC + 2 * PC:3 * EC + 3 * PC]
        padwini = work[:, 3 * EC + 3 * PC:3 * EC + 4 * PC].bitcast(I32)

        def ring(n, width, depth=2):
            return work[:, n:n + depth * width].rearrange("p (s w) -> p s w", s=depth)

        sq = ring(0, HD)
        ex1 = ring(2 * HD, HD)
        re1 = ring(4 * HD, HD)
        u1 = ring(6 * HD, HD)
        x1s = ring(8 * HD, HD)
        yb = ring(0, C)
        zb = ring(2 * C, C)
        ex2 = ring(4 * C, C)
        re2 = ring(6 * C, C)
        u2 = ring(8 * C, C)
        xre = ring(10 * C, C)
        yg = ring(12 * C, C)
        hT = work[:, 0:MC * BT * P].rearrange("p (c q) -> p c q", c=MC)
        tok = work[:, MC * BT * P:MC * BT * P + 2 * BT * XR].rearrange("p (s r) -> p s r", s=2 * BT)
        xn2 = work[:, MC * BT * P:MC * BT * P + 2 * BT * C].rearrange("p (s r) -> p s r", s=2 * BT)
        lg = work[:, MC * BT * P + 2 * BT * C:MC * BT * P + 2 * BT * C + NT * NE].rearrange("p (t e) -> p t e", t=NT)
        lgx = work[:, 0:NT * NE].rearrange("p (t e) -> p t e", t=NT)
        assert MC * BT * P + 2 * BT * XR <= US * HR and MC * BT * P + 2 * BT * C + NT * NE <= US * HR

        ident = sb("ident", [P, P])
        iota = sb("iota", [P, P])
        iotai = work[:, 3 * EC + 4 * PC:3 * EC + 4 * PC + P].bitcast(I32)
        ones = sb("ones", [P, P])
        wT = sb("wT", [P, KF, HD + 2 * H])
        amat = sb("amat", [P, KH, 2 * H])
        bcol = sb("bcol", [P, KH])
        brow = sb("brow", [1, HD + 2 * H])
        woT = sb("woT", [P, KH, C + 2])
        a2 = sb("a2", [P, KF, 2])
        bocol = sb("bocol", [P, KF])
        brow2 = sb("brow2", [1, C + 2])
        gcol = sb("gcol", [P, KH])
        becol = sb("becol", [P, KH])
        goutb = sb("goutb", [P, C])
        beoutb = sb("beoutb", [P, C])
        stats = sb("stats", [P, NT, 6])
        mean = sb("mean", [P, NT])
        var = sb("var", [P, NT])
        rstd = sb("rstd", [P, NT])
        tmp = sb("tmp", [P, NT])
        headsum = sb("headsum", [P, 2, H])
        xnT = sb("xnT", [P, 2, KF, P])
        hrow = sb("hrow", [P, 2, HR])
        s_tab = sb("s_tab", [P, (NT + 1) * H])
        s_tab2 = sb("s_tab2", [P, NT + 1])

        keys = [sb("keys_a", [P, SC]), sb("keys_b", [P, SC])]
        var1, rstd1 = (keys[0][:, n * NT * H:(n + 1) * NT * H] for n in range(2))
        tmp1 = keys[1][:, 0:NT * H]
        xT = [k[:, :].rearrange("p (k q) -> p k q", k=KF) for k in keys]
        cnt = sb("cnt", [P, NT])
        tot = sb("tot", [P, NT + 1])
        toti = sb("toti", [P, NT], I32)
        padf = sb("padf", [P, NT])
        padcum = sb("padcum", [P, NT])
        zeros = sb("zeros", [P, NT])
        sgn = sb("sgn", [P, 1])
        sgni = sb("sgni", [P, 1], I32)
        dst_idx = sb("dst_idx", [P, NTL], I32)
        src_lo = sb("src_lo", [P, NTL])
        win_i = sb("win_i", [P, NG], I32)
        staged = sb("staged", [P, 2, US // 2], I32)

        hot = sb("hot", [P, 4, GT, P])
        hotT = sb("hotT", [P, 2, GT, P])
        score = sb("score", [P, 4, GT, H])
        lrel = sb("lrel", [P, 4, GT, H])
        ew = sb("ew", [P, 4, GT, H])
        scaled = sb("scaled", [P, 2 * GT * HD])
        scaled1 = scaled[:, :].rearrange("p (s u f) -> p s u f", s=2, u=GT)
        scaled2 = scaled[:, 0:2 * GT * P].rearrange("p (s u f) -> p s u f", s=2, u=GT)
        w1_sb = scaled[:, :].rearrange("p (k f) -> p k f", k=KF)
        assert 2 * GT * HD == KF * HID

        b1c = sb("b1c", [P, MC])
        wg_sb = sb("wg_sb", [P, MC, NE])
        bg_sb = sb("bg_sb", [1, NE])
        eiota = sb("eiota", [P, NE])
        lgmax = sb("lgmax", [P, NT])
        prob = sb("prob", [P, NT])
        pick = sb("pick", [P, NT])
        cnt_e = sb("cnt_e", [P, NE])
        tokno = sb("tokno", [P, NT], I32)
        picki = sb("picki", [P, NT], I32)
        tpadno = sb("tpadno", [P, TPC], I32)
        tpadnof = sb("tpadnof", [P, TPC])
        tpadwin = sb("tpadwin", [P, TPC])
        tpadwini = sb("tpadwini", [P, TPC], I32)
        hotf = hot[:, :, :, :].rearrange("p a b c -> p (a b c)")
        tkeys = [hotf[:, n * P:(n + 1) * P] for n in range(2)]
        tord, tok_to, tok_from, exp_i, exp_c, exp_b = (hotf[:, 2 * P + n * TC:2 * P + (n + 1) * TC].bitcast(I32) for n in range(6))
        st_from = sb("st_from", [P, 2, BT], I32)
        st_to = sb("st_to", [P, 2, BT], I32)
        orow = arena[:, 0:2 * BT * C].rearrange("p (s c) -> p s c", s=2 * BT)
        bd_sb = arena[0:1, 2 * BT * C:(2 * BT + NE) * C]

        big = ps("big", [P, 4, 512])
        tps = ps("tps", [P, 2, 512])
        keyps = ps("keyps", [P, 2, 512])

        x_in, w_in, edges_in, zero_x, consts = sem("x_in"), sem("w_in"), sem("edges_in"), sem("zero_x"), sem("consts")
        dve, pool_own = sem("dve"), sem("pool_own")
        sqrt_asked, sqrt_done, xn_ready = sem("sqrt_asked"), sem("sqrt_done"), sem("xn_ready")
        rstd_done = sem("rstd_done")
        wt_mm, wt_ready, bh_in = sem("wt_mm"), sem("wt_ready"), sem("bh_in")
        xt_mm, xt_ready, h_mm, h_ready = sem("xt_mm"), sem("xt_ready"), sem("h_mm"), sem("h_ready")
        s_ready = sem("s_ready")
        h_stored = [sem("h_stored0"), sem("h_stored1")]
        cnt_ready, cnt_mm, turn_asked, turned = sem("cnt_ready"), sem("cnt_mm"), sem("turn_asked"), sem("turned")
        acc_zero, sorted_ = sem("acc_zero"), sem("sorted")

        class Agg:
            def __init__(self, n):
                self.staged = sem(f"idx_staged{n}")
                self.got = [sem(f"got{n}_{c}") for c in range(US)]
                self.hot = sem(f"hot{n}")
                self.hotT_mm = sem(f"hotT_mm{n}")
                self.hotT = sem(f"hotT{n}")
                self.src_mm = sem(f"src_mm{n}")
                self.score = sem(f"score{n}")
                self.lrel = sem(f"lrel{n}")
                self.exp = sem(f"exp{n}")
                self.scaled = sem(f"scaled{n}")
                self.mm = sem(f"agg_mm{n}")
                self.added = sem(f"added{n}")

        agg = [Agg(1), Agg(2)]

        sums, centred, squared, sq_added = sem("sums"), sem("centred"), sem("squared"), sem("sq_added")
        x1_scaled, x1t_mm, elu_act, elu_u, h2_mm, h2_ready = (sem("x1_scaled"), sem("x1t_mm"), sem("elu_act"),
                                                              sem("elu_u"), sem("h2_mm"), sem("h2_ready"))
        s2_ready = sem("s2_ready")
        h2_stored = [sem("h2_stored0"), sem("h2_stored1")]
        xre_in = [sem("xre_in0"), sem("xre_in1")]
        w1_in, wd_in, sum_done = sem("w1_in"), sem("wd_in"), sem("sum_done")
        y_norm, y_g, z_ready, elu2_act, u2_done, x2_done = (sem("y_norm"), sem("y_g"), sem("z_ready"), sem("elu2_act"),
                                                            sem("u2_done"), sem("x2_done"))
        xn2_ready, xn2T_mm, xn2T_ready = sem("xn2_ready"), sem("xn2T_mm"), sem("xn2T_ready")
        up_mm, up_ready, lg_mm, lg_ready = sem("up_mm"), sem("up_ready"), sem("lg_mm"), sem("lg_ready")
        tok_stored = [sem("tok_stored0"), sem("tok_stored1")]
        lexp_asked, lexp_done, prob_ready, prob_stored = (sem("lexp_asked"), sem("lexp_done"), sem("prob_ready"),
                                                          sem("prob_stored"))
        order_ready, order_out, order_in, order_dec = (sem("order_ready"), sem("order_out"), sem("order_in"),
                                                       sem("order_dec"))
        st_done = sem("st_done")
        tok_in = [sem(f"tok_in{c}") for c in range(2 * BT)]
        xt2_mm, xt2_ready, up2_mm, up2_ready = sem("xt2_mm"), sem("xt2_ready"), sem("up2_mm"), sem("up2_ready")
        y_mm, o_ready, sto_done, out_done = sem("y_mm"), sem("o_ready"), sem("sto_done"), sem("out_done")

        def wait(eng, s, n):
            if not (isinstance(n, int) and n <= 0):
                eng.wait_ge(s, n)

        def pool_wait(s, n):
            wait(nc.gpsimd, s, n)
            if not isinstance(n, int):
                nc.gpsimd.sem_inc(pool_gate, 1)

        def is_in(t, n):
            return not isinstance(t, int) or 0 <= t < n

        def steps(eng, n, extra, step):
            step(0, 0)
            step(1, 1)
            m = n // 2
            with eng.Fori(1, m) as i:
                step(2 * i, 0)
                step(2 * i + 1, 1)
            for t in range(2 * m, n + extra):
                step(t, t % 2)

        def group_steps(eng, step):
            for g in range(-3, UG):
                step(g, g % UG)
            with eng.Fori(1, NG // UG - 1) as i:
                for j in range(UG):
                    step(UG * i + j, j)
            for g in range(NG - UG, NG):
                step(g, g % UG)

        def cols(t, width):
            return bass.ds(t * width, width)

        def buffers_turned(fb):
            at, read = 0, []
            for k in range(1, fb + 8):
                if k <= fb:
                    at ^= k & 1
                    continue
                read.append(at)
                at ^= 1 ^ ((k - min(fb, 7)) & 1)
                read.append(at)
                at ^= 1 ^ (min(fb, 7) & 1)
            return read, at

        E_TURNS, E_END = buffers_turned(FB)
        E_TURNS = E_TURNS + [E_END]
        T_TURNS, T_END = buffers_turned(TFB)
        pool_gate = sem("pool_gate")
        br2_ready, y_batch, bd_in = sem("br2_ready"), sem("y_batch"), sem("bd_in")
        prob2 = sb("prob2", [P, NT, 2])

        chain = [0]
        block = ctx.enter_context(nc.Block())

        @block.sync
        def _(sp):
            sp.dma_start(srcdst[0:EP, 0, :], src.rearrange("(p c) -> p c", p=EP)).then_inc(edges_in, 16)
            sp.dma_start(srcdst[0:EP, 1, :], dst.rearrange("(p c) -> p c", p=EP)).then_inc(edges_in, 16)
            sp.wait_ge(zero_x, 2)
            sp.dma_start(xn[:, 0:NT - 1, :], x[0:(NT - 1) * P, :].rearrange("(t p) f -> p t f", p=P)).then_inc(x_in, 16)
            sp.dma_start(xn[0:LASTP, NT - 1, :], x[(NT - 1) * P:N, :]).then_inc(x_in, 16)
            sp.dma_start(wraw, W_heads.rearrange("h d f -> (h d) f").rearrange("(c p) f -> p c f", p=P)).then_inc(w_in, 16)
            sp.dma_start(woraw, W_out.rearrange("(m p) f -> p m f", p=P)).then_inc(w_in, 16)

            def column(to, v):
                sp.dma_start(to, v.rearrange("(c p) -> p c", p=P), allow_slow_non_contiguous=True).then_inc(w_in, 16)

            column(bcol[:, :], b_heads.rearrange("h d -> (h d)"))
            column(gcol[:, :], g_heads.rearrange("h d -> (h d)"))
            column(becol[:, :], beta_heads.rearrange("h d -> (h d)"))
            column(bocol[:, :], b_out)
            column(b1c[:, :], b1)
            for s in range(2):
                column(a2[:, :, s], a_out[s * C:(s + 1) * C])
            for h in range(H):
                lo = (h * D) % P
                for s in range(2):
                    sp.dma_start(amat[lo:lo + D, h * D // P, s * H + h:s * H + h + 1],
                                 a_heads[h, s * D:(s + 1) * D].rearrange("(d o) -> d o", o=1),
                                 allow_slow_non_contiguous=True).then_inc(w_in, 16)
            sp.dma_start(wg_sb[:, :, :], Wg.rearrange("(c p) e -> p c e", p=P)).then_inc(w_in, 16)
            sp.dma_start(bg_sb[:, :], bg.rearrange("(o e) -> o e", o=1)).then_inc(w_in, 16)
            for to, v in ((goutb, g_out), (beoutb, beta_out)):
                sp.dma_start(to[:, :], v.rearrange("(o n) -> o n", o=1).broadcast_to([P, C])).then_inc(w_in, 16)

            def store1(t, j):
                wait(sp, h_ready, t + 1)
                sp.dma_start(h1_dram[cols(t, P), :], hrow[:, j, :]).then_inc(h_stored[j], 16)

            steps(sp, NT, 0, store1)

            def store2(t, j):
                wait(sp, h2_ready, t + 1)
                sp.dma_start(h2_dram[cols(t, P), :], hrow[:, j, 0:HR2]).then_inc(h2_stored[j], 16)

            steps(sp, NT, 0, store2)
            sp.wait_ge(h2_mm, NT)
            for e in range(NE):
                sp.dma_start(wd_sb[:, e * MC * C:(e + 1) * MC * C].rearrange("p (c f) -> p c f", c=MC),
                             Wd[e].rearrange("(c p) f -> p c f", p=P)).then_inc(wd_in, 16)
            sp.wait_ge(agg[1].mm, NG)
            sp.dma_start(w1_sb, W1.rearrange("(k p) f -> p k f", p=P)).then_inc(w1_in, 16)

            def reload(t, j):
                wait(sp, x2_done, t - 1)
                if isinstance(t, int) and t == NT - 1:
                    sp.dma_start(xre[0:LASTP, j, :], x[(NT - 1) * P:N, :]).then_inc(xre_in[j], 16)
                else:
                    sp.dma_start(xre[:, j, :], x[cols(t, P), :]).then_inc(xre_in[j], 16)

            steps(sp, NT, 0, reload)

            def store_tok(b, j):
                for q in range(BT if not isinstance(b, int) or b < NB1 - 1 else NT - BT * (NB1 - 1)):
                    t = BT * b + q
                    wait(sp, xn2_ready, t + 1)
                    sp.dma_start(tok_dram[cols(t, P), 0:C], arena[:, cols(t, C)]).then_inc(tok_stored[j], 16)
                    sp.dma_start(tok_dram[cols(t, P), C:2 * C], xn2[:, BT * j + q, :]).then_inc(tok_stored[j], 16)

            steps(sp, NB1, 0, store_tok)
            sp.wait_ge(prob_ready, 1)
            sp.dma_start(tok_dram.rearrange("(t p) r -> p t r", p=P)[:, :, 2 * C:2 * C + 2],
                         prob2[:, :, :]).then_inc(prob_stored, 16)
            sp.wait_ge(tok_stored[0], 32 * (NT - BT * (NB1 // 2)))
            sp.wait_ge(tok_stored[1], 32 * BT * (NB1 // 2))
            sp.dma_start(bd_sb, bd.rearrange("(o e) c -> o (e c)", o=1)).then_inc(bd_in, 16)
            sp.wait_ge(order_ready, 1)
            sp.dma_start(order_dram.rearrange("(p c) -> p c", p=P), tkeys[T_END][:, 0:TC]).then_inc(order_out, 16)
            sp.wait_ge(order_out, 16)
            sp.dma_start(tord[:, :].bitcast(F32), order_dram.rearrange("(c p) -> p c", p=P),
                         allow_slow_non_contiguous=True).then_inc(order_in, 16)
            sp.wait_ge(out_done, 16 * TT)

        @block.gpsimd
        def _(pool):
            pool.memset(xn[:, NT - 1, :], 0.0).then_inc(zero_x, 1)
            pool.memset(amat[:, :, :], 0.0).then_inc(zero_x, 1)
            pool.memset(ones[:, :], 1.0).then_inc(consts, 1)
            pool.memset(ident[:, :], 0.0).then_inc(pool_own, 1)
            pool.wait_ge(pool_own, 1)
            pool.affine_select(out=ident[:, :], in_=ident[:, :], compare_op=ALU.not_equal, fill=1.0, base=0,
                               pattern=[[-1, P]], channel_multiplier=1).then_inc(consts, 1)
            pool.iota(padno, pattern=[[1, PC]], base=0, channel_multiplier=PC).then_inc(consts, 1)
            pool.iota(tpadno[:, :], pattern=[[1, TPC]], base=0, channel_multiplier=TPC).then_inc(consts, 1)
            pool.iota(tokno[:, :], pattern=[[P, NT]], base=0, channel_multiplier=1).then_inc(consts, 1)
            pool.iota(sgni[:, :], pattern=[[0, 1]], base=0, channel_multiplier=1).then_inc(consts, 1)
            pool.iota(iotai[:, :], pattern=[[1, P]], base=0, channel_multiplier=0).then_inc(consts, 1)
            pool.memset(s_tab[:, NT * H:(NT + 1) * H], 0.0).then_inc(consts, 1)
            pool.memset(s_tab2[:, NT:NT + 1], 0.0).then_inc(consts, 1)
            pool.memset(hrow[:, :, :], 0.0).then_inc(consts, 1)
            pool.wait_ge(rstd_done, 1)

            def norm(t, j):
                tile = arena[:, cols(t, C)]
                pool.tensor_scalar(tile, tile, mean[:, cols(t, 1)], rstd[:, cols(t, 1)],
                                   ALU.subtract, ALU.mult).then_inc(xn_ready, 1)

            for t in range(NT):
                norm(t, 0)

            def gathers(a, table, rows, width, used):
                def turn(i):
                    for half in range(2):
                        lo = half * (US // 2)
                        first = UG * i + half * (UG // 2)
                        pool_wait(used, first - UG // 2)
                        pool.tensor_copy(staged[:, half, :], dst_idx[:, bass.ds(US * i + lo, US // 2)]).then_inc(a.staged, 1)
                        pool_wait(a.staged, 2 * i + half + 1)
                        for c in range(lo, lo + US // 2):
                            pool.indirect_dma_start(rows[:, c, 0:width], None, table[:, :],
                                                    bass.IndirectOffsetOnAxis(ap=staged[:, half, c - lo:c - lo + 1].bitcast(U32),
                                                                              axis=0)).then_inc(a.got[c], 16)
                turn(0)
                with pool.Fori(1, NG // UG) as i:
                    turn(i)

            pool.wait_ge(sorted_, 1)
            pool.wait_ge(h_stored[0], 16 * ((NT + 1) // 2))
            pool.wait_ge(h_stored[1], 16 * (NT // 2))
            gathers(agg[0], h1_dram, got1, HR, agg[0].scaled)
            pool.wait_ge(h2_stored[0], 16 * ((NT + 1) // 2))
            pool.wait_ge(h2_stored[1], 16 * (NT // 2))
            gathers(agg[1], h2_dram, got2, HR2, agg[1].mm)

            def affine2(t, j):
                pool_wait(y_norm, t + 1)
                pool_wait(z_ready, t - 1)
                pool.tensor_tensor(yg[:, j, :], yb[:, j, :], goutb[:, :], ALU.mult).then_inc(y_g, 1)
                pool_wait(y_g, t + 1)
                pool_wait(elu2_act, t - 1)
                pool.tensor_tensor(zb[:, j, :], yg[:, j, :], beoutb[:, :], ALU.add).then_inc(z_ready, 1)

            steps(pool, NT, 0, affine2)

            pool.wait_ge(order_dec, 1)
            pool.wait_ge(prob_stored, 16)
            nb = -(-NB1 // 2)
            pool.wait_ge(tok_stored[0], 32 * (NT - BT * (NB1 // 2)))
            pool.wait_ge(tok_stored[1], 32 * BT * (NB1 // 2))
            pool.wait_ge(lg_mm, NB1)

            def tokens(b, j):
                if is_in(b, NB2):
                    pool_wait(o_ready, BT * (b - 1))
                    pool.tensor_copy(st_from[:, j, :], tok_from[:, bass.ds(BT * b, BT)]).then_inc(st_done, 1)
                    pool_wait(st_done, b + 1)
                    for q in range(BT):
                        c = BT * j + q
                        pool.indirect_dma_start(tok[:, c, :], None, tok_dram[:, :],
                                                bass.IndirectOffsetOnAxis(ap=st_from[:, j, q:q + 1].bitcast(U32), axis=0)
                                                ).then_inc(tok_in[c], 16)
                if is_in(b - 1, NB2):
                    k = 1 - j
                    pool_wait(out_done, 16 * BT * (b - 1))
                    pool.tensor_copy(st_to[:, k, :], tok_to[:, bass.ds(BT * (b - 1), BT)]).then_inc(sto_done, 1)
                    pool_wait(sto_done, b)
                    for q in range(BT):
                        pool_wait(o_ready, BT * (b - 1) + q + 1)
                        pool_wait(out_done, 16 * (BT * (b - 1) + q))
                        pool.indirect_dma_start(out[:, :], bass.IndirectOffsetOnAxis(ap=st_to[:, k, q:q + 1].bitcast(U32), axis=0),
                                                orow[:, BT * k + q, :], None, bounds_check=N - 1, oob_is_err=False
                                                ).then_inc(out_done, 16)

            steps(pool, NB2, 1, tokens)

        @block.vector
        def _(v):
            def done(ins):
                chain[0] += 1
                return ins.then_inc(dve, 1)

            def settle():
                v.wait_ge(dve, chain[0])

            asked = [0]

            def inverse_root(var_, y, t_):
                settle()
                asked[0] += 1
                done(v.tensor_copy(t_, var_))
                settle()
                v.sem_inc(sqrt_asked, 1)
                v.wait_ge(sqrt_done, asked[0])
                done(v.reciprocal(y, y))
                settle()
                done(v.tensor_tensor(t_, y, y, ALU.mult))
                settle()
                done(v.tensor_tensor(t_, t_, var_, ALU.mult))
                settle()
                done(v.tensor_scalar(t_, t_, -0.5, 1.5, ALU.mult, ALU.add))
                settle()
                done(v.tensor_tensor(y, y, t_, ALU.mult))
                settle()

            def finish_stats():
                settle()
                done(v.tensor_tensor(mean[:, :], stats[:, :, 1], stats[:, :, 4], ALU.add))
                done(v.tensor_tensor(tmp[:, :], stats[:, :, 1], stats[:, :, 4], ALU.subtract))
                done(v.tensor_tensor(var[:, :], stats[:, :, 2], stats[:, :, 5], ALU.add))
                settle()
                done(v.tensor_scalar(mean[:, :], mean[:, :], 0.5, None, ALU.mult))
                done(v.tensor_tensor(tmp[:, :], tmp[:, :], tmp[:, :], ALU.mult))
                done(v.tensor_scalar(var[:, :], var[:, :], 1.0 / C, LN_EPS, ALU.mult, ALU.add))
                settle()
                done(v.scalar_tensor_tensor(var[:, :], tmp[:, :], 0.25, var[:, :], ALU.mult, ALU.add))
                inverse_root(var[:, :], rstd[:, :], tmp[:, :])
                v.sem_inc(rstd_done, 1)

            v.wait_ge(x_in, 32)
            for t in range(NT):
                done(v.bn_stats(stats[:, t, :], xn[:, t, :]))
            finish_stats()

            v.wait_ge(wt_mm, 2 * KH + 2)
            v.tensor_tensor(brow2[:, :], brow2[:, :], big[0:1, 3, 0:C + 2], ALU.subtract).then_inc(br2_ready, 1)

            v.wait_ge(edges_in, 32)
            v.wait_ge(consts, 10)
            done(v.memset(zeros[:, :], 0.0))
            done(v.memset(keys[0][:, :].bitcast(I32), SURPLUS))
            done(v.tensor_copy(iota[:, :], iotai[:, :]))
            done(v.tensor_copy(eiota[:, :], iotai[:, 0:NE]))
            done(v.tensor_copy(srcf[0:EP, :], srcdst[0:EP, 0, :]))
            settle()
            ki = keys[0][0:EP, 0:EC].bitcast(I32)
            done(v.tensor_scalar(ki, srcdst[0:EP, 0, :], DST_BITS, ONE_TAG, ALU.logical_shift_left, ALU.bitwise_or))
            settle()
            done(v.tensor_tensor(ki, ki, srcdst[0:EP, 1, :], ALU.bitwise_or))
            for w in range(NT):
                settle()
                done(v.tensor_scalar(keys[1][0:EP, 0:EC], srcf[0:EP, :], float((w + 1) * P), 0.0, ALU.is_lt, ALU.add,
                                     accum_out=cnt[0:EP, w:w + 1]))
            settle()

            counted = [0]

            def pad_keys(nw, unit, pno, pnof, pwin, pwini, to, tag, step_, offset):
                v.sem_inc(cnt_ready, 1)
                done(v.memset(tot[:, 0:1], 0.0))
                counted[0] += 1
                v.wait_ge(cnt_mm, counted[0])
                done(v.tensor_copy(tot[:, 1:nw + 1], big[:, 0, 0:nw]))
                settle()
                done(v.tensor_tensor(padf[:, 0:nw], tot[:, 1:nw + 1], tot[:, 0:nw], ALU.subtract))
                settle()
                done(v.tensor_scalar(toti[:, 0:nw], padf[:, 0:nw], float(unit - 1), None, ALU.add))
                settle()
                sh = unit.bit_length() - 1
                done(v.tensor_scalar(toti[:, 0:nw], toti[:, 0:nw], sh, sh, ALU.logical_shift_right, ALU.logical_shift_left))
                settle()
                done(v.tensor_tensor(padf[:, 0:nw], toti[:, 0:nw], padf[:, 0:nw], ALU.subtract))
                done(v.tensor_copy(pnof, pno))
                done(v.memset(pwin, 0.0))
                settle()
                done(v.tensor_tensor_scan(padcum[:, 0:nw], padf[:, 0:nw], zeros[:, 0:nw], 0.0, ALU.add, ALU.add))
                for w in range(nw):
                    settle()
                    done(v.scalar_tensor_tensor(pwin, pnof, padcum[:, w:w + 1], pwin, ALU.is_ge, ALU.add))
                settle()
                done(v.tensor_scalar(pwini, pwin, float(step_), float(offset), ALU.mult, ALU.add))
                settle()
                done(v.tensor_scalar(to.bitcast(I32), pwini, DST_BITS, PAD_DST | tag,
                                     ALU.logical_shift_left, ALU.bitwise_or))
                settle()

            pad_keys(NT, GT * P, padno, padnof, padwin, padwini, keys[0][:, EC:SC], ONE_TAG, P, P - 1)
            done(v.tensor_scalar(sgni[:, :], sgni[:, :], 1, None, ALU.bitwise_and))
            settle()
            done(v.tensor_scalar(sgn[:, :], sgni[:, :], -2.0, 1.0, ALU.mult, ALU.add))
            settle()

            turns = [0]

            def ask_turn():
                v.sem_inc(turn_asked, 1)
                turns[0] += 1
                v.wait_ge(turned, turns[0])

            def bitonic(bufs, cur, fb):
                width = 1 << fb
                low = min(fb, 7)
                twidth = P << max(fb - 7, 0)
                parts, tparts = P, 1 << low

                def exchange(cur, bit, np_, w):
                    a = bufs[cur][0:np_, 0:w].rearrange("p (b s q) -> p b s q", s=2, q=1 << bit)
                    b = bufs[1 - cur][0:np_, 0:w].rearrange("p (b s q) -> p b s q", s=2, q=1 << bit)
                    done(v.tensor_tensor(b[:, :, 0, :], a[:, :, 0, :], a[:, :, 1, :], ALU.min))
                    done(v.tensor_tensor(b[:, :, 1, :], a[:, :, 0, :], a[:, :, 1, :], ALU.max))
                    settle()
                    return 1 - cur

                def flip(cur, np_, w, q, lo, hi):
                    part = bufs[cur][0:np_, 0:w].rearrange("p (b q) -> p b q", q=q)[:, :, lo:hi]
                    done(v.tensor_scalar(part, part, -1.0, None, ALU.mult))
                    settle()

                def turn(cur, np_, w):
                    ask_turn()
                    for h in range(-(-w // 512)):
                        n = min(512, w)
                        done(v.tensor_copy(bufs[1 - cur][0:np_, h * 512:h * 512 + n], keyps[0:np_, h, 0:n]))
                    settle()
                    return 1 - cur

                flip(cur, parts, width, 4, 2, 4)
                for k in range(1, fb + 8):
                    if 2 <= k < fb:
                        flip(cur, parts, width, 4 << (k - 1), 1 << (k - 1), 3 << (k - 1))
                    if k == fb:
                        h = width // 2
                        done(v.tensor_scalar(bufs[cur][:, 0:h], bufs[cur][:, 0:h], sgn[:, :], None, ALU.mult))
                        done(v.tensor_scalar(bufs[cur][:, h:width], bufs[cur][:, h:width], sgn[:, :], -1.0,
                                             ALU.mult, ALU.mult))
                        settle()
                    if k <= fb:
                        for d in range(k - 1, -1, -1):
                            cur = exchange(cur, d, parts, width)
                        continue
                    cur = turn(cur, tparts, twidth)
                    b = k - 1 - fb
                    if k < fb + 7:
                        flip(cur, tparts, twidth, 4 << b, 1 << b, 3 << b)
                    else:
                        flip(cur, tparts, twidth, P, P // 2, P)
                    for d in range(k - 1, fb - 1, -1):
                        cur = exchange(cur, d - fb, tparts, twidth)
                    for d in range(fb - 1, 6, -1):
                        cur = exchange(cur, d, tparts, twidth)
                    cur = turn(cur, parts, width)
                    for d in range(low - 1, -1, -1):
                        cur = exchange(cur, d, parts, width)
                return cur

            cur = bitonic(keys, 0, FB)
            assert cur == E_END
            ask_turn()
            final = keys[1 - cur]
            fo = final[:, :].rearrange("p (r b) -> p b r", b=8)
            for h in range(2):
                done(v.tensor_copy(fo[:, 4 * h:4 * h + 4, :], keyps[:, h, :].rearrange("p (b r) -> p b r", b=4)))
            settle()
            fi = final[:, 0:NTL].bitcast(I32)
            lo_i = keys[cur][:, 0:NTL].bitcast(I32)
            done(v.tensor_scalar(dst_idx[:, :], fi, PAD_DST, None, ALU.bitwise_and))
            done(v.tensor_scalar(lo_i, fi, DST_BITS, P - 1, ALU.logical_shift_right, ALU.bitwise_and))
            done(v.tensor_scalar(win_i[:, :], fi.rearrange("p (g t) -> p g t", t=GT)[:, :, 0], DST_BITS + 7, 63,
                                 ALU.logical_shift_right, ALU.bitwise_and))
            settle()
            done(v.tensor_scalar(src_lo[:, :], dst_idx[:, :], float(N) - 0.5, float(P), ALU.is_gt, ALU.mult))
            settle()
            done(v.tensor_tensor(src_lo[:, :], src_lo[:, :], lo_i, ALU.add))
            done(v.tensor_scalar(dst_idx[:, :], dst_idx[:, :], float(NT * P - 1), None, ALU.min))
            settle()
            v.sem_inc(sorted_, 1)

            v.wait_ge(h_mm, NT)
            v.wait_ge(wt_mm, 2 * KH + 2)
            done(v.memset(arena[:, 0:(NT + 1) * HD], 0.0))
            settle()

            def aggregate(a, layer):
                nh, width, got, hr = (H, HD, got1, HR) if layer == 0 else (1, C, got2, HR2)

                def step(g, j):
                    k = (j + 3) % UG
                    if is_in(g + 3, NG):
                        wait(v, a.mm, g)
                        lo = src_lo[:, bass.ds(GT * (g + 3), GT)]
                        v.tensor_tensor(hot[:, k % 4, :, :], iota[:, :].rearrange("p (o n) -> p o n", o=1).broadcast_to([P, GT, P]),
                                        lo.rearrange("p (u o) -> p u o", o=1).broadcast_to([P, GT, P]),
                                        ALU.is_equal).then_inc(a.hot, 1)
                    k = (j + 2) % UG
                    if is_in(g + 2, NG):
                        wait(v, a.src_mm, g + 3)
                        turn = (g + 2) // UG if isinstance(g, int) else None
                        for u in range(GT):
                            if turn is not None:
                                v.wait_ge(a.got[GT * k + u], 16 * (turn + 1))
                            else:
                                v.wait_ge(a.got[GT * k + u], GT * (g + 2 - k) + 16)
                        v.tensor_tensor(score[:, k % 4, :, 0:nh], big[:, 2 + k % 2, 0:GT * nh].rearrange("p (u h) -> p u h", u=GT),
                                        got[:, GT * k:GT * k + GT, width:width + nh], ALU.add).then_inc(a.score, 1)
                        wait(v, a.score, g + 3)
                        v.scalar_tensor_tensor(lrel[:, k % 4, :, 0:nh], score[:, k % 4, :, 0:nh], LEAK, score[:, k % 4, :, 0:nh],
                                               ALU.mult, ALU.max).then_inc(a.lrel, 1)
                    k = (j + 1) % UG
                    if is_in(g + 1, NG):
                        wait(v, a.exp, g + 2)
                        wait(v, a.mm, g)
                        if layer == 0:
                            for u in range(GT):
                                ins = v.tensor_tensor(
                                    scaled1[:, k % 2, u, :].rearrange("p (h d) -> p h d", h=H),
                                    got[:, GT * k + u, 0:HD].rearrange("p (h d) -> p h d", h=H),
                                    ew[:, k % 4, u, :].rearrange("p (h o) -> p h o", o=1).broadcast_to([P, H, D]), ALU.mult)
                            ins.then_inc(a.scaled, 1)
                        else:
                            v.tensor_tensor(scaled2[:, k % 2, :, :], hot[:, k % 4, :, :],
                                            ew[:, k % 4, :, 0:1].broadcast_to([P, GT, P]), ALU.mult).then_inc(a.scaled, 1)
                    if is_in(g, NG):
                        w = v.value_load(win_i[0:1, bass.ds(g, 1)], min_val=0, max_val=NT)
                        wait(v, a.mm, g + 1)
                        wait(v, a.added, g)
                        to = arena[:, bass.ds(w * width, width)]
                        v.tensor_tensor(to, to, big[:, j % 2, 0:width], ALU.add).then_inc(a.added, 1)

                group_steps(v, step)
                v.wait_ge(a.added, NG)

            aggregate(agg[0], 0)

            def centre(t, j):
                if is_in(t, NT):
                    tile = arena[:, cols(t, HD)].rearrange("p (h d) -> p h d", h=H)
                    v.tensor_reduce(headsum[:, j, :], tile, AX.X, ALU.add).then_inc(sums, 1)
                    wait(v, sums, t + 1)
                    v.scalar_tensor_tensor(tile, headsum[:, j, :].rearrange("p (h o) -> p h o", o=1).broadcast_to([P, H, D]),
                                           -1.0 / D, tile, ALU.mult, ALU.add).then_inc(centred, 1)
                if is_in(t - 1, NT):
                    wait(v, squared, t)
                    v.tensor_reduce(var1[:, cols(t - 1, H)], sq[:, 1 - j, :].rearrange("p (h d) -> p h d", h=H),
                                    AX.X, ALU.add).then_inc(sq_added, 1)

            steps(v, NT, 1, centre)
            v.wait_ge(sq_added, NT)
            done(v.tensor_scalar(var1, var1, 1.0 / D, LN_EPS, ALU.mult, ALU.add))
            inverse_root(var1, rstd1, tmp1)

            def x1_tile(t, j):
                if is_in(t, NT):
                    tile = arena[:, cols(t, HD)].rearrange("p (h d) -> p h d", h=H)
                    rs = rstd1[:, cols(t, H)].rearrange("p (h o) -> p h o", o=1).broadcast_to([P, H, D])
                    wait(v, x1t_mm, t - 1)
                    v.tensor_tensor(x1s[:, j, :].rearrange("p (h d) -> p h d", h=H), tile, rs, ALU.mult).then_inc(x1_scaled, 1)
                if is_in(t - 1, NT):
                    wait(v, elu_act, t)
                    wait(v, h2_mm, t - 2)
                    v.scalar_tensor_tensor(u1[:, 1 - j, :], ex1[:, 1 - j, :], 1.0, re1[:, 1 - j, :],
                                           ALU.min, ALU.add).then_inc(elu_u, 1)

            steps(v, NT, 1, x1_tile)

            v.wait_ge(x1t_mm, NT)
            done(v.memset(arena[:, 0:(NT + 1) * C], 0.0))
            settle()
            aggregate(agg[1], 1)

            def stat2(t, j):
                v.bn_stats(stats[:, bass.ds(t, 1), :].rearrange("p o s -> p (o s)"), arena[:, cols(t, C)]).then_inc(sum_done, 1)

            steps(v, NT, 0, stat2)
            v.wait_ge(sum_done, NT)
            finish_stats()

            def x2_tile(t, j):
                if is_in(t, NT):
                    wait(v, y_g, t - 1)
                    v.tensor_scalar(yb[:, j, :], arena[:, cols(t, C)], mean[:, cols(t, 1)], rstd[:, cols(t, 1)],
                                    ALU.subtract, ALU.mult).then_inc(y_norm, 1)
                if is_in(t - 1, NT):
                    k = 1 - j
                    wait(v, elu2_act, t)
                    v.scalar_tensor_tensor(u2[:, k, :], ex2[:, k, :], 1.0, re2[:, k, :], ALU.min, ALU.add).then_inc(u2_done, 1)
                    wait(v, u2_done, t)
                    if isinstance(t, int):
                        v.wait_ge(xre_in[k], 16 * ((t - 1) // 2 + 1))
                    else:
                        v.wait_ge(xre_in[k], 8 * (t - 1 - k) + 16)
                    tile = arena[:, cols(t - 1, C)]
                    v.scalar_tensor_tensor(tile, u2[:, k, :], -1.0, xre[:, k, :], ALU.add, ALU.add).then_inc(x2_done, 1)
                    wait(v, x2_done, t)
                    v.bn_stats(stats[:, bass.ds(t - 1, 1), :].rearrange("p o s -> p (o s)"), tile).then_inc(sum_done, 1)

            steps(v, NT, 1, x2_tile)
            v.wait_ge(sum_done, 2 * NT)
            finish_stats()

            def logits(b, j):
                if is_in(b, NB1):
                    wait(v, tok_stored[j], 16 * BT * (b - j))
                    wait(v, xn2T_mm, BT * (b - 1))
                    for q in range(BT if not isinstance(b, int) or b < NB1 - 1 else NT - BT * (NB1 - 1)):
                        t = BT * b + q
                        v.tensor_scalar(xn2[:, BT * j + q, :], arena[:, cols(t, C)], mean[:, cols(t, 1)], rstd[:, cols(t, 1)],
                                        ALU.subtract, ALU.mult).then_inc(xn2_ready, 1)
                if is_in(b - 1, NB1):
                    wait(v, lg_mm, b)
                    nq = BT if not isinstance(b, int) or b - 1 < NB1 - 1 else NT - BT * (NB1 - 1)
                    flat = lg.rearrange("p t e -> p (t e)")
                    v.tensor_copy(flat[:, bass.ds((b - 1) * BT * NE, nq * NE)], keyps[:, 1 - j, 0:nq * NE]).then_inc(lg_ready, 1)

            steps(v, NB1, 1, logits)
            v.wait_ge(lg_ready, NB1)

            def each(ap):
                return ap.rearrange("p (t o) -> p t o", o=1).broadcast_to([P, NT, NE])

            done(v.tensor_reduce(lgmax[:, :], lg, AX.X, ALU.max))
            settle()
            done(v.tensor_tensor(lg, lg, each(lgmax[:, :]), ALU.subtract))
            settle()
            v.sem_inc(lexp_asked, 1)
            v.wait_ge(lexp_done, 1)
            done(v.tensor_reduce(prob[:, :], lgx, AX.X, ALU.add))
            settle()
            done(v.reciprocal(prob[:, :], prob[:, :]))
            settle()
            done(v.tensor_copy(prob2[:, :, :], prob[:, :].rearrange("p (t o) -> p t o", o=1).broadcast_to([P, NT, 2])))
            settle()
            v.sem_inc(prob_ready, 1)
            done(v.tensor_scalar(lgx, lg, 0.0, float(NE), ALU.is_lt, ALU.mult))
            settle()
            done(v.tensor_tensor(lgx, lgx, eiota[:, :].rearrange("p (o e) -> p o e", o=1).broadcast_to([P, NT, NE]), ALU.add))
            done(v.memset(pick[:, :], float(2 * NE)))
            settle()
            done(v.tensor_reduce(pick[:, 0:NT - 1], lgx[:, 0:NT - 1, :], AX.X, ALU.min))
            done(v.tensor_reduce(pick[0:LASTP, NT - 1:NT], lgx[0:LASTP, NT - 1:NT, :], AX.X, ALU.min))
            settle()
            for e in range(NE):
                done(v.tensor_scalar(tmp[:, :], pick[:, :], float(e), 0.0, ALU.is_le, ALU.add, accum_out=cnt_e[:, e:e + 1]))
                settle()
            done(v.memset(tkeys[0][:, 0:TC].bitcast(I32), T_SURPLUS))
            done(v.tensor_copy(picki[:, :], pick[:, :]))
            settle()
            done(v.tensor_scalar(picki[:, :], picki[:, :], DST_BITS, ONE_TAG, ALU.logical_shift_left, ALU.bitwise_or))
            settle()
            done(v.tensor_tensor(tkeys[0][:, 0:NT - 1].bitcast(I32), picki[:, 0:NT - 1], tokno[:, 0:NT - 1], ALU.bitwise_or))
            done(v.tensor_tensor(tkeys[0][0:LASTP, NT - 1:NT].bitcast(I32), picki[0:LASTP, NT - 1:NT],
                                 tokno[0:LASTP, NT - 1:NT], ALU.bitwise_or))
            settle()
            pad_keys(NE, P, tpadno[:, :], tpadnof[:, :], tpadwin[:, :], tpadwini[:, :], tkeys[0][:, NT:TC], ONE_TAG, 1, 0)
            cur = bitonic(tkeys, 0, TFB)
            assert cur == T_END
            v.sem_inc(order_ready, 1)
            v.wait_ge(order_in, 16)
            done(v.tensor_scalar(tok_to[:, :], tord[:, :], PAD_DST, None, ALU.bitwise_and))
            done(v.tensor_scalar(exp_i[:, :], tord[:, :], DST_BITS, 15, ALU.logical_shift_right, ALU.bitwise_and))
            settle()
            done(v.tensor_scalar(tok_from[:, :], tok_to[:, :], float(NT * P - 1), None, ALU.min))
            done(v.tensor_scalar(exp_c[:, :], exp_i[:, :], float(NE - 1), float(MC * C), ALU.min, ALU.mult))
            done(v.tensor_scalar(exp_b[:, :], exp_i[:, :], float(NE - 1), float(C), ALU.min, ALU.mult))
            settle()
            v.sem_inc(order_dec, 1)

            def outputs(b, j):
                for q in range(BT):
                    t = BT * b + q
                    c = BT * j + q
                    wait(v, y_mm, t + 1)
                    wait(v, out_done, 16 * (t - 2 * BT + 1))
                    v.scalar_tensor_tensor(orow[:, c, :], keyps[:, q % 2, 0:C], tok[:, c, 2 * C:2 * C + 1], tok[:, c, 0:C],
                                           ALU.mult, ALU.add).then_inc(o_ready, 1)

            steps(v, NB2, 0, outputs)

        @block.scalar
        def _(act):
            act.dma_start(brow[:, 0:HD], b_heads.rearrange("h d -> (h d)").rearrange("(o n) -> o n", o=1)).then_inc(bh_in, 16)
            act.dma_start(brow2[:, 0:C], b_out.rearrange("(o n) -> o n", o=1)).then_inc(bh_in, 16)
            asked = [0]

            def root(y, v_):
                asked[0] += 1
                act.wait_ge(sqrt_asked, asked[0])
                act.activation(y, v_, ACT.Sqrt).then_inc(sqrt_done, 1)

            root(rstd[:, :], var[:, :])
            for c in range(KH):
                act.wait_ge(wt_mm, c + 1)
                act.activation(wT[:, :, c * P:(c + 1) * P], tps[:, c % 2, 0:KF * P].rearrange("p (k q) -> p k q", k=KF),
                               ACT.Copy).then_inc(wt_ready, 1)
            for c in range(KH):
                act.wait_ge(wt_mm, KH + c + 1)
                act.activation(woT[:, c, 0:C], tps[:, c % 2, 0:C], ACT.Copy).then_inc(wt_ready, 1)
            act.wait_ge(wt_mm, 2 * KH + 1)
            act.activation(wT[:, :, HD:HD + 2 * H], big[:, 1, 0:KF * 2 * H].rearrange("p (k q) -> p k q", k=KF),
                           ACT.Copy).then_inc(wt_ready, 1)
            act.activation(brow[:, HD:HD + 2 * H], big[0:1, 2, 0:2 * H], ACT.Copy).then_inc(wt_ready, 1)
            act.activation(woT[:, :, C:C + 2], big[:, 0, 0:KH * 2].rearrange("p (k q) -> p k q", k=KH),
                           ACT.Copy).then_inc(wt_ready, 1)
            act.activation(brow2[:, C:C + 2], big[0:1, 3, 0:2], ACT.Copy).then_inc(wt_ready, 1)

            def rows1(t, j):
                wait(act, xt_mm, t + 1)
                act.activation(xnT[:, j, :, :], tps[:, j, 0:KF * P].rearrange("p (k q) -> p k q", k=KF),
                               ACT.Copy).then_inc(xt_ready, 1)
                wait(act, h_mm, t + 1)
                if isinstance(t, int):
                    wait(act, h_stored[j], 16 * (t // 2))
                else:
                    act.wait_ge(h_stored[j], 8 * (t - j))
                act.activation(s_tab[:, cols(t, H)], big[:, 2 * j + 1, 0:H], ACT.Copy).then_inc(s_ready, 1)
                act.activation(hrow[:, j, 0:HD], big[:, 2 * j, 0:HD], ACT.Copy)
                act.activation(hrow[:, j, HD:HR], big[:, 2 * j + 1, H:2 * H], ACT.Copy).then_inc(h_ready, 1)

            act.wait_ge(consts, 10)
            steps(act, NT, 0, rows1)

            def weights(a, layer):
                nh = H if layer == 0 else 1

                def step(g, j):
                    if is_in(g + 3, NG):
                        wait(act, a.hotT_mm, g + 4)
                        wait(act, a.src_mm, g + 2)
                        act.activation(hotT[:, (j + 3) % 2, :, :], tps[:, (j + 3) % 2, 0:GT * P].rearrange("p (u q) -> p u q", u=GT),
                                       ACT.Copy).then_inc(a.hotT, 1)
                    if is_in(g + 2, NG):
                        k = (j + 2) % 4
                        wait(act, a.lrel, g + 3)
                        wait(act, a.scaled, g - 1)
                        act.activation(ew[:, k, :, 0:nh], lrel[:, k, :, 0:nh], ACT.Exp, scale=-1.0).then_inc(a.exp, 1)

                group_steps(act, step)

            weights(agg[0], 0)

            def squares(t, j):
                wait(act, centred, t + 1)
                wait(act, sq_added, t - 1)
                act.activation(sq[:, j, :], arena[:, cols(t, HD)], ACT.Square).then_inc(squared, 1)

            steps(act, NT, 0, squares)
            root(rstd1, var1)

            def elu1(t, j):
                if is_in(t, NT):
                    wait(act, x1t_mm, t + 1)
                    wait(act, elu_u, t - 1)
                    for c in range(KH):
                        z = tps[:, j, c * P:(c + 1) * P]
                        act.activation(ex1[:, j, c * P:(c + 1) * P], z, ACT.Exp, bias=becol[:, c:c + 1], scale=gcol[:, c:c + 1])
                        ins = act.activation(re1[:, j, c * P:(c + 1) * P], z, ACT.Relu, bias=becol[:, c:c + 1], scale=gcol[:, c:c + 1])
                    ins.then_inc(elu_act, 1)
                if is_in(t - 2, NT):
                    wait(act, h2_mm, t - 1)
                    if isinstance(t, int):
                        wait(act, h2_stored[j], 16 * ((t - 2) // 2))
                    else:
                        act.wait_ge(h2_stored[j], 8 * (t - 2 - j))
                    act.activation(s_tab2[:, cols(t - 2, 1)], big[:, j, C:C + 1], ACT.Copy).then_inc(s2_ready, 1)
                    act.activation(hrow[:, j, 0:C], big[:, j, 0:C], ACT.Copy)
                    act.activation(hrow[:, j, C:C + 1], big[:, j, C + 1:C + 2], ACT.Copy).then_inc(h2_ready, 1)

            def elu1_first(t, j):
                elu1(t, j)

            for t in range(4):
                elu1(t, t % 2)
            with act.Fori(2, NT // 2) as i:
                elu1(2 * i, 0)
                elu1(2 * i + 1, 1)
            for t in range(2 * (NT // 2), NT + 2):
                elu1(t, t % 2)

            weights(agg[1], 1)
            root(rstd[:, :], var[:, :])

            def elu2(t, j):
                wait(act, z_ready, t + 1)
                wait(act, u2_done, t - 1)
                act.activation(ex2[:, j, :], zb[:, j, :], ACT.Exp)
                act.activation(re2[:, j, :], zb[:, j, :], ACT.Relu).then_inc(elu2_act, 1)

            steps(act, NT, 0, elu2)
            root(rstd[:, :], var[:, :])

            def hidden(b, j, nq, t_mm, t_ready, u_mm, u_ready, used, to, x_used):
                for q in range(nq):
                    wait(act, t_mm, BT * b + q + 1)
                    if q == 0:
                        wait(act, x_used, MC * (b - 1))
                    act.activation(to(j)[:, :, q * P:(q + 1) * P], tps[:, q % 2, 0:KF * P].rearrange("p (k q) -> p k q", k=KF),
                                   ACT.Copy).then_inc(t_ready, 1)
                wait(act, used, b)
                for c in range(MC):
                    wait(act, u_mm, MC * b + c + 1)
                    act.activation(hT[:, c, 0:nq * P], big[:, c % 4, 0:nq * P], ACT.Gelu, bias=b1c[:, c:c + 1]).then_inc(u_ready, 1)

            def last1(b):
                return BT if not isinstance(b, int) or b < NB1 - 1 else NT - BT * (NB1 - 1)

            steps(act, NB1, 0, lambda b, j: hidden(b, j, last1(b), xn2T_mm, xn2T_ready, up_mm, up_ready, lg_mm,
                                                   lambda j: xT[j], up_mm))
            act.wait_ge(lexp_asked, 1)
            act.activation(lgx, lg, ACT.Exp).then_inc(lexp_done, 1)
            act.wait_ge(prob_stored, 16)
            steps(act, NB2, 0, lambda b, j: hidden(b, j, BT, xt2_mm, xt2_ready, up2_mm, up2_ready, y_batch,
                                                   lambda j: xT[j], up2_mm))

        @block.tensor
        def _(pe):
            pe.wait_ge(consts, 10)
            pe.wait_ge(w_in, 16 * (2 + 7 + 2 * H + 4))
            for c in range(2 * KH):
                if c >= 2:
                    pe.wait_ge(wt_ready, c - 1)
                for k in range(KF):
                    raw = wraw[:, c, k * P:(k + 1) * P] if c < KH else woraw[:, k, (c - KH) * P:(c - KH + 1) * P]
                    last = pe.transpose(tps[:, c % 2, k * P:(k + 1) * P], raw, ident[:, :])
                last.then_inc(wt_mm, 1)
            for k in range(KF):
                for c in range(KH):
                    pe.matmul(big[:, 1, k * 2 * H:(k + 1) * 2 * H], wraw[:, c, k * P:(k + 1) * P], amat[:, c, :],
                              start=(c == 0), stop=(c == KH - 1))
            for c in range(KH):
                pe.matmul(big[0:1, 2, 0:2 * H], bcol[:, c:c + 1], amat[:, c, :], start=(c == 0), stop=(c == KH - 1))
            for c in range(KH):
                for m in range(KF):
                    pe.matmul(big[:, 0, 2 * c:2 * c + 2], woraw[:, m, c * P:(c + 1) * P], a2[:, m, :],
                              start=(m == 0), stop=(m == KF - 1))
            for m in range(KF):
                last = pe.matmul(big[0:1, 3, 0:2], bocol[:, m:m + 1], a2[:, m, :], start=(m == 0), stop=(m == KF - 1))
            last.then_inc(wt_mm, 1)
            pe.wait_ge(wt_ready, 2 * KH + 4)
            pe.wait_ge(bh_in, 32)
            for c in range(KH):
                last = pe.matmul(big[0:1, 3, 0:C + 2], ones[:, 0:1], woT[:, c, :], start=(c == 0), stop=(c == KH - 1))
            last.then_inc(wt_mm, 1)

            def turn_x(t, j):
                wait(pe, xn_ready, t + 1)
                wait(pe, xt_ready, t - 1)
                for k in range(KF):
                    last = pe.transpose(tps[:, j, k * P:(k + 1) * P], xn[:, t, k * P:(k + 1) * P], ident[:, :])
                last.then_inc(xt_mm, 1)

            def h1(t, j):
                wait(pe, xt_ready, t + 1)
                wait(pe, h_ready, t - 1)
                for lo, n, bank in ((0, HD, 2 * j), (HD, 2 * H, 2 * j + 1)):
                    for k in range(KF):
                        pe.matmul(big[:, bank, 0:n], xnT[:, j, k, :], wT[:, k, lo:lo + n], start=(k == 0), stop=False)
                    last = pe.matmul(big[:, bank, 0:n], ones[0:1, :], brow[:, lo:lo + n], start=False, stop=True)
                last.then_inc(h_mm, 1)

            pe.wait_ge(br2_ready, 1)
            for t in range(NT):
                turn_x(t, t % 2)
                h1(t, t % 2)
            pe.wait_ge(h_ready, NT)
            pe.wait_ge(cnt_ready, 1)
            pe.matmul(big[:, 0, 0:NT], ones[0:EP, :], cnt[0:EP, :], start=True, stop=True).then_inc(cnt_mm, 1)
            turns = 0
            for c in E_TURNS:
                turns += 1
                pe.wait_ge(turn_asked, turns)
                for b in range(SC // P):
                    last = pe.transpose(keyps[:, b // 4, (b % 4) * P:(b % 4 + 1) * P], keys[c][:, b * P:(b + 1) * P], ident[:, :])
                last.then_inc(turned, 1)

            def sums_of(a, layer):
                nh, width, got, tab = (H, HD, got1, s_tab) if layer == 0 else (1, C, got2, s_tab2)
                if layer == 0:
                    pe.wait_ge(s_ready, NT)
                else:
                    pe.wait_ge(s2_ready, NT)

                def step(g, j):
                    if is_in(g + 3, NG):
                        k = (j + 3) % UG
                        wait(pe, a.hot, g + 4)
                        wait(pe, a.hotT, g + 2)
                        for u in range(GT):
                            last = pe.transpose(tps[:, k % 2, u * P:(u + 1) * P], hot[:, k % 4, u, :], ident[:, :])
                        last.then_inc(a.hotT_mm, 1)
                    if is_in(g + 2, NG):
                        k = (j + 2) % UG
                        w = pe.value_load(win_i[0:1, bass.ds(g + 2, 1)], min_val=0, max_val=NT)
                        wait(pe, a.hotT, g + 3)
                        wait(pe, a.score, g + 1)
                        for u in range(GT):
                            last = pe.matmul(big[:, 2 + k % 2, u * nh:(u + 1) * nh], hotT[:, k % 2, u, :],
                                             tab[:, bass.ds(w * nh, nh)], start=True, stop=True)
                        last.then_inc(a.src_mm, 1)
                    if is_in(g, NG):
                        wait(pe, a.scaled, g + 1)
                        wait(pe, a.added, g - 1)
                        for u in range(GT):
                            if layer == 0:
                                lhs, rhs = hot[:, j % 4, u, :], scaled1[:, j % 2, u, :]
                            else:
                                lhs, rhs = scaled2[:, j % 2, u, :], got[:, GT * j + u, 0:C]
                            last = pe.matmul(big[:, j % 2, 0:width], lhs, rhs, start=(u == 0), stop=(u == GT - 1))
                        last.then_inc(a.mm, 1)

                group_steps(pe, step)

            sums_of(agg[0], 0)

            def h2(t, j):
                if is_in(t, NT):
                    wait(pe, x1_scaled, t + 1)
                    wait(pe, elu_act, t - 1)
                    for c in range(KH):
                        last = pe.transpose(tps[:, j, c * P:(c + 1) * P], x1s[:, j, c * P:(c + 1) * P], ident[:, :])
                    last.then_inc(x1t_mm, 1)
                if is_in(t - 1, NT):
                    k = 1 - j
                    wait(pe, elu_u, t)
                    wait(pe, h2_ready, t - 2)
                    for c in range(KH):
                        pe.matmul(big[:, k, 0:C + 2], u1[:, k, c * P:(c + 1) * P], woT[:, c, :], start=(c == 0), stop=False)
                    pe.matmul(big[:, k, 0:C + 2], ones[0:1, :], brow2[:, :], start=False, stop=True).then_inc(h2_mm, 1)

            steps(pe, NT, 1, h2)
            sums_of(agg[1], 1)

            def last1(b):
                return BT if not isinstance(b, int) or b < NB1 - 1 else NT - BT * (NB1 - 1)

            def up(b, j, nq, src_of, ready_of, t_mm, t_ready, u_mm, u_ready):
                for q in range(nq):
                    ready_of(b, j, q)
                    wait(pe, t_ready, BT * b + q - 1)
                    for k in range(KF):
                        last = pe.transpose(tps[:, q % 2, k * P:(k + 1) * P], src_of(j, q)[:, k * P:(k + 1) * P], ident[:, :])
                    last.then_inc(t_mm, 1)
                wait(pe, t_ready, BT * b + nq)
                for c in range(MC):
                    wait(pe, u_ready, MC * b + c - 3)
                    for k in range(KF):
                        last = pe.matmul(big[:, c % 4, 0:nq * P], w1_sb[:, k, c * P:(c + 1) * P], xT[j][:, k, 0:nq * P],
                                         start=(k == 0), stop=(k == KF - 1))
                    last.then_inc(u_mm, 1)

            pe.wait_ge(w1_in, 16)

            def logit_batch(b, j):
                nq = last1(b)
                up(b, j, nq, lambda j, q: xn2[:, BT * j + q, :], lambda b, j, q: wait(pe, xn2_ready, BT * b + q + 1),
                   xn2T_mm, xn2T_ready, up_mm, up_ready)
                wait(pe, up_ready, MC * (b + 1))
                wait(pe, lg_ready, b - 1)
                for q in range(nq):
                    to = keyps[:, j, q * NE:(q + 1) * NE]
                    for c in range(MC):
                        pe.matmul(to, hT[:, c, q * P:(q + 1) * P], wg_sb[:, c, :], start=(c == 0), stop=False)
                    last = pe.matmul(to, ones[0:1, :], bg_sb[:, :], start=False, stop=True)
                last.then_inc(lg_mm, 1)

            steps(pe, NB1, 0, logit_batch)
            pe.wait_ge(cnt_ready, 2)
            pe.matmul(big[:, 0, 0:NE], ones[:, :], cnt_e[:, :], start=True, stop=True).then_inc(cnt_mm, 1)
            for n, c in enumerate(T_TURNS):
                turns += 1
                pe.wait_ge(turn_asked, turns)
                if n % 2 == 0:
                    pe.transpose(keyps[0:TC, 0, 0:P], tkeys[c][:, 0:TC], ident[:, :]).then_inc(turned, 1)
                else:
                    pe.transpose(keyps[:, 0, 0:TC], tkeys[c][0:TC, :], ident[0:TC, 0:TC]).then_inc(turned, 1)

            pe.wait_ge(wd_in, 16 * NE)
            pe.wait_ge(order_dec, 1)
            pe.wait_ge(bd_in, 16)

            def expert_batch(b, j):
                def arrived(b, j, q):
                    if isinstance(b, int):
                        pe.wait_ge(tok_in[BT * j + q], 16 * (b // 2 + 1))
                    else:
                        pe.wait_ge(tok_in[BT * j + q], 8 * (b - j) + 16)

                up(b, j, BT, lambda j, q: tok[:, BT * j + q, C:2 * C], arrived, xt2_mm, xt2_ready, up2_mm, up2_ready)
                wait(pe, up2_ready, MC * (b + 1))
                for q in range(BT):
                    t = BT * b + q
                    e = pe.value_load(exp_c[0:1, cols(t, 1)], min_val=0, max_val=(NE - 1) * MC * C)
                    eb = pe.value_load(exp_b[0:1, cols(t, 1)], min_val=0, max_val=(NE - 1) * C)
                    wait(pe, o_ready, t - 1)
                    for c in range(MC):
                        pe.matmul(keyps[:, q % 2, 0:C], hT[:, c, q * P:(q + 1) * P], wd_sb[:, bass.ds(e + c * C, C)],
                                  start=(c == 0), stop=False)
                    last = pe.matmul(keyps[:, q % 2, 0:C], ones[0:1, :], bd_sb[:, bass.ds(eb, C)], start=False, stop=True)
                    last.then_inc(y_mm, 1)
                pe.sem_inc(y_batch, 1)

            steps(pe, NB2, 0, expert_batch)


_INS = ['x', 'src', 'dst', 'L0_gnn_W_heads', 'L0_gnn_b_heads', 'L0_gnn_a_heads', 'L0_gnn_g_heads', 'L0_gnn_beta_heads',
        'L0_gnn_W_out', 'L0_gnn_b_out', 'L0_gnn_a_out', 'L0_gnn_g_out', 'L0_gnn_beta_out',
        'L0_ffn_W1', 'L0_ffn_b1', 'L0_ffn_Wg', 'L0_ffn_bg', 'L0_ffn_Wd', 'L0_ffn_bd']
_OUTS = [((6250, 256), 'float32')]


def kernel(**inputs):
    import numpy as _np
    import concourse.bacc as _bacc
    from concourse import mybir as _mybir
    from concourse.bass_utils import run_bass_kernel_spmd as _run

    nc = _bacc.Bacc("TRN2", target_bir_lowering=False, num_devices=1)
    arrays, args = {}, []
    for name in _INS:
        a = _np.ascontiguousarray(inputs[name])
        arrays[f"in_{name}_dram"] = a
        args.append(nc.dram_tensor(f"in_{name}_dram", a.shape, _mybir.dt.from_np(a.dtype), kind="ExternalInput").ap())
    for i, (shape, dtype) in enumerate(_OUTS):
        dt = _mybir.dt.from_np(_np.dtype(dtype))
        args.append(nc.dram_tensor(f"out_{i}_dram", shape, dt, kind="ExternalOutput").ap())
    build(nc, *args)
    r = _run(nc, [arrays], core_ids=[0])
    return r.results[0]["out_0_dram"]
```

```python
from contextlib import ExitStack

import concourse.bass as bass
from concourse import mybir

P = 128
F32 = mybir.dt.float32
I32 = mybir.dt.int32
BF16 = mybir.dt.bfloat16
U32 = mybir.dt.uint32
ALU = mybir.AluOpType
ACT = mybir.ActivationFunctionType
AX = mybir.AxisListType

ONE_TAG = 0x40000000
DST_BITS = 13
PAD_DST = (1 << DST_BITS) - 1
LN_EPS = 1e-5
LEAK = 0.2


def build(nc, x, src, dst, W_heads, b_heads, a_heads, g_heads, beta_heads, W_out, b_out, a_out, g_out, beta_out,
          W1, b1, Wg, bg, Wd, bd, out):
    N, C = x.shape
    E = src.shape[0]
    H, D, _ = W_heads.shape
    HD = H * D
    HID = W1.shape[1]
    NE = Wg.shape[1]
    NT = -(-N // P)
    LASTP = N - (NT - 1) * P
    KF = C // P
    KH = HD // P
    HR = HD + H
    HR2 = C + 4
    MC = HID // P

    EP = 125
    EC = E // EP
    SC = 1024
    PC = SC - EC
    FB = SC.bit_length() - 1
    GT = 2
    UG = 8
    NG = -(-((E + NT * (GT * P - 1)) // (GT * P)) // UG) * UG
    NTL = NG * GT
    US = UG * GT
    SURPLUS = ((NT * P + P - 1) << DST_BITS) | PAD_DST | ONE_TAG
    assert EP * EC == E and P * PC >= NT * (GT * P - 1) and NTL <= SC and N <= NT * P < PAD_DST

    TC = 64
    TFB = TC.bit_length() - 1
    TPC = TC - NT
    BT = 4
    NB1 = -(-NT // BT)
    NB2 = -(-((N + NE * (P - 1)) // P) // BT)
    TT = NB2 * BT
    T_SURPLUS = (NE << DST_BITS) | PAD_DST | ONE_TAG
    assert P * TPC >= NE * (P - 1) and TT <= TC and NB2 % 2 == 0 and NB1 % 2 == 1
    XR = 2 * C + 2

    with ExitStack() as ctx:
        def sb(name, shape, dt=F32):
            return ctx.enter_context(nc.sbuf_tensor(name, shape, dt))

        def ps(name, shape, dt=F32):
            return ctx.enter_context(nc.psum_tensor(name, shape, dt))

        def sem(name):
            return ctx.enter_context(nc.semaphore(name))

        h1_dram = nc.dram_tensor("h1_rows", (NT * P, HR), F32, kind="Internal").ap()
        h2_dram = nc.dram_tensor("h2_rows", (NT * P, HR2), F32, kind="Internal").ap()
        tok_dram = nc.dram_tensor("token_rows", (NT * P, XR), F32, kind="Internal").ap()
        order_dram = nc.dram_tensor("token_order", (P * TC,), F32, kind="Internal").ap()

        WD0 = (NT + 1) * C
        arena = sb("arena", [P, max((NT + 1) * HD, WD0 + NE * MC * C)])
        xn = arena[:, 0:NT * C].rearrange("p (t f) -> p t f", t=NT)
        wraw = arena[:, NT * C:NT * C + KH * C].rearrange("p (c f) -> p c f", c=KH)
        wo0 = NT * C + KH * C
        woraw = arena[:, wo0:wo0 + KF * HD].rearrange("p (m f) -> p m f", m=KF)
        wd_sb = arena[:, WD0:WD0 + NE * MC * C]
        work = sb("work", [P, US * HR])
        got1 = work[:, :].rearrange("p (s r) -> p s r", s=US)
        got2 = work[:, 0:US * HR2].rearrange("p (s r) -> p s r", s=US)
        srcdst = work[:, 0:2 * EC].bitcast(I32).rearrange("p (a c) -> p a c", a=2)
        srcf = work[:, 2 * EC:3 * EC]
        padno = work[:, 3 * EC:3 * EC + PC].bitcast(I32)
        padnof = work[:, 3 * EC + PC:3 * EC + 2 * PC]
        padwin = work[:, 3 * EC + 2 * PC:3 * EC + 3 * PC]
        padwini = work[:, 3 * EC + 3 * PC:3 * EC + 4 * PC].bitcast(I32)

        def ring(n, width, depth=2):
            return work[:, n:n + depth * width].rearrange("p (s w) -> p s w", s=depth)

        hstats = work[:, 10 * HD:10 * HD + NT * H * 6]
        assert 10 * HD + NT * H * 6 <= US * HR
        ex1 = ring(2 * HD, HD)
        re1 = ring(4 * HD, HD)
        u1 = ring(6 * HD, HD)
        x1s = ring(8 * HD, HD)
        yb = ring(0, C)
        zb = ring(2 * C, C)
        ex2 = ring(4 * C, C)
        re2 = ring(6 * C, C)
        u2 = ring(8 * C, C)
        xre = ring(10 * C, C)
        hT = work[:, 0:MC * BT * P].rearrange("p (c q) -> p c q", c=MC)
        tok = work[:, MC * BT * P:MC * BT * P + 2 * BT * XR].rearrange("p (s r) -> p s r", s=2 * BT)
        xn2 = work[:, MC * BT * P:MC * BT * P + 2 * BT * C].rearrange("p (s r) -> p s r", s=2 * BT)
        lg = work[:, MC * BT * P + 2 * BT * C:MC * BT * P + 2 * BT * C + NT * NE].rearrange("p (t e) -> p t e", t=NT)
        lgx = work[:, 0:NT * NE].rearrange("p (t e) -> p t e", t=NT)
        assert MC * BT * P + 2 * BT * XR <= US * HR and MC * BT * P + 2 * BT * C + NT * NE <= US * HR

        ident = sb("ident", [P, P])
        iota = sb("iota", [P, P])
        iotai = work[:, 3 * EC + 4 * PC:3 * EC + 4 * PC + P].bitcast(I32)
        ones = sb("ones", [P, P])
        wT = sb("wT", [P, KF, HD + 2 * H])
        amat = sb("amat", [P, KH, 2 * H])
        bcol = sb("bcol", [P, KH])
        brow = sb("brow", [1, HD + 2 * H])
        woT = sb("woT", [P, KH, C + 2])
        a2 = sb("a2", [P, KF, 2])
        bocol = sb("bocol", [P, KF])
        brow2 = sb("brow2", [1, C + 2])
        gcol = sb("gcol", [P, KH])
        becol = sb("becol", [P, KH])
        goutb, beoutb = wT[:, 0, 0:C], wT[:, 1, 0:C]
        stats = sb("stats", [P, NT, 6])
        mean = sb("mean", [P, NT])
        var = sb("var", [P, NT])
        rstd = sb("rstd", [P, NT])
        tmp = sb("tmp", [P, NT])
        xnT = work[:, 10 * HD:11 * HD].rearrange("p (s k q) -> p s k q", s=2, k=KF)
        hrow = ring(11 * HD, HR)
        s_tab = sb("s_tab", [P, (NT + 1) * H])
        s_tab2 = sb("s_tab2", [P, NT + 1])

        keys = [sb("keys_a", [P, SC]), sb("keys_b", [P, SC])]
        var1, rstd1 = (keys[0][:, n * NT * H:(n + 1) * NT * H] for n in range(2))
        mean1, tmp1 = (keys[1][:, n * NT * H:(n + 1) * NT * H] for n in range(2))
        xT = [k[:, :].rearrange("p (k q) -> p k q", k=KF) for k in keys]
        cnt = sb("cnt", [P, NT])
        tot = sb("tot", [P, NT + 1])
        toti = sb("toti", [P, NT], I32)
        padf = sb("padf", [P, NT])
        padcum = sb("padcum", [P, NT])
        zeros = sb("zeros", [P, NT])
        sgn = sb("sgn", [P, 1])
        sgni = sb("sgni", [P, 1], I32)
        dst_idx = sb("dst_idx", [P, NTL], I32)
        src_lo = sb("src_lo", [P, NTL])
        win_i = sb("win_i", [P, NG], I32)
        staged = sb("staged", [P, 2, US // 2], I32)

        hot = sb("hot", [P, UG, GT, P])
        hotT = sb("hotT", [P, 2, GT, P], BF16)
        s_parts = sb("s_parts", [P, (NT + 1) * 3 * H], BF16)
        s_rest = keys[0][:, 0:2 * (NT + 1) * H].rearrange("p (a n) -> p a n", a=2)
        score = sb("score", [P, 4, GT, H])
        lrel = sb("lrel", [P, 4, GT, H])
        ew = sb("ew", [P, 4, GT, H])
        scaled = sb("scaled", [P, 2 * GT * HD])
        scaled1 = scaled[:, :].rearrange("p (s u f) -> p s u f", s=2, u=GT)
        scaled2 = scaled[:, 0:2 * GT * P].rearrange("p (s u f) -> p s u f", s=2, u=GT)
        w1_sb = scaled[:, :].rearrange("p (k f) -> p k f", k=KF)
        assert 2 * GT * HD == KF * HID

        b1c = sb("b1c", [P, MC])
        wg_sb = sb("wg_sb", [P, MC, NE])
        bg_sb = sb("bg_sb", [NE, 1])
        eiota = sb("eiota", [P, NE])
        lgmax = sb("lgmax", [P, NT])
        prob = sb("prob", [P, NT])
        pick = sb("pick", [P, NT])
        cnt_e = sb("cnt_e", [P, NE])
        tokno = sb("tokno", [P, NT], I32)
        picki = sb("picki", [P, NT], I32)
        tpadno = sb("tpadno", [P, TPC], I32)
        tpadnof = sb("tpadnof", [P, TPC])
        tpadwin = sb("tpadwin", [P, TPC])
        tpadwini = sb("tpadwini", [P, TPC], I32)
        hotf = hot[:, :, :, :].rearrange("p a b c -> p (a b c)")
        lgT = hotf[:, 8 * P:8 * P + BT * P]
        tkeys = [hotf[:, n * P:(n + 1) * P] for n in range(2)]
        tord, tok_to, tok_from, exp_i, exp_c, exp_b = (hotf[:, 2 * P + n * TC:2 * P + (n + 1) * TC].bitcast(I32) for n in range(6))
        st_from = sb("st_from", [P, 2, BT], I32)
        st_to = sb("st_to", [P, 2, BT], I32)
        orow = arena[:, 0:2 * BT * C].rearrange("p (s c) -> p s c", s=2 * BT)
        bd_sb = arena[0:1, 2 * BT * C:(2 * BT + NE) * C]

        big = ps("big", [P, 4, 512])
        tps = ps("tps", [P, 2, 512])
        keyps = ps("keyps", [P, 2, 512])

        x_in, w_in, edges_in, zero_x, consts = sem("x_in"), sem("w_in"), sem("edges_in"), sem("zero_x"), sem("consts")
        dve, pool_own = sem("dve"), sem("pool_own")
        sqrt_asked, sqrt_done, xn_ready = sem("sqrt_asked"), sem("sqrt_done"), sem("xn_ready")
        rstd_done = sem("rstd_done")
        wt_mm, wt_ready, bh_in = sem("wt_mm"), sem("wt_ready"), sem("bh_in")
        xt_mm, xt_ready, h_mm, h_ready = sem("xt_mm"), sem("xt_ready"), sem("h_mm"), sem("h_ready")
        s_ready = sem("s_ready")
        h_stored = [sem("h_stored0"), sem("h_stored1")]
        cnt_ready, cnt_mm, turn_asked, turned = sem("cnt_ready"), sem("cnt_mm"), sem("turn_asked"), sem("turned")
        acc_zero, sorted_ = sem("acc_zero"), sem("sorted")

        class Agg:
            def __init__(self, n):
                self.staged = sem(f"idx_staged{n}")
                self.got = [sem(f"got{n}_{c}") for c in range(US)]
                self.hot = sem(f"hot{n}")
                self.hotT_mm = sem(f"hotT_mm{n}")
                self.hotT = sem(f"hotT{n}")
                self.src_mm = sem(f"src_mm{n}")
                self.score = sem(f"score{n}")
                self.lrel = sem(f"lrel{n}")
                self.exp = sem(f"exp{n}")
                self.scaled = sem(f"scaled{n}")
                self.mm = sem(f"agg_mm{n}")
                self.added = sem(f"added{n}")

        agg = [Agg(1), Agg(2)]

        sums, centred = sem("sums"), sem("centred")
        x1_scaled, x1t_mm, elu_act, elu_u, h2_mm, h2_ready = (sem("x1_scaled"), sem("x1t_mm"), sem("elu_act"),
                                                              sem("elu_u"), sem("h2_mm"), sem("h2_ready"))
        s2_ready = sem("s2_ready")
        h2_stored = [sem("h2_stored0"), sem("h2_stored1")]
        xre_in = [sem("xre_in0"), sem("xre_in1")]
        w1_in, wd_in, sum_done = sem("w1_in"), sem("wd_in"), sem("sum_done")
        y_norm, z_ready, elu2_act, u2_done, x2_done = (sem("y_norm"), sem("z_ready"), sem("elu2_act"),
                                                            sem("u2_done"), sem("x2_done"))
        xn2_ready, xn2T_mm, xn2T_ready = sem("xn2_ready"), sem("xn2T_mm"), sem("xn2T_ready")
        up_mm, up_ready, lg_mm, lg_ready = sem("up_mm"), sem("up_ready"), sem("lg_mm"), sem("lg_ready")
        tok_stored = [sem("tok_stored0"), sem("tok_stored1")]
        lexp_asked, lexp_done, prob_ready, prob_stored = (sem("lexp_asked"), sem("lexp_done"), sem("prob_ready"),
                                                          sem("prob_stored"))
        order_ready, order_out, order_in, order_dec = (sem("order_ready"), sem("order_out"), sem("order_in"),
                                                       sem("order_dec"))
        st_done = sem("st_done")
        tok_in = [sem(f"tok_in{c}") for c in range(2 * BT)]
        xt2_mm, xt2_ready, up2_mm, up2_ready = sem("xt2_mm"), sem("xt2_ready"), sem("up2_mm"), sem("up2_ready")
        y_mm, o_ready, sto_done, out_done = sem("y_mm"), sem("o_ready"), sem("sto_done"), sem("out_done")

        def wait(eng, s, n):
            if not (isinstance(n, int) and n <= 0):
                eng.wait_ge(s, n)

        def pool_wait(s, n):
            wait(nc.gpsimd, s, n)
            if not isinstance(n, int):
                nc.gpsimd.sem_inc(pool_gate, 1)

        def is_in(t, n):
            return not isinstance(t, int) or 0 <= t < n

        def steps(eng, n, extra, step):
            step(0, 0)
            step(1, 1)
            m = n // 2
            with eng.Fori(1, m) as i:
                step(2 * i, 0)
                step(2 * i + 1, 1)
            for t in range(2 * m, n + extra):
                step(t, t % 2)

        def group_steps(eng, step):
            for g in range(-5, UG):
                step(g, g % UG)
            with eng.Fori(1, NG // UG - 1) as i:
                for j in range(UG):
                    step(UG * i + j, j)
            for g in range(NG - UG, NG + 1):
                step(g, g % UG)

        def cols(t, width):
            return bass.ds(t * width, width)

        def buffers_turned(fb):
            at, read = 0, []
            for k in range(1, fb + 8):
                if k <= fb:
                    at ^= k & 1
                    continue
                read.append(at)
                at ^= 1 ^ ((k - min(fb, 7)) & 1)
                read.append(at)
                at ^= 1 ^ (min(fb, 7) & 1)
            return read, at

        E_TURNS, E_END = buffers_turned(FB)
        E_TURNS = E_TURNS + [E_END]
        T_TURNS, T_END = buffers_turned(TFB)
        pe_gate = sem("pe_gate")
        gb_in, lgT_ready, lgt_mm = sem("gb_in"), sem("lgT_ready"), sem("lgt_mm")
        pool_gate, s_split = sem("pool_gate"), sem("s_split")
        br2_ready, y_batch, bd_in = sem("br2_ready"), sem("y_batch"), sem("bd_in")
        prob2 = sb("prob2", [P, NT, 2])

        chain = [0]
        block = ctx.enter_context(nc.Block())

        @block.sync
        def _(sp):
            sp.dma_start(srcdst[0:EP, 0, :], src.rearrange("(p c) -> p c", p=EP)).then_inc(edges_in, 16)
            sp.dma_start(srcdst[0:EP, 1, :], dst.rearrange("(p c) -> p c", p=EP)).then_inc(edges_in, 16)
            sp.wait_ge(zero_x, 2)
            sp.dma_start(xn[:, 0:NT - 1, :], x[0:(NT - 1) * P, :].rearrange("(t p) f -> p t f", p=P)).then_inc(x_in, 16)
            sp.dma_start(xn[0:LASTP, NT - 1, :], x[(NT - 1) * P:N, :]).then_inc(x_in, 16)
            sp.dma_start(wraw, W_heads.rearrange("h d f -> (h d) f").rearrange("(c p) f -> p c f", p=P)).then_inc(w_in, 16)
            sp.dma_start(woraw, W_out.rearrange("(m p) f -> p m f", p=P)).then_inc(w_in, 16)

            def column(to, v):
                sp.dma_start(to, v.rearrange("(c p) -> p c", p=P), allow_slow_non_contiguous=True).then_inc(w_in, 16)

            column(bcol[:, :], b_heads.rearrange("h d -> (h d)"))
            column(gcol[:, :], g_heads.rearrange("h d -> (h d)"))
            column(becol[:, :], beta_heads.rearrange("h d -> (h d)"))
            column(bocol[:, :], b_out)
            column(b1c[:, :], b1)
            for s in range(2):
                column(a2[:, :, s], a_out[s * C:(s + 1) * C])
            for h in range(H):
                lo = (h * D) % P
                for s in range(2):
                    sp.dma_start(amat[lo:lo + D, h * D // P, s * H + h:s * H + h + 1],
                                 a_heads[h, s * D:(s + 1) * D].rearrange("(d o) -> d o", o=1),
                                 allow_slow_non_contiguous=True).then_inc(w_in, 16)
            sp.dma_start(wg_sb[:, :, :], Wg.rearrange("(c p) e -> p c e", p=P)).then_inc(w_in, 16)
            sp.dma_start(bg_sb[:, :], bg.rearrange("(e o) -> e o", o=1), allow_slow_non_contiguous=True).then_inc(w_in, 16)

            def store1(t, j):
                wait(sp, h_ready, t + 1)
                sp.dma_start(h1_dram[cols(t, P), :], hrow[:, j, :]).then_inc(h_stored[j], 16)

            steps(sp, NT, 0, store1)

            for to, vec in ((goutb, g_out), (beoutb, beta_out)):
                sp.dma_start(to, vec.rearrange("(o n) -> o n", o=1).broadcast_to([P, C])).then_inc(gb_in, 16)

            def store2(t, j):
                wait(sp, h2_ready, t + 1)
                sp.dma_start(h2_dram[cols(t, P), :], hrow[:, j, 0:HR2]).then_inc(h2_stored[j], 16)

            steps(sp, NT, 0, store2)
            sp.wait_ge(h2_mm, NT)
            for e in range(NE):
                sp.dma_start(wd_sb[:, e * MC * C:(e + 1) * MC * C].rearrange("p (c f) -> p c f", c=MC),
                             Wd[e].rearrange("(c p) f -> p c f", p=P)).then_inc(wd_in, 16)
            sp.wait_ge(agg[1].mm, NG)
            sp.dma_start(w1_sb, W1.rearrange("(k p) f -> p k f", p=P)).then_inc(w1_in, 16)

            def reload(t, j):
                wait(sp, x2_done, t - 1)
                if isinstance(t, int) and t == NT - 1:
                    sp.dma_start(xre[0:LASTP, j, :], x[(NT - 1) * P:N, :]).then_inc(xre_in[j], 16)
                else:
                    sp.dma_start(xre[:, j, :], x[cols(t, P), :]).then_inc(xre_in[j], 16)

            steps(sp, NT, 0, reload)

            def store_tok(b, j):
                for q in range(BT if not isinstance(b, int) or b < NB1 - 1 else NT - BT * (NB1 - 1)):
                    t = BT * b + q
                    wait(sp, xn2_ready, t + 1)
                    sp.dma_start(tok_dram[cols(t, P), 0:C], arena[:, cols(t, C)]).then_inc(tok_stored[j], 16)
                    sp.dma_start(tok_dram[cols(t, P), C:2 * C], xn2[:, BT * j + q, :]).then_inc(tok_stored[j], 16)

            steps(sp, NB1, 0, store_tok)
            sp.wait_ge(prob_ready, 1)
            sp.dma_start(tok_dram.rearrange("(t p) r -> p t r", p=P)[:, :, 2 * C:2 * C + 2],
                         prob2[:, :, :]).then_inc(prob_stored, 16)
            sp.wait_ge(tok_stored[0], 32 * (NT - BT * (NB1 // 2)))
            sp.wait_ge(tok_stored[1], 32 * BT * (NB1 // 2))
            sp.dma_start(bd_sb, bd.rearrange("(o e) c -> o (e c)", o=1)).then_inc(bd_in, 16)
            sp.wait_ge(order_ready, 1)
            sp.dma_start(order_dram.rearrange("(p c) -> p c", p=P), tkeys[T_END][:, 0:TC]).then_inc(order_out, 16)
            sp.wait_ge(order_out, 16)
            sp.dma_start(tord[:, :].bitcast(F32), order_dram.rearrange("(c p) -> p c", p=P),
                         allow_slow_non_contiguous=True).then_inc(order_in, 16)
            sp.wait_ge(out_done, 16 * TT)

        @block.gpsimd
        def _(pool):
            pool.memset(xn[:, NT - 1, :], 0.0).then_inc(zero_x, 1)
            pool.memset(amat[:, :, :], 0.0).then_inc(zero_x, 1)
            pool.memset(ones[:, :], 1.0).then_inc(consts, 1)
            pool.memset(ident[:, :], 0.0).then_inc(pool_own, 1)
            pool.wait_ge(pool_own, 1)
            pool.affine_select(out=ident[:, :], in_=ident[:, :], compare_op=ALU.not_equal, fill=1.0, base=0,
                               pattern=[[-1, P]], channel_multiplier=1).then_inc(consts, 1)
            pool.iota(padno, pattern=[[1, PC]], base=0, channel_multiplier=PC).then_inc(consts, 1)
            pool.iota(tpadno[:, :], pattern=[[1, TPC]], base=0, channel_multiplier=TPC).then_inc(consts, 1)
            pool.iota(tokno[:, :], pattern=[[P, NT]], base=0, channel_multiplier=1).then_inc(consts, 1)
            pool.iota(sgni[:, :], pattern=[[0, 1]], base=0, channel_multiplier=1).then_inc(consts, 1)
            pool.iota(iotai[:, :], pattern=[[1, P]], base=0, channel_multiplier=0).then_inc(consts, 1)
            pool.memset(s_tab[:, NT * H:(NT + 1) * H], 0.0).then_inc(consts, 1)
            pool.memset(s_tab2[:, NT:NT + 1], 0.0).then_inc(consts, 1)
            pool.memset(hrow[:, :, :], 0.0).then_inc(consts, 1)
            def gathers(a, table, rows, width, used):
                def turn(i):
                    for half in range(2):
                        lo = half * (US // 2)
                        first = UG * i + half * (UG // 2)
                        pool_wait(used, first - UG // 2)
                        pool.tensor_copy(staged[:, half, :], dst_idx[:, bass.ds(US * i + lo, US // 2)]).then_inc(a.staged, 1)
                        pool_wait(a.staged, 2 * i + half + 1)
                        for c in range(lo, lo + US // 2):
                            pool.indirect_dma_start(rows[:, c, 0:width], None, table[:, :],
                                                    bass.IndirectOffsetOnAxis(ap=staged[:, half, c - lo:c - lo + 1].bitcast(U32),
                                                                              axis=0)).then_inc(a.got[c], 16)
                turn(0)
                with pool.Fori(1, NG // UG) as i:
                    turn(i)

            pool.wait_ge(sorted_, 1)
            pool.wait_ge(h_stored[0], 16 * ((NT + 1) // 2))
            pool.wait_ge(h_stored[1], 16 * (NT // 2))
            gathers(agg[0], h1_dram, got1, HR, agg[0].scaled)
            pool.wait_ge(h2_stored[0], 16 * ((NT + 1) // 2))
            pool.wait_ge(h2_stored[1], 16 * (NT // 2))
            gathers(agg[1], h2_dram, got2, HR2, agg[1].mm)

            pool.wait_ge(order_dec, 1)
            pool.wait_ge(prob_stored, 16)
            nb = -(-NB1 // 2)
            pool.wait_ge(tok_stored[0], 32 * (NT - BT * (NB1 // 2)))
            pool.wait_ge(tok_stored[1], 32 * BT * (NB1 // 2))
            pool.wait_ge(lg_mm, NB1)

            def tokens(b, j):
                if is_in(b, NB2):
                    pool_wait(o_ready, BT * (b - 1))
                    pool.tensor_copy(st_from[:, j, :], tok_from[:, bass.ds(BT * b, BT)]).then_inc(st_done, 1)
                    pool_wait(st_done, b + 1)
                    for q in range(BT):
                        c = BT * j + q
                        pool.indirect_dma_start(tok[:, c, :], None, tok_dram[:, :],
                                                bass.IndirectOffsetOnAxis(ap=st_from[:, j, q:q + 1].bitcast(U32), axis=0)
                                                ).then_inc(tok_in[c], 16)
                if is_in(b - 1, NB2):
                    k = 1 - j
                    pool_wait(out_done, 16 * BT * (b - 1))
                    pool.tensor_copy(st_to[:, k, :], tok_to[:, bass.ds(BT * (b - 1), BT)]).then_inc(sto_done, 1)
                    pool_wait(sto_done, b)
                    for q in range(BT):
                        pool_wait(o_ready, BT * (b - 1) + q + 1)
                        pool_wait(out_done, 16 * (BT * (b - 1) + q))
                        pool.indirect_dma_start(out[:, :], bass.IndirectOffsetOnAxis(ap=st_to[:, k, q:q + 1].bitcast(U32), axis=0),
                                                orow[:, BT * k + q, :], None, bounds_check=N - 1, oob_is_err=False
                                                ).then_inc(out_done, 16)

            steps(pool, NB2, 1, tokens)

        @block.vector
        def _(v):
            def done(ins):
                chain[0] += 1
                return ins.then_inc(dve, 1)

            def settle():
                v.wait_ge(dve, chain[0])

            asked = [0]

            def inverse_root(var_, y, t_):
                settle()
                asked[0] += 1
                done(v.tensor_copy(t_, var_))
                settle()
                v.sem_inc(sqrt_asked, 1)
                v.wait_ge(sqrt_done, asked[0])
                done(v.reciprocal(y, y))
                settle()
                done(v.tensor_tensor(t_, y, y, ALU.mult))
                settle()
                done(v.tensor_tensor(t_, t_, var_, ALU.mult))
                settle()
                done(v.tensor_scalar(t_, t_, -0.5, 1.5, ALU.mult, ALU.add))
                settle()
                done(v.tensor_tensor(y, y, t_, ALU.mult))
                settle()

            def finish_stats():
                settle()
                done(v.tensor_tensor(mean[:, :], stats[:, :, 1], stats[:, :, 4], ALU.add))
                done(v.tensor_tensor(tmp[:, :], stats[:, :, 1], stats[:, :, 4], ALU.subtract))
                done(v.tensor_tensor(var[:, :], stats[:, :, 2], stats[:, :, 5], ALU.add))
                settle()
                done(v.tensor_scalar(mean[:, :], mean[:, :], 0.5, None, ALU.mult))
                done(v.tensor_tensor(tmp[:, :], tmp[:, :], tmp[:, :], ALU.mult))
                done(v.tensor_scalar(var[:, :], var[:, :], 1.0 / C, LN_EPS, ALU.mult, ALU.add))
                settle()
                done(v.scalar_tensor_tensor(var[:, :], tmp[:, :], 0.25, var[:, :], ALU.mult, ALU.add))
                inverse_root(var[:, :], rstd[:, :], tmp[:, :])
                v.sem_inc(rstd_done, 1)

            v.wait_ge(edges_in, 32)
            v.wait_ge(consts, 10)
            done(v.memset(zeros[:, :], 0.0))
            done(v.memset(keys[0][:, :].bitcast(I32), SURPLUS))
            done(v.tensor_copy(iota[:, :], iotai[:, :]))
            done(v.tensor_copy(eiota[:, :], iotai[:, 0:NE]))
            done(v.tensor_copy(srcf[0:EP, :], srcdst[0:EP, 0, :]))
            settle()
            ki = keys[0][0:EP, 0:EC].bitcast(I32)
            done(v.tensor_scalar(ki, srcdst[0:EP, 0, :], DST_BITS, ONE_TAG, ALU.logical_shift_left, ALU.bitwise_or))
            settle()
            done(v.tensor_tensor(ki, ki, srcdst[0:EP, 1, :], ALU.bitwise_or))
            for w in range(NT):
                settle()
                done(v.tensor_scalar(keys[1][0:EP, 0:EC], srcf[0:EP, :], float((w + 1) * P), 0.0, ALU.is_lt, ALU.add,
                                     accum_out=cnt[0:EP, w:w + 1]))
            settle()
            v.sem_inc(cnt_ready, 1)

            v.wait_ge(x_in, 32)
            for t in range(NT):
                done(v.bn_stats(stats[:, t, :], xn[:, t, :]))
            finish_stats()
            for t in range(NT):
                v.tensor_scalar(xn[:, t, :], xn[:, t, :], mean[:, t:t + 1], rstd[:, t:t + 1],
                                ALU.subtract, ALU.mult).then_inc(xn_ready, 1)
            v.wait_ge(wt_mm, 2 * KH + 2)
            v.tensor_tensor(brow2[:, :], brow2[:, :], big[0:1, 3, 0:C + 2], ALU.subtract).then_inc(br2_ready, 1)

            counted = [0]

            def pad_keys(nw, unit, pno, pnof, pwin, pwini, to, tag, step_, offset):
                done(v.memset(tot[:, 0:1], 0.0))
                counted[0] += 1
                v.wait_ge(cnt_mm, counted[0])
                done(v.tensor_copy(tot[:, 1:nw + 1], keyps[:, 0, 0:nw]))
                settle()
                done(v.tensor_tensor(padf[:, 0:nw], tot[:, 1:nw + 1], tot[:, 0:nw], ALU.subtract))
                settle()
                done(v.tensor_scalar(toti[:, 0:nw], padf[:, 0:nw], float(unit - 1), None, ALU.add))
                settle()
                sh = unit.bit_length() - 1
                done(v.tensor_scalar(toti[:, 0:nw], toti[:, 0:nw], sh, sh, ALU.logical_shift_right, ALU.logical_shift_left))
                settle()
                done(v.tensor_tensor(padf[:, 0:nw], toti[:, 0:nw], padf[:, 0:nw], ALU.subtract))
                done(v.tensor_copy(pnof, pno))
                done(v.memset(pwin, 0.0))
                settle()
                done(v.tensor_tensor_scan(padcum[:, 0:nw], padf[:, 0:nw], zeros[:, 0:nw], 0.0, ALU.add, ALU.add))
                for w in range(nw):
                    settle()
                    done(v.scalar_tensor_tensor(pwin, pnof, padcum[:, w:w + 1], pwin, ALU.is_ge, ALU.add))
                settle()
                done(v.tensor_scalar(pwini, pwin, float(step_), float(offset), ALU.mult, ALU.add))
                settle()
                done(v.tensor_scalar(to.bitcast(I32), pwini, DST_BITS, PAD_DST | tag,
                                     ALU.logical_shift_left, ALU.bitwise_or))
                settle()

            pad_keys(NT, GT * P, padno, padnof, padwin, padwini, keys[0][:, EC:SC], ONE_TAG, P, P - 1)
            done(v.tensor_scalar(sgni[:, :], sgni[:, :], 1, None, ALU.bitwise_and))
            settle()
            done(v.tensor_scalar(sgn[:, :], sgni[:, :], -2.0, 1.0, ALU.mult, ALU.add))
            settle()

            turns = [0]

            def ask_turn():
                v.sem_inc(turn_asked, 1)
                turns[0] += 1
                v.wait_ge(turned, turns[0])

            def bitonic(bufs, cur, fb):
                width = 1 << fb
                low = min(fb, 7)
                twidth = P << max(fb - 7, 0)
                parts, tparts = P, 1 << low

                def exchange(cur, bit, np_, w):
                    a = bufs[cur][0:np_, 0:w].rearrange("p (b s q) -> p b s q", s=2, q=1 << bit)
                    b = bufs[1 - cur][0:np_, 0:w].rearrange("p (b s q) -> p b s q", s=2, q=1 << bit)
                    done(v.tensor_tensor(b[:, :, 0, :], a[:, :, 0, :], a[:, :, 1, :], ALU.min))
                    done(v.tensor_tensor(b[:, :, 1, :], a[:, :, 0, :], a[:, :, 1, :], ALU.max))
                    settle()
                    return 1 - cur

                def flip(cur, np_, w, q, lo, hi):
                    part = bufs[cur][0:np_, 0:w].rearrange("p (b q) -> p b q", q=q)[:, :, lo:hi]
                    done(v.tensor_scalar(part, part, -1.0, None, ALU.mult))
                    settle()

                def turn(cur, np_, w):
                    ask_turn()
                    for h in range(-(-w // 512)):
                        n = min(512, w)
                        done(v.tensor_copy(bufs[1 - cur][0:np_, h * 512:h * 512 + n], keyps[0:np_, h, 0:n]))
                    settle()
                    return 1 - cur

                flip(cur, parts, width, 4, 2, 4)
                for k in range(1, fb + 8):
                    if 2 <= k < fb:
                        flip(cur, parts, width, 4 << (k - 1), 1 << (k - 1), 3 << (k - 1))
                    if k == fb:
                        h = width // 2
                        done(v.tensor_scalar(bufs[cur][:, 0:h], bufs[cur][:, 0:h], sgn[:, :], None, ALU.mult))
                        done(v.tensor_scalar(bufs[cur][:, h:width], bufs[cur][:, h:width], sgn[:, :], -1.0,
                                             ALU.mult, ALU.mult))
                        settle()
                    if k <= fb:
                        for d in range(k - 1, -1, -1):
                            cur = exchange(cur, d, parts, width)
                        continue
                    cur = turn(cur, tparts, twidth)
                    b = k - 1 - fb
                    if k < fb + 7:
                        flip(cur, tparts, twidth, 4 << b, 1 << b, 3 << b)
                    else:
                        flip(cur, tparts, twidth, P, P // 2, P)
                    for d in range(k - 1, fb - 1, -1):
                        cur = exchange(cur, d - fb, tparts, twidth)
                    for d in range(fb - 1, 6, -1):
                        cur = exchange(cur, d, tparts, twidth)
                    cur = turn(cur, parts, width)
                    for d in range(low - 1, -1, -1):
                        cur = exchange(cur, d, parts, width)
                return cur

            cur = bitonic(keys, 0, FB)
            assert cur == E_END
            ask_turn()
            final = keys[1 - cur]
            fo = final[:, :].rearrange("p (r b) -> p b r", b=8)
            for h in range(2):
                done(v.tensor_copy(fo[:, 4 * h:4 * h + 4, :], keyps[:, h, :].rearrange("p (b r) -> p b r", b=4)))
            settle()
            fi = final[:, 0:NTL].bitcast(I32)
            lo_i = keys[cur][:, 0:NTL].bitcast(I32)
            done(v.tensor_scalar(dst_idx[:, :], fi, PAD_DST, None, ALU.bitwise_and))
            done(v.tensor_scalar(lo_i, fi, DST_BITS, P - 1, ALU.logical_shift_right, ALU.bitwise_and))
            done(v.tensor_scalar(win_i[:, :], fi.rearrange("p (g t) -> p g t", t=GT)[:, :, 0], DST_BITS + 7, 63,
                                 ALU.logical_shift_right, ALU.bitwise_and))
            settle()
            done(v.tensor_scalar(src_lo[:, :], dst_idx[:, :], float(N) - 0.5, float(P), ALU.is_gt, ALU.mult))
            settle()
            done(v.tensor_tensor(src_lo[:, :], src_lo[:, :], lo_i, ALU.add))
            done(v.tensor_scalar(dst_idx[:, :], dst_idx[:, :], float(NT * P - 1), None, ALU.min))
            settle()
            v.sem_inc(sorted_, 1)

            v.wait_ge(h_mm, NT)
            v.wait_ge(wt_mm, 2 * KH + 2)
            done(v.memset(arena[:, 0:(NT + 1) * HD], 0.0))
            settle()

            def split_scores(tab, nh):
                n = (NT + 1) * nh
                parts = s_parts[:, 0:3 * n].rearrange("p (t a h) -> p t a h", a=3, h=nh)
                rest = [tab] + [s_rest[:, k, 0:n] for k in range(2)]
                for k in range(3):
                    to = parts[:, :, k, :]
                    of = rest[k].rearrange("p (t h) -> p t h", h=nh)
                    done(v.tensor_copy(to, of))
                    settle()
                    if k < 2:
                        done(v.tensor_tensor(rest[k + 1].rearrange("p (t h) -> p t h", h=nh), of, to, ALU.subtract))
                        settle()
                v.sem_inc(s_split, 1)

            v.wait_ge(s_ready, NT)
            split_scores(s_tab[:, :], H)

            def aggregate(a, layer):
                nh, width, got, hr = (H, HD, got1, HR) if layer == 0 else (1, C, got2, HR2)

                def step(g, j):
                    k = (j + 5) % UG
                    if is_in(g + 5, NG):
                        wait(v, a.mm, g - 2)
                        lo = src_lo[:, bass.ds(GT * (g + 5), GT)]
                        v.tensor_tensor(hot[:, k, :, :], iota[:, :].rearrange("p (o n) -> p o n", o=1).broadcast_to([P, GT, P]),
                                        lo.rearrange("p (u o) -> p u o", o=1).broadcast_to([P, GT, P]),
                                        ALU.is_equal).then_inc(a.hot, 1)
                    k = (j + 2) % UG
                    if is_in(g + 2, NG):
                        wait(v, a.src_mm, g + 3)
                        turn = (g + 2) // UG if isinstance(g, int) else None
                        for u in range(GT):
                            if turn is not None:
                                v.wait_ge(a.got[GT * k + u], 16 * (turn + 1))
                            else:
                                v.wait_ge(a.got[GT * k + u], GT * (g + 2 - k) + 16)
                        v.tensor_tensor(score[:, k % 4, :, 0:nh], big[:, 2 + k % 2, 0:GT * nh].rearrange("p (u h) -> p u h", u=GT),
                                        got[:, GT * k:GT * k + GT, width:width + nh], ALU.add).then_inc(a.score, 1)
                        wait(v, a.score, g + 3)
                        v.scalar_tensor_tensor(lrel[:, k % 4, :, 0:nh], score[:, k % 4, :, 0:nh], LEAK, score[:, k % 4, :, 0:nh],
                                               ALU.mult, ALU.max).then_inc(a.lrel, 1)
                    k = (j + 1) % UG
                    if is_in(g + 1, NG):
                        wait(v, a.exp, g + 2)
                        wait(v, a.mm, g)
                        if layer == 0:
                            for u in range(GT):
                                ins = v.tensor_tensor(
                                    scaled1[:, k % 2, u, :].rearrange("p (h d) -> p h d", h=H),
                                    got[:, GT * k + u, 0:HD].rearrange("p (h d) -> p h d", h=H),
                                    ew[:, k % 4, u, :].rearrange("p (h o) -> p h o", o=1).broadcast_to([P, H, D]), ALU.mult)
                            ins.then_inc(a.scaled, 1)
                        else:
                            v.tensor_tensor(scaled2[:, k % 2, :, :], hot[:, k, :, :],
                                            ew[:, k % 4, :, 0:1].broadcast_to([P, GT, P]), ALU.mult).then_inc(a.scaled, 1)
                    if is_in(g - 1, NG):
                        w = v.value_load(win_i[0:1, bass.ds(g - 1, 1)], min_val=0, max_val=NT)
                        wait(v, a.mm, g)
                        wait(v, a.added, g - 1)
                        to = arena[:, bass.ds(w * width, width)]
                        v.tensor_tensor(to, to, big[:, (j + 1) % 2, 0:width], ALU.add).then_inc(a.added, 1)

                group_steps(v, step)
                v.wait_ge(a.added, NG)

            aggregate(agg[0], 0)

            def head_stats(t, j):
                for h in range(H):
                    ins = v.bn_stats(hstats[:, bass.ds(t * (H * 6) + h * 6, 6)], arena[:, bass.ds(t * HD + h * D, D)])
                ins.then_inc(sums, 1)

            steps(v, NT, 0, head_stats)
            v.wait_ge(sums, NT)
            hs = hstats.rearrange("p (n s) -> p n s", s=6)
            done(v.tensor_tensor(mean1, hs[:, :, 1], hs[:, :, 4], ALU.add))
            done(v.tensor_tensor(tmp1, hs[:, :, 1], hs[:, :, 4], ALU.subtract))
            done(v.tensor_tensor(var1, hs[:, :, 2], hs[:, :, 5], ALU.add))
            settle()
            done(v.tensor_scalar(mean1, mean1, 0.5, None, ALU.mult))
            done(v.tensor_tensor(tmp1, tmp1, tmp1, ALU.mult))
            done(v.tensor_scalar(var1, var1, 1.0 / D, LN_EPS, ALU.mult, ALU.add))
            settle()
            done(v.scalar_tensor_tensor(var1, tmp1, 0.25, var1, ALU.mult, ALU.add))
            inverse_root(var1, rstd1, tmp1)

            def by_head(ap):
                return ap.rearrange("p (h o) -> p h o", o=1).broadcast_to([P, H, D])

            def x1_tile(t, j):
                if is_in(t, NT):
                    tile = arena[:, cols(t, HD)].rearrange("p (h d) -> p h d", h=H)
                    v.tensor_tensor(tile, tile, by_head(mean1[:, cols(t, H)]), ALU.subtract).then_inc(centred, 1)
                    wait(v, centred, t + 1)
                    wait(v, x1t_mm, t - 1)
                    v.tensor_tensor(x1s[:, j, :].rearrange("p (h d) -> p h d", h=H), tile, by_head(rstd1[:, cols(t, H)]),
                                    ALU.mult).then_inc(x1_scaled, 1)
                if is_in(t - 1, NT):
                    wait(v, elu_act, t)
                    wait(v, h2_mm, t - 2)
                    v.scalar_tensor_tensor(u1[:, 1 - j, :], ex1[:, 1 - j, :], 1.0, re1[:, 1 - j, :],
                                           ALU.min, ALU.add).then_inc(elu_u, 1)

            steps(v, NT, 1, x1_tile)

            v.wait_ge(x1t_mm, NT)
            done(v.memset(arena[:, 0:(NT + 1) * C], 0.0))
            settle()
            v.wait_ge(s2_ready, NT)
            split_scores(s_tab2[:, :], 1)
            aggregate(agg[1], 1)

            def stat2(t, j):
                v.bn_stats(stats[:, bass.ds(t, 1), :].rearrange("p o s -> p (o s)"), arena[:, cols(t, C)]).then_inc(sum_done, 1)

            steps(v, NT, 0, stat2)
            v.wait_ge(sum_done, NT)
            finish_stats()

            v.wait_ge(gb_in, 32)

            def x2_tile(t, j):
                if is_in(t, NT):
                    v.scalar_tensor_tensor(yb[:, j, :], arena[:, cols(t, C)], mean[:, cols(t, 1)], goutb,
                                           ALU.subtract, ALU.mult).then_inc(y_norm, 1)
                    wait(v, y_norm, t + 1)
                    wait(v, elu2_act, t - 1)
                    v.scalar_tensor_tensor(zb[:, j, :], yb[:, j, :], rstd[:, cols(t, 1)], beoutb,
                                           ALU.mult, ALU.add).then_inc(z_ready, 1)
                if is_in(t - 1, NT):
                    k = 1 - j
                    wait(v, elu2_act, t)
                    v.scalar_tensor_tensor(u2[:, k, :], ex2[:, k, :], 1.0, re2[:, k, :], ALU.min, ALU.add).then_inc(u2_done, 1)
                    wait(v, u2_done, t)
                    if isinstance(t, int):
                        v.wait_ge(xre_in[k], 16 * ((t - 1) // 2 + 1))
                    else:
                        v.wait_ge(xre_in[k], 8 * (t - 1 - k) + 16)
                    tile = arena[:, cols(t - 1, C)]
                    v.scalar_tensor_tensor(tile, u2[:, k, :], -1.0, xre[:, k, :], ALU.add, ALU.add).then_inc(x2_done, 1)
                    wait(v, x2_done, t)
                    v.bn_stats(stats[:, bass.ds(t - 1, 1), :].rearrange("p o s -> p (o s)"), tile).then_inc(sum_done, 1)

            steps(v, NT, 1, x2_tile)
            v.wait_ge(sum_done, 2 * NT)
            finish_stats()

            def logits(b, j):
                if is_in(b, NB1):
                    wait(v, tok_stored[j], 16 * BT * (b - j))
                    wait(v, xn2T_mm, BT * (b - 1))
                    for q in range(BT if not isinstance(b, int) or b < NB1 - 1 else NT - BT * (NB1 - 1)):
                        t = BT * b + q
                        v.tensor_scalar(xn2[:, BT * j + q, :], arena[:, cols(t, C)], mean[:, cols(t, 1)], rstd[:, cols(t, 1)],
                                        ALU.subtract, ALU.mult).then_inc(xn2_ready, 1)
                if is_in(b - 1, NB1):
                    wait(v, lg_mm, b)
                    nq = BT if not isinstance(b, int) or b - 1 < NB1 - 1 else NT - BT * (NB1 - 1)
                    wait(v, lgt_mm, b - 1)
                    v.tensor_scalar(lgT[0:NE, 0:nq * P], keyps[0:NE, 0, 0:nq * P], bg_sb[:, 0:1], None, ALU.add).then_inc(lgT_ready, 1)
                    flat = lg.rearrange("p t e -> p (t e)")
                    wait(v, lgt_mm, b)
                    v.tensor_copy(flat[:, bass.ds((b - 1) * BT * NE, nq * NE)], keyps[:, 1, 0:nq * NE]).then_inc(lg_ready, 1)

            steps(v, NB1, 1, logits)
            v.wait_ge(lg_ready, NB1)

            def each(ap):
                return ap.rearrange("p (t o) -> p t o", o=1).broadcast_to([P, NT, NE])

            done(v.tensor_reduce(lgmax[:, :], lg, AX.X, ALU.max))
            settle()
            done(v.tensor_tensor(lg, lg, each(lgmax[:, :]), ALU.subtract))
            settle()
            v.sem_inc(lexp_asked, 1)
            v.wait_ge(lexp_done, 1)
            done(v.tensor_reduce(prob[:, :], lgx, AX.X, ALU.add))
            settle()
            done(v.reciprocal(prob[:, :], prob[:, :]))
            settle()
            done(v.tensor_copy(prob2[:, :, :], prob[:, :].rearrange("p (t o) -> p t o", o=1).broadcast_to([P, NT, 2])))
            settle()
            v.sem_inc(prob_ready, 1)
            done(v.tensor_scalar(lgx, lg, 0.0, float(NE), ALU.is_lt, ALU.mult))
            settle()
            done(v.tensor_tensor(lgx, lgx, eiota[:, :].rearrange("p (o e) -> p o e", o=1).broadcast_to([P, NT, NE]), ALU.add))
            done(v.memset(pick[:, :], float(2 * NE)))
            settle()
            done(v.tensor_reduce(pick[:, 0:NT - 1], lgx[:, 0:NT - 1, :], AX.X, ALU.min))
            done(v.tensor_reduce(pick[0:LASTP, NT - 1:NT], lgx[0:LASTP, NT - 1:NT, :], AX.X, ALU.min))
            settle()
            for e in range(NE):
                done(v.tensor_scalar(tmp[:, :], pick[:, :], float(e), 0.0, ALU.is_le, ALU.add, accum_out=cnt_e[:, e:e + 1]))
                settle()
            v.sem_inc(cnt_ready, 1)
            done(v.memset(tkeys[0][:, 0:TC].bitcast(I32), T_SURPLUS))
            done(v.tensor_copy(picki[:, :], pick[:, :]))
            settle()
            done(v.tensor_scalar(picki[:, :], picki[:, :], DST_BITS, ONE_TAG, ALU.logical_shift_left, ALU.bitwise_or))
            settle()
            done(v.tensor_tensor(tkeys[0][:, 0:NT - 1].bitcast(I32), picki[:, 0:NT - 1], tokno[:, 0:NT - 1], ALU.bitwise_or))
            done(v.tensor_tensor(tkeys[0][0:LASTP, NT - 1:NT].bitcast(I32), picki[0:LASTP, NT - 1:NT],
                                 tokno[0:LASTP, NT - 1:NT], ALU.bitwise_or))
            settle()
            pad_keys(NE, P, tpadno[:, :], tpadnof[:, :], tpadwin[:, :], tpadwini[:, :], tkeys[0][:, NT:TC], ONE_TAG, 1, 0)
            cur = bitonic(tkeys, 0, TFB)
            assert cur == T_END
            v.sem_inc(order_ready, 1)
            v.wait_ge(order_in, 16)
            done(v.tensor_scalar(tok_to[:, :], tord[:, :], PAD_DST, None, ALU.bitwise_and))
            done(v.tensor_scalar(exp_i[:, :], tord[:, :], DST_BITS, 15, ALU.logical_shift_right, ALU.bitwise_and))
            settle()
            done(v.tensor_scalar(tok_from[:, :], tok_to[:, :], float(NT * P - 1), None, ALU.min))
            done(v.tensor_scalar(exp_c[:, :], exp_i[:, :], float(NE - 1), float(MC * C), ALU.min, ALU.mult))
            done(v.tensor_scalar(exp_b[:, :], exp_i[:, :], float(NE - 1), float(C), ALU.min, ALU.mult))
            settle()
            v.sem_inc(order_dec, 1)

            def outputs(b, j):
                for q in range(BT):
                    t = BT * b + q
                    c = BT * j + q
                    wait(v, y_mm, t + 1)
                    wait(v, out_done, 16 * (t - 2 * BT + 1))
                    v.scalar_tensor_tensor(orow[:, c, :], keyps[:, q % 2, 0:C], tok[:, c, 2 * C:2 * C + 1], tok[:, c, 0:C],
                                           ALU.mult, ALU.add).then_inc(o_ready, 1)

            steps(v, NB2, 0, outputs)

        @block.scalar
        def _(act):
            act.dma_start(brow[:, 0:HD], b_heads.rearrange("h d -> (h d)").rearrange("(o n) -> o n", o=1)).then_inc(bh_in, 16)
            act.dma_start(brow2[:, 0:C], b_out.rearrange("(o n) -> o n", o=1)).then_inc(bh_in, 16)
            asked = [0]

            def root(y, v_):
                asked[0] += 1
                act.wait_ge(sqrt_asked, asked[0])
                act.activation(y, v_, ACT.Sqrt).then_inc(sqrt_done, 1)

            root(rstd[:, :], var[:, :])
            for c in range(KH):
                act.wait_ge(wt_mm, c + 1)
                act.activation(wT[:, :, c * P:(c + 1) * P], tps[:, c % 2, 0:KF * P].rearrange("p (k q) -> p k q", k=KF),
                               ACT.Copy).then_inc(wt_ready, 1)
            for c in range(KH):
                act.wait_ge(wt_mm, KH + c + 1)
                act.activation(woT[:, c, 0:C], tps[:, c % 2, 0:C], ACT.Copy).then_inc(wt_ready, 1)
            act.wait_ge(wt_mm, 2 * KH + 1)
            act.activation(wT[:, :, HD:HD + 2 * H], big[:, 1, 0:KF * 2 * H].rearrange("p (k q) -> p k q", k=KF),
                           ACT.Copy).then_inc(wt_ready, 1)
            act.activation(brow[:, HD:HD + 2 * H], big[0:1, 2, 0:2 * H], ACT.Copy).then_inc(wt_ready, 1)
            act.activation(woT[:, :, C:C + 2], big[:, 0, 0:KH * 2].rearrange("p (k q) -> p k q", k=KH),
                           ACT.Copy).then_inc(wt_ready, 1)
            act.activation(brow2[:, C:C + 2], big[0:1, 3, 0:2], ACT.Copy).then_inc(wt_ready, 1)

            def rows1(t, j):
                wait(act, xt_mm, t + 1)
                act.activation(xnT[:, j, :, :], tps[:, j, 0:KF * P].rearrange("p (k q) -> p k q", k=KF),
                               ACT.Copy).then_inc(xt_ready, 1)
                wait(act, h_mm, t + 1)
                if isinstance(t, int):
                    wait(act, h_stored[j], 16 * (t // 2))
                else:
                    act.wait_ge(h_stored[j], 8 * (t - j))
                act.activation(s_tab[:, cols(t, H)], big[:, 2 * j + 1, 0:H], ACT.Copy).then_inc(s_ready, 1)
                act.activation(hrow[:, j, 0:HD], big[:, 2 * j, 0:HD], ACT.Copy)
                act.activation(hrow[:, j, HD:HR], big[:, 2 * j + 1, H:2 * H], ACT.Copy).then_inc(h_ready, 1)

            act.wait_ge(consts, 10)
            steps(act, NT, 0, rows1)

            def weights(a, layer):
                nh = H if layer == 0 else 1

                def step(g, j):
                    if is_in(g + 4, NG):
                        wait(act, a.hotT_mm, g + 5)
                        wait(act, a.src_mm, g + 3)
                        act.activation(hotT[:, j % 2, :, :], tps[:, j % 2, 0:GT * P].rearrange("p (u q) -> p u q", u=GT),
                                       ACT.Copy).then_inc(a.hotT, 1)
                    if is_in(g + 2, NG):
                        k = (j + 2) % 4
                        wait(act, a.lrel, g + 3)
                        wait(act, a.scaled, g - 1)
                        act.activation(ew[:, k, :, 0:nh], lrel[:, k, :, 0:nh], ACT.Exp, scale=-1.0).then_inc(a.exp, 1)

                group_steps(act, step)

            weights(agg[0], 0)

            root(rstd1, var1)

            def elu1(t, j):
                if is_in(t, NT):
                    wait(act, x1t_mm, t + 1)
                    wait(act, elu_u, t - 1)
                    for c in range(KH):
                        z = tps[:, j, c * P:(c + 1) * P]
                        act.activation(ex1[:, j, c * P:(c + 1) * P], z, ACT.Exp, bias=becol[:, c:c + 1], scale=gcol[:, c:c + 1])
                        ins = act.activation(re1[:, j, c * P:(c + 1) * P], z, ACT.Relu, bias=becol[:, c:c + 1], scale=gcol[:, c:c + 1])
                    ins.then_inc(elu_act, 1)
                if is_in(t - 2, NT):
                    wait(act, h2_mm, t - 1)
                    if isinstance(t, int):
                        wait(act, h2_stored[j], 16 * ((t - 2) // 2))
                    else:
                        act.wait_ge(h2_stored[j], 8 * (t - 2 - j))
                    act.activation(s_tab2[:, cols(t - 2, 1)], big[:, j, C:C + 1], ACT.Copy).then_inc(s2_ready, 1)
                    act.activation(hrow[:, j, 0:C], big[:, j, 0:C], ACT.Copy)
                    act.activation(hrow[:, j, C:C + 1], big[:, j, C + 1:C + 2], ACT.Copy).then_inc(h2_ready, 1)

            def elu1_first(t, j):
                elu1(t, j)

            for t in range(4):
                elu1(t, t % 2)
            with act.Fori(2, NT // 2) as i:
                elu1(2 * i, 0)
                elu1(2 * i + 1, 1)
            for t in range(2 * (NT // 2), NT + 2):
                elu1(t, t % 2)

            weights(agg[1], 1)
            root(rstd[:, :], var[:, :])

            def elu2(t, j):
                wait(act, z_ready, t + 1)
                wait(act, u2_done, t - 1)
                act.activation(ex2[:, j, :], zb[:, j, :], ACT.Exp)
                act.activation(re2[:, j, :], zb[:, j, :], ACT.Relu).then_inc(elu2_act, 1)

            steps(act, NT, 0, elu2)
            root(rstd[:, :], var[:, :])

            def hidden(b, j, nq, t_mm, t_ready, u_mm, u_ready, used, to, x_used):
                for q in range(nq):
                    wait(act, t_mm, BT * b + q + 1)
                    if q == 0:
                        wait(act, x_used, MC * (b - 1))
                    act.activation(to(j)[:, :, q * P:(q + 1) * P], tps[:, q % 2, 0:KF * P].rearrange("p (k q) -> p k q", k=KF),
                                   ACT.Copy).then_inc(t_ready, 1)
                wait(act, used, b)
                for c in range(MC):
                    wait(act, u_mm, MC * b + c + 1)
                    act.activation(hT[:, c, 0:nq * P], big[:, c % 4, 0:nq * P], ACT.Gelu, bias=b1c[:, c:c + 1]).then_inc(u_ready, 1)

            def last1(b):
                return BT if not isinstance(b, int) or b < NB1 - 1 else NT - BT * (NB1 - 1)

            steps(act, NB1, 0, lambda b, j: hidden(b, j, last1(b), xn2T_mm, xn2T_ready, up_mm, up_ready, lg_mm,
                                                   lambda j: xT[j], up_mm))
            act.wait_ge(lexp_asked, 1)
            act.activation(lgx, lg, ACT.Exp).then_inc(lexp_done, 1)
            act.wait_ge(prob_stored, 16)
            steps(act, NB2, 0, lambda b, j: hidden(b, j, BT, xt2_mm, xt2_ready, up2_mm, up2_ready, y_batch,
                                                   lambda j: xT[j], up2_mm))

        @block.tensor
        def _(pe):
            pe.wait_ge(consts, 10)
            pe.wait_ge(cnt_ready, 1)
            pe.matmul(keyps[:, 0, 0:NT], ones[0:EP, :], cnt[0:EP, :], start=True, stop=True).then_inc(cnt_mm, 1)
            pe.wait_ge(w_in, 16 * (2 + 7 + 2 * H + 2))
            for c in range(2 * KH):
                if c >= 2:
                    pe.wait_ge(wt_ready, c - 1)
                for k in range(KF):
                    raw = wraw[:, c, k * P:(k + 1) * P] if c < KH else woraw[:, k, (c - KH) * P:(c - KH + 1) * P]
                    last = pe.transpose(tps[:, c % 2, k * P:(k + 1) * P], raw, ident[:, :])
                last.then_inc(wt_mm, 1)
            for k in range(KF):
                for c in range(KH):
                    pe.matmul(big[:, 1, k * 2 * H:(k + 1) * 2 * H], wraw[:, c, k * P:(k + 1) * P], amat[:, c, :],
                              start=(c == 0), stop=(c == KH - 1))
            for c in range(KH):
                pe.matmul(big[0:1, 2, 0:2 * H], bcol[:, c:c + 1], amat[:, c, :], start=(c == 0), stop=(c == KH - 1))
            for c in range(KH):
                for m in range(KF):
                    pe.matmul(big[:, 0, 2 * c:2 * c + 2], woraw[:, m, c * P:(c + 1) * P], a2[:, m, :],
                              start=(m == 0), stop=(m == KF - 1))
            for m in range(KF):
                last = pe.matmul(big[0:1, 3, 0:2], bocol[:, m:m + 1], a2[:, m, :], start=(m == 0), stop=(m == KF - 1))
            last.then_inc(wt_mm, 1)
            pe.wait_ge(wt_ready, 2 * KH + 4)
            pe.wait_ge(bh_in, 32)
            for c in range(KH):
                last = pe.matmul(big[0:1, 3, 0:C + 2], ones[:, 0:1], woT[:, c, :], start=(c == 0), stop=(c == KH - 1))
            last.then_inc(wt_mm, 1)

            def turn_x(t, j):
                wait(pe, xn_ready, t + 1)
                wait(pe, xt_ready, t - 1)
                for k in range(KF):
                    last = pe.transpose(tps[:, j, k * P:(k + 1) * P], xn[:, t, k * P:(k + 1) * P], ident[:, :])
                last.then_inc(xt_mm, 1)

            def h1(t, j):
                wait(pe, xt_ready, t + 1)
                wait(pe, h_ready, t - 1)
                for lo, n, bank in ((0, HD, 2 * j), (HD, 2 * H, 2 * j + 1)):
                    for k in range(KF):
                        pe.matmul(big[:, bank, 0:n], xnT[:, j, k, :], wT[:, k, lo:lo + n], start=(k == 0), stop=False)
                    last = pe.matmul(big[:, bank, 0:n], ones[0:1, :], brow[:, lo:lo + n], start=False, stop=True)
                last.then_inc(h_mm, 1)

            pe.wait_ge(br2_ready, 1)

            turns = 0
            before = NT - 2 * len(E_TURNS)
            for t in range(NT):
                turn_x(t, t % 2)
                h1(t, t % 2)
                if t >= before and (t - before) % 2 == 0:
                    c = E_TURNS[turns]
                    turns += 1
                    pe.wait_ge(turn_asked, turns)
                    for b in range(SC // P):
                        last = pe.transpose(keyps[:, b // 4, (b % 4) * P:(b % 4 + 1) * P], keys[c][:, b * P:(b + 1) * P],
                                            ident[:, :])
                    last.then_inc(turned, 1)
            assert turns == len(E_TURNS)

            def sums_of(a, layer):
                nh, width, got, tab = (H, HD, got1, s_parts) if layer == 0 else (1, C, got2, s_parts)
                pe.wait_ge(s_split, layer + 1)

                def step(g, j):
                    if is_in(g + 4, NG):
                        k = (j + 4) % UG
                        wait(pe, a.hot, g + 5)
                        wait(pe, a.hotT, g + 3)
                        for u in range(GT):
                            last = pe.transpose(tps[:, k % 2, u * P:(u + 1) * P], hot[:, k, u, :], ident[:, :])
                        last.then_inc(a.hotT_mm, 1)
                    if is_in(g + 3, NG):
                        k = (j + 3) % UG
                        w = pe.value_load(win_i[0:1, bass.ds(g + 3, 1)], min_val=0, max_val=NT)
                        wait(pe, a.hotT, g + 4)
                        wait(pe, a.score, g + 2)
                        for u in range(GT):
                            for part in range(3):
                                last = pe.matmul(big[:, 2 + k % 2, u * nh:(u + 1) * nh], hotT[:, k % 2, u, :],
                                                 tab[:, bass.ds(w * (3 * nh) + part * nh, nh)], start=(part == 0), stop=(part == 2))
                        last.then_inc(a.src_mm, 1)
                    if is_in(g, NG):
                        wait(pe, a.scaled, g + 1)
                        wait(pe, a.added, g - 1)
                        for u in range(GT):
                            if layer == 0:
                                lhs, rhs = hot[:, j, u, :], scaled1[:, j % 2, u, :]
                            else:
                                lhs, rhs = scaled2[:, j % 2, u, :], got[:, GT * j + u, 0:C]
                            last = pe.matmul(big[:, j % 2, 0:width], lhs, rhs, start=(u == 0), stop=(u == GT - 1))
                        last.then_inc(a.mm, 1)

                group_steps(pe, step)

            sums_of(agg[0], 0)

            def h2(t, j):
                if is_in(t, NT):
                    wait(pe, x1_scaled, t + 1)
                    wait(pe, elu_act, t - 1)
                    for c in range(KH):
                        last = pe.transpose(tps[:, j, c * P:(c + 1) * P], x1s[:, j, c * P:(c + 1) * P], ident[:, :])
                    last.then_inc(x1t_mm, 1)
                if is_in(t - 1, NT):
                    k = 1 - j
                    wait(pe, elu_u, t)
                    wait(pe, h2_ready, t - 2)
                    for c in range(KH):
                        pe.matmul(big[:, k, 0:C + 2], u1[:, k, c * P:(c + 1) * P], woT[:, c, :], start=(c == 0), stop=False)
                    pe.matmul(big[:, k, 0:C + 2], ones[0:1, :], brow2[:, :], start=False, stop=True).then_inc(h2_mm, 1)

            steps(pe, NT, 1, h2)
            sums_of(agg[1], 1)

            def last1(b):
                return BT if not isinstance(b, int) or b < NB1 - 1 else NT - BT * (NB1 - 1)

            def up(b, j, nq, src_of, ready_of, t_mm, t_ready, u_mm, u_ready):
                for q in range(nq):
                    ready_of(b, j, q)
                    wait(pe, t_ready, BT * b + q - 1)
                    for k in range(KF):
                        last = pe.transpose(tps[:, q % 2, k * P:(k + 1) * P], src_of(j, q)[:, k * P:(k + 1) * P], ident[:, :])
                    last.then_inc(t_mm, 1)
                wait(pe, t_ready, BT * b + nq)
                for c in range(MC):
                    wait(pe, u_ready, MC * b + c - 3)
                    for k in range(KF):
                        last = pe.matmul(big[:, c % 4, 0:nq * P], w1_sb[:, k, c * P:(c + 1) * P], xT[j][:, k, 0:nq * P],
                                         start=(k == 0), stop=(k == KF - 1))
                    last.then_inc(u_mm, 1)

            pe.wait_ge(w1_in, 16)

            def logit_batch(b, j):
                nq = last1(b)
                up(b, j, nq, lambda j, q: xn2[:, BT * j + q, :], lambda b, j, q: wait(pe, xn2_ready, BT * b + q + 1),
                   xn2T_mm, xn2T_ready, up_mm, up_ready)
                wait(pe, up_ready, MC * (b + 1))
                wait(pe, lgT_ready, b)
                for c in range(MC):
                    last = pe.matmul(keyps[0:NE, 0, 0:nq * P], wg_sb[:, c, :], hT[:, c, 0:nq * P],
                                     start=(c == 0), stop=(c == MC - 1))
                last.then_inc(lg_mm, 1)

            def logit_turn(b, j):
                wait(pe, lgT_ready, b + 1)
                wait(pe, lg_ready, b)
                pe.sem_inc(pe_gate, 1)
                for q in range(last1(b)):
                    last = pe.transpose(keyps[:, 1, q * NE:(q + 1) * NE], lgT[0:NE, q * P:(q + 1) * P], ident[0:NE, 0:NE])
                last.then_inc(lgt_mm, 1)

            def logit_both(b, j):
                logit_batch(b, j)
                logit_turn(b, j)

            steps(pe, NB1, 0, logit_both)
            pe.wait_ge(cnt_ready, 2)
            pe.matmul(keyps[:, 0, 0:NE], ones[:, :], cnt_e[:, :], start=True, stop=True).then_inc(cnt_mm, 1)
            for n, c in enumerate(T_TURNS):
                turns += 1
                pe.wait_ge(turn_asked, turns)
                if n % 2 == 0:
                    pe.transpose(keyps[0:TC, 0, 0:P], tkeys[c][:, 0:TC], ident[:, :]).then_inc(turned, 1)
                else:
                    pe.transpose(keyps[:, 0, 0:TC], tkeys[c][0:TC, :], ident[0:TC, 0:TC]).then_inc(turned, 1)

            pe.wait_ge(wd_in, 16 * NE)
            pe.wait_ge(order_dec, 1)
            pe.wait_ge(bd_in, 16)

            def expert_batch(b, j):
                def arrived(b, j, q):
                    if isinstance(b, int):
                        pe.wait_ge(tok_in[BT * j + q], 16 * (b // 2 + 1))
                    else:
                        pe.wait_ge(tok_in[BT * j + q], 8 * (b - j) + 16)

                up(b, j, BT, lambda j, q: tok[:, BT * j + q, C:2 * C], arrived, xt2_mm, xt2_ready, up2_mm, up2_ready)
                wait(pe, up2_ready, MC * (b + 1))
                for q in range(BT):
                    t = BT * b + q
                    e = pe.value_load(exp_c[0:1, cols(t, 1)], min_val=0, max_val=(NE - 1) * MC * C)
                    eb = pe.value_load(exp_b[0:1, cols(t, 1)], min_val=0, max_val=(NE - 1) * C)
                    wait(pe, o_ready, t - 1)
                    for c in range(MC):
                        pe.matmul(keyps[:, q % 2, 0:C], hT[:, c, q * P:(q + 1) * P], wd_sb[:, bass.ds(e + c * C, C)],
                                  start=(c == 0), stop=False)
                    last = pe.matmul(keyps[:, q % 2, 0:C], ones[0:1, :], bd_sb[:, bass.ds(eb, C)], start=False, stop=True)
                    last.then_inc(y_mm, 1)
                pe.sem_inc(y_batch, 1)

            steps(pe, NB2, 0, expert_batch)


_INS = ['x', 'src', 'dst', 'L0_gnn_W_heads', 'L0_gnn_b_heads', 'L0_gnn_a_heads', 'L0_gnn_g_heads', 'L0_gnn_beta_heads',
        'L0_gnn_W_out', 'L0_gnn_b_out', 'L0_gnn_a_out', 'L0_gnn_g_out', 'L0_gnn_beta_out',
        'L0_ffn_W1', 'L0_ffn_b1', 'L0_ffn_Wg', 'L0_ffn_bg', 'L0_ffn_Wd', 'L0_ffn_bd']
_OUTS = [((6250, 256), 'float32')]


def kernel(**inputs):
    import numpy as _np
    import concourse.bacc as _bacc
    from concourse import mybir as _mybir
    from concourse.bass_utils import run_bass_kernel_spmd as _run

    nc = _bacc.Bacc("TRN2", target_bir_lowering=False, num_devices=1)
    arrays, args = {}, []
    for name in _INS:
        a = _np.ascontiguousarray(inputs[name])
        arrays[f"in_{name}_dram"] = a
        args.append(nc.dram_tensor(f"in_{name}_dram", a.shape, _mybir.dt.from_np(a.dtype), kind="ExternalInput").ap())
    for i, (shape, dtype) in enumerate(_OUTS):
        dt = _mybir.dt.from_np(_np.dtype(dtype))
        args.append(nc.dram_tensor(f"out_{i}_dram", shape, dt, kind="ExternalOutput").ap())
    build(nc, *args)
    r = _run(nc, [arrays], core_ids=[0])
    return r.results[0]["out_0_dram"]
```

```python
from contextlib import ExitStack

import concourse.bass as bass
from concourse import mybir

P = 128
F32 = mybir.dt.float32
I32 = mybir.dt.int32
BF16 = mybir.dt.bfloat16
U32 = mybir.dt.uint32
ALU = mybir.AluOpType
ACT = mybir.ActivationFunctionType
AX = mybir.AxisListType

ONE_TAG = 0x40000000
DST_BITS = 13
PAD_DST = (1 << DST_BITS) - 1
LN_EPS = 1e-5
LEAK = 0.2
ROOT_SEED = 0x5f3759df


def build(nc, x, src, dst, W_heads, b_heads, a_heads, g_heads, beta_heads, W_out, b_out, a_out, g_out, beta_out,
          W1, b1, Wg, bg, Wd, bd, out):
    N, C = x.shape
    E = src.shape[0]
    H, D, _ = W_heads.shape
    HD = H * D
    HID = W1.shape[1]
    NE = Wg.shape[1]
    NT = -(-N // P)
    LASTP = N - (NT - 1) * P
    KF = C // P
    KH = HD // P
    HR = HD + H
    HR2 = C + 4
    MC = HID // P

    EP = 125
    EC = E // EP
    SC = 1024
    PC = SC - EC
    FB = SC.bit_length() - 1
    GT = 2
    UG = 8
    NG = -(-((E + NT * (GT * P - 1)) // (GT * P)) // UG) * UG
    NTL = NG * GT
    US = UG * GT
    HV = H - 2
    SURPLUS = ((NT * P + P - 1) << DST_BITS) | PAD_DST | ONE_TAG
    assert EP * EC == E and P * PC >= NT * (GT * P - 1) and NTL <= SC and N <= NT * P < PAD_DST

    TC = 64
    TFB = TC.bit_length() - 1
    TPC = TC - NT
    BT = 4
    NB1 = -(-NT // BT)
    NB2 = -(-((N + NE * (P - 1)) // P) // BT)
    TT = NB2 * BT
    T_SURPLUS = (NE << DST_BITS) | PAD_DST | ONE_TAG
    assert P * TPC >= NE * (P - 1) and TT <= TC and NB2 % 2 == 0 and NB1 % 2 == 1
    XR = C + 2 + HID
    HB = HID // 2

    with ExitStack() as ctx:
        def sb(name, shape, dt=F32):
            return ctx.enter_context(nc.sbuf_tensor(name, shape, dt))

        def ps(name, shape, dt=F32):
            return ctx.enter_context(nc.psum_tensor(name, shape, dt))

        def sem(name):
            return ctx.enter_context(nc.semaphore(name))

        h1_dram = nc.dram_tensor("h1_rows", (NT * P, HR), F32, kind="Internal").ap()
        h2_dram = nc.dram_tensor("h2_rows", (NT * P, HR2), F32, kind="Internal").ap()
        tok_dram = nc.dram_tensor("token_rows", (NT * P, XR), F32, kind="Internal").ap()
        order_dram = nc.dram_tensor("token_order", (P * TC,), F32, kind="Internal").ap()

        WD0 = (NT + 1) * C
        arena = sb("arena", [P, max((NT + 1) * HD, WD0 + NE * MC * C)])
        xn = arena[:, 0:NT * C].rearrange("p (t f) -> p t f", t=NT)
        wraw = arena[:, NT * C:NT * C + KH * C].rearrange("p (c f) -> p c f", c=KH)
        wo0 = NT * C + KH * C
        woraw = arena[:, wo0:wo0 + KF * HD].rearrange("p (m f) -> p m f", m=KF)
        wd_sb = arena[:, WD0:WD0 + NE * MC * C]
        work = sb("work", [P, US * HR])
        got1 = work[:, :].rearrange("p (s r) -> p s r", s=US)
        got2 = work[:, 0:US * HR2].rearrange("p (s r) -> p s r", s=US)
        srcdst = work[:, 0:2 * EC].bitcast(I32).rearrange("p (a c) -> p a c", a=2)
        src_win = work[:, 2 * EC:3 * EC]
        src_winb = work[:, 3 * EC + 4 * PC + P:3 * EC + 4 * PC + P + EC // 2].bitcast(BF16)
        padno = work[:, 3 * EC:3 * EC + PC].bitcast(I32)
        padnof = work[:, 3 * EC + PC:3 * EC + 2 * PC]
        padwin = work[:, 3 * EC + 2 * PC:3 * EC + 3 * PC]
        padwini = work[:, 3 * EC + 3 * PC:3 * EC + 4 * PC].bitcast(I32)

        def ring(n, width, depth=2):
            return work[:, n:n + depth * width].rearrange("p (s w) -> p s w", s=depth)

        hstats = work[:, 11 * HD:11 * HD + NT * H * 6]
        assert 11 * HD + NT * H * 6 <= US * HR and 4 * HR2 + C + 2 <= 3 * HD
        x1s = ring(0, 2 * HD)
        u1 = ring(4 * HD, 2 * HD)
        h2row = ring(8 * HD, HR2, 4)
        bias2 = work[:, 8 * HD + 4 * HR2:8 * HD + 4 * HR2 + C + 2]
        hT = work[:, 0:MC * BT * P].rearrange("p (c q) -> p c q", c=MC)
        node = work[:, MC * BT * P:MC * BT * P + 2 * BT * 2 * C].rearrange("p (s r) -> p s r", s=2 * BT)
        xn2 = node[:, :, C:2 * C]
        orow = work[:, MC * BT * P:MC * BT * P + 2 * BT * C].rearrange("p (s c) -> p s c", s=2 * BT)
        hrows = arena[:, WD0:WD0 + 2 * BT * HID].rearrange("p (s r) -> p s r", s=2 * BT)
        tok = arena[:, 0:2 * BT * XR].rearrange("p (s r) -> p s r", s=2 * BT)
        xre = arena[:, WD0 + 2 * BT * HID:WD0 + 2 * BT * (HID + C)].rearrange("p (s q c) -> p s q c", s=2, q=BT)
        assert MC * BT * P + 2 * BT * 2 * C <= US * HR and 2 * BT * XR <= WD0 and 2 * BT * (HID + C) <= NE * MC * C
        lgx = work[:, 0:NT * NE].rearrange("p (t e) -> p t e", t=NT)

        ident = sb("ident", [P, P])
        iota = sb("iota", [P, P])
        iotai = work[:, 3 * EC + 4 * PC:3 * EC + 4 * PC + P].bitcast(I32)
        ones = sb("ones", [P, P])
        wT = sb("wT", [P, KF, HD + 2 * H])
        amat = sb("amat", [P, KH, 2 * H])
        bcol = sb("bcol", [P, KH])
        brow = sb("brow", [1, HD + 2 * H])
        woT = sb("woT", [P, KH, C + 2])
        a2 = sb("a2", [P, KF, 2])
        bocol = sb("bocol", [P, KF])
        brow2 = sb("brow2", [1, C + 2])
        gcol = sb("gcol", [P, KH])
        becol = sb("becol", [P, KH])
        goutb, beoutb = wT[:, 0, 0:C], wT[:, 1, 0:C]
        CG = 32
        wg_cg = wT[:, 0, C:C + MC * CG].rearrange("p (c e) -> p c e", c=MC)
        stats = sb("stats", [P, NT, 6])
        mean = sb("mean", [P, NT])
        var = sb("var", [P, NT])
        rstd = sb("rstd", [P, NT])
        tmp = sb("tmp", [P, NT])
        xnT = work[:, 8 * HD:9 * HD].rearrange("p (s k q) -> p s k q", s=2, k=KF)
        hrow = ring(11 * HD, HR)
        hraw = ring(11 * HD + 2 * HR, HR)
        bias1 = work[:, 9 * HD:9 * HD + HR]
        bias_s = sb("bias_s", [P, H])
        s_tab = sb("s_tab", [P, (NT + 1) * H])
        s_tab2 = sb("s_tab2", [P, NT + 1])
        lg = s_tab[:, 0:NT * NE].rearrange("p (t e) -> p t e", t=NT)

        keys = [sb("keys_a", [P, SC]), sb("keys_b", [P, SC])]
        var1, rstd1 = (keys[0][:, n * NT * H:(n + 1) * NT * H] for n in range(2))
        mean1, tmp1 = (keys[1][:, n * NT * H:(n + 1) * NT * H] for n in range(2))
        xT = [k[:, :].rearrange("p (k q) -> p k q", k=KF) for k in keys]
        cnt = sb("cnt", [P, NT])
        tot = sb("tot", [P, NT + 1])
        toti = sb("toti", [P, NT], I32)
        padf = sb("padf", [P, NT])
        padcum = sb("padcum", [P, NT])
        zeros = sb("zeros", [P, NT])
        sgn = sb("sgn", [P, 1])
        sgni = sb("sgni", [P, 1], I32)
        dst_idx = sb("dst_idx", [P, NTL], I32)
        src_lo = sb("src_lo", [P, NTL])
        win_i = sb("win_i", [P, NG], I32)
        win_pe = sb("win_pe", [P, NG // 4], I32)
        win_dve = sb("win_dve", [P, NG // 4], I32)
        staged = sb("staged", [P, 2, US // 2], I32)

        hot = sb("hot", [P, UG, GT, P])
        hotT = sb("hotT", [P, 2, GT, P], BF16)
        s_parts = sb("s_parts", [P, (NT + 1) * 3 * H], BF16)
        s_rest = keys[0][:, 0:2 * (NT + 1) * H].rearrange("p (a n) -> p a n", a=2)
        score = sb("score", [P, 4, GT, H])
        lrel = sb("lrel", [P, 4, GT, H])
        ew = sb("ew", [P, 4, GT, H])
        scaled = sb("scaled", [P, 2 * GT * HD])
        scaled1 = scaled[:, :].rearrange("p (s u f) -> p s u f", s=2, u=GT)
        scaled2 = scaled[:, 0:2 * GT * P].rearrange("p (s u f) -> p s u f", s=2, u=GT)
        w1_sb = scaled[:, :].rearrange("p (k f) -> p k f", k=KF)
        assert 2 * GT * HD == KF * HID

        b1c = sb("b1c", [P, MC])
        wg_sb = sb("wg_sb", [P, MC, NE])
        bg_sb = sb("bg_sb", [NE, 1])
        bg_cg = sb("bg_cg", [P, 1])
        eiota = sb("eiota", [P, NE])
        lgmax = sb("lgmax", [P, NT])
        prob = sb("prob", [P, NT])
        bst = sb("bst", [P, BT, 6])
        bsm = sb("bsm", [P, 4, BT])
        pick = sb("pick", [P, NT])
        cnt_e = sb("cnt_e", [P, NE])
        tokno = sb("tokno", [P, NT], I32)
        picki = sb("picki", [P, NT], I32)
        tpadno = sb("tpadno", [P, TPC], I32)
        tpadnof = sb("tpadnof", [P, TPC])
        tpadwin = sb("tpadwin", [P, TPC])
        tpadwini = sb("tpadwini", [P, TPC], I32)
        hotf = hot[:, :, :, :].rearrange("p a b c -> p (a b c)")
        ex1 = hotf.rearrange("p (s w) -> p s w", s=2)
        re1 = scaled[:, :].rearrange("p (s w) -> p s w", s=2)
        expz = hotf[:, 0:BT * C].rearrange("p (q c) -> p q c", q=BT)
        lgT = hotf[:, 8 * P:8 * P + BT * P]
        tkeys = [hotf[:, n * P:(n + 1) * P] for n in range(2)]
        tord, tok_to, tok_from, exp_i, exp_c, exp_b = (hotf[:, 2 * P + n * TC:2 * P + (n + 1) * TC].bitcast(I32) for n in range(6))
        st_from = sb("st_from", [P, 2, BT], I32)
        st_to = sb("st_to", [P, 2, BT], I32)
        bd_sb = scaled[:, 0:NE * C]

        big = ps("big", [P, 4, 512])
        tps = ps("tps", [P, 2, 512])
        keyps = ps("keyps", [P, 2, 512])

        x_in, w_in, edges_in, zero_x, consts = sem("x_in"), sem("w_in"), sem("edges_in"), sem("zero_x"), sem("consts")
        dve, pool_own = sem("dve"), sem("pool_own")
        sqrt_asked, sqrt_done, xn_ready = sem("sqrt_asked"), sem("sqrt_done"), sem("xn_ready")
        wt_mm, wt_ready, bh_in = sem("wt_mm"), sem("wt_ready"), sem("bh_in")
        xt_mm, xt_ready, h_mm, h_ready = sem("xt_mm"), sem("xt_ready"), sem("h_mm"), sem("h_ready")
        s_ready = sem("s_ready")
        h_stored = [sem("h_stored0"), sem("h_stored1")]
        cnt_ready, cnt_mm, turn_asked, turned = sem("cnt_ready"), sem("cnt_mm"), sem("turn_asked"), sem("turned")
        sorted_ = sem("sorted")

        class Agg:
            def __init__(self, n):
                self.staged = sem(f"idx_staged{n}")
                self.got = [sem(f"got{n}_{c}") for c in range(US)]
                self.hot = sem(f"hot{n}")
                self.hotT_mm = sem(f"hotT_mm{n}")
                self.hotT = sem(f"hotT{n}")
                self.src_mm = sem(f"src_mm{n}")
                self.score = sem(f"score{n}")
                self.lrel = sem(f"lrel{n}")
                self.exp = sem(f"exp{n}")
                self.scaled = sem(f"scaled{n}")
                self.scaled_act = sem(f"scaled_act{n}")
                self.mm = sem(f"agg_mm{n}")
                self.added = sem(f"added{n}")

        agg = [Agg(1), Agg(2)]

        centred, zeroed = sem("centred"), sem("zeroed")
        x1_scaled, x1t_mm, elu_act, elu_u, h2_mm, h2_ready = (sem("x1_scaled"), sem("x1t_mm"), sem("elu_act"),
                                                              sem("elu_u"), sem("h2_mm"), sem("h2_ready"))
        s2_ready, bias2_mm, bias2_ready, means = sem("s2_ready"), sem("bias2_mm"), sem("bias2_ready"), sem("means")
        h2_stored = [sem("h2_stored0"), sem("h2_stored1")]
        xre_in = [sem("xre_in0"), sem("xre_in1")]
        small, exp2_done = sem("small"), sem("exp2_done")
        w1_in, wd_in, sum_done = sem("w1_in"), sem("wd_in"), sem("sum_done")
        y_norm, z_ready, elu2_act, u2_done, x2_done = (sem("y_norm"), sem("z_ready"), sem("elu2_act"),
                                                            sem("u2_done"), sem("x2_done"))
        xn2_ready, xn2T_mm, xn2T_ready = sem("xn2_ready"), sem("xn2T_mm"), sem("xn2T_ready")
        up_mm, up_ready, lg_mm, lg_ready = sem("up_mm"), sem("up_ready"), sem("lg_mm"), sem("lg_ready")
        tok_stored = [sem("tok_stored0"), sem("tok_stored1")]
        lexp_asked, lexp_done, prob_ready, prob_stored = (sem("lexp_asked"), sem("lexp_done"), sem("prob_ready"),
                                                          sem("prob_stored"))
        order_ready, order_out, order_in, order_dec = (sem("order_ready"), sem("order_out"), sem("order_in"),
                                                       sem("order_dec"))
        st_done = sem("st_done")
        tok_in = [sem(f"tok_in{c}") for c in range(2 * BT)]
        hr_mm, hr_ready, et_mm, et_ready = ([sem(f"{n}{h}") for h in range(2)] for n in ("hr_mm", "hr_ready", "et_mm", "et_ready"))
        hr_stored = [sem("hr_stored0"), sem("hr_stored1")]
        y_biased = sem("y_biased")
        y_mm, o_ready, sto_done, out_done = sem("y_mm"), sem("o_ready"), sem("sto_done"), sem("out_done")

        def wait(eng, s, n):
            if not (isinstance(n, int) and n <= 0):
                eng.wait_ge(s, n)

        def pool_wait(s, n):
            wait(nc.gpsimd, s, n)
            if not isinstance(n, int):
                nc.gpsimd.sem_inc(pool_gate, 1)

        NP = (NT + 1) // 2

        def pair(p):
            return 1 if isinstance(p, int) and p == NT // 2 else 2

        PARTS = [0, 12, 30, NT]
        NEWTON = 3

        def by_head(ap):
            return ap.rearrange("p (h o) -> p h o", o=1).broadcast_to([P, ap.shape[1], D])

        def last1(b):
            return BT if not isinstance(b, int) or b < NB1 - 1 else NT - BT * (NB1 - 1)

        def is_in(t, n):
            return not isinstance(t, int) or 0 <= t < n

        def steps(eng, n, extra, step, first=2, last=0):
            for t in range(first):
                step(t, t % 2)
            m = (n - last) // 2
            with eng.Fori(first // 2, m) as i:
                step(2 * i, 0)
                step(2 * i + 1, 1)
            for t in range(2 * m, n + extra):
                step(t, t % 2)

        def group_steps(eng, step):
            for g in range(-5, UG):
                step(g, g % UG)
            with eng.Fori(1, NG // UG - 1) as i:
                for j in range(UG):
                    step(UG * i + j, j)
            for g in range(NG - UG, NG + 1):
                step(g, g % UG)

        def cols(t, width):
            return bass.ds(t * width, width)

        def buffers_turned(fb):
            at, read = 0, []
            for k in range(1, fb + 8):
                if k <= fb:
                    at ^= k & 1
                    continue
                read.append(at)
                at ^= 1 ^ ((k - min(fb, 7)) & 1)
                read.append(at)
                at ^= 1 ^ (min(fb, 7) & 1)
            return read, at

        E_TURNS, E_END = buffers_turned(FB)
        E_TURNS = E_TURNS + [E_END]
        T_TURNS, T_END = buffers_turned(TFB)
        biased, bias_ready = sem("biased"), sem("bias_ready")
        gb_in, lgT_ready, lgt_mm = sem("gb_in"), sem("lgT_ready"), sem("lgt_mm")
        pool_gate, s_split = sem("pool_gate"), sem("s_split")
        br2_ready, bd_in = sem("br2_ready"), sem("bd_in")
        prob2 = sb("prob2", [P, NT, 2])

        class Windows:
            def __init__(self, eng, packed, ahead):
                self.eng, self.packed, self.ahead = eng, packed, ahead

            def load(self, g, j):
                if not isinstance(g, int) and j % 4 == 0:
                    self.word = self.eng.value_load(self.packed[0:1, bass.ds(g // 4, 1)])

            def of(self, g, j):
                if isinstance(g, int):
                    return self.eng.value_load(win_i[0:1, g + self.ahead:g + self.ahead + 1], min_val=0, max_val=NT)
                return ((self.word >> (8 * (j % 4))) & 63).with_bounds(min_val=0, max_val=NT)

        chain = [0]
        block = ctx.enter_context(nc.Block())

        def turn_back(eng, t, q, h):
            wait(eng, et_mm[h], t + 1)
            wait(eng, y_mm, t - BT + 1)
            to = hT[:, h * MC // 2:(h + 1) * MC // 2, q * P:(q + 1) * P]
            of = big[:, 2 * (q % 2) + h, :].rearrange("p (c q) -> p c q", q=P)
            ins = eng.tensor_copy(to, of) if h else eng.activation(to, of, ACT.Copy)
            ins.then_inc(et_ready[h], 1)

        @block.sync
        def _(sp):
            sp.dma_start(srcdst[0:EP, 0, :], src.rearrange("(p c) -> p c", p=EP)).then_inc(edges_in, 16)
            sp.dma_start(srcdst[0:EP, 1, :], dst.rearrange("(p c) -> p c", p=EP)).then_inc(edges_in, 16)
            sp.wait_ge(zero_x, 2)
            sp.dma_start(xn[:, 0:NT - 1, :], x[0:(NT - 1) * P, :].rearrange("(t p) f -> p t f", p=P)).then_inc(x_in, 16)
            sp.dma_start(xn[0:LASTP, NT - 1, :], x[(NT - 1) * P:N, :]).then_inc(x_in, 16)
            sp.dma_start(wraw, W_heads.rearrange("h d f -> (h d) f").rearrange("(c p) f -> p c f", p=P)).then_inc(w_in, 16)
            sp.dma_start(woraw, W_out.rearrange("(m p) f -> p m f", p=P)).then_inc(w_in, 16)

            def column(to, v):
                sp.dma_start(to, v.rearrange("(c p) -> p c", p=P), allow_slow_non_contiguous=True).then_inc(w_in, 16)

            column(bcol[:, :], b_heads.rearrange("h d -> (h d)"))
            column(gcol[:, :], g_heads.rearrange("h d -> (h d)"))
            column(becol[:, :], beta_heads.rearrange("h d -> (h d)"))
            column(bocol[:, :], b_out)
            column(b1c[:, :], b1)
            for s in range(2):
                column(a2[:, :, s], a_out[s * C:(s + 1) * C])
            for h in range(H):
                lo = (h * D) % P
                for s in range(2):
                    sp.dma_start(amat[lo:lo + D, h * D // P, s * H + h:s * H + h + 1],
                                 a_heads[h, s * D:(s + 1) * D].rearrange("(d o) -> d o", o=1),
                                 allow_slow_non_contiguous=True).then_inc(w_in, 16)
            sp.dma_start(wg_sb[:, :, :], Wg.rearrange("(c p) e -> p c e", p=P)).then_inc(w_in, 16)
            sp.dma_start(bg_sb[:, :], bg.rearrange("(e o) -> e o", o=1), allow_slow_non_contiguous=True).then_inc(w_in, 16)

            def store1(t, j):
                wait(sp, biased, t + 1)
                sp.dma_start(h1_dram[cols(t, P), :], hrow[:, j, :]).then_inc(h_stored[j], 16)

            steps(sp, NT, 0, store1)

            for to, vec in ((goutb, g_out), (beoutb, beta_out)):
                sp.dma_start(to, vec.rearrange("(o n) -> o n", o=1).broadcast_to([P, C])).then_inc(gb_in, 16)

            def store2(p, j):
                wait(sp, h2_ready, p + 1)
                nq = pair(p)
                sp.dma_start(h2_dram[bass.ds(p * 2 * P, nq * P), :].rearrange("(q p) c -> p q c", p=P),
                             h2row[:, 2 * j:2 * j + nq, :]).then_inc(h2_stored[j], 16)

            steps(sp, NP, 0, store2)
            sp.wait_ge(agg[1].mm, NG)
            sp.dma_start(w1_sb, W1.rearrange("(k p) f -> p k f", p=P)).then_inc(w1_in, 16)

            def x_again(b, j):
                if isinstance(b, int) and b == NB1 - 1:
                    sp.dma_start(xre[0:LASTP, j, 0, :], x[(NT - 1) * P:N, :]).then_inc(xre_in[j], 16)
                else:
                    sp.dma_start(xre[:, j, :, :],
                                 x[bass.ds(b * BT * P, BT * P), :].rearrange("(q p) c -> p q c", p=P)).then_inc(xre_in[j], 16)

            def node_batch(b, j):
                if is_in(b + 1, NB1):
                    wait(sp, x2_done, b)
                    x_again(b + 1, 1 - j)
                if is_in(b - 1, NB1):
                    k = 1 - j
                    nq = last1(b - 1)
                    wait(sp, x2_done, b)
                    rows = tok_dram[bass.ds((b - 1) * BT * P, nq * P), :].rearrange("(q p) c -> p q c", p=P)
                    sp.dma_start(rows[:, :, 0:C], node[:, BT * k:BT * k + nq, 0:C]).then_inc(tok_stored[k], 16)
                    for h in range(2):
                        wait(sp, hr_ready[h], BT * (b - 1) + nq)
                    sp.dma_start(rows[:, :, C + 2:XR], hrows[:, BT * k:BT * k + nq, :]).then_inc(hr_stored[k], 16)

            assert NT - BT * (NB1 - 1) == 1
            x_again(0, 0)
            steps(sp, NB1, 1, node_batch, last=2)
            sp.wait_ge(hr_stored[0], 16 * (NB1 - NB1 // 2))
            sp.wait_ge(hr_stored[1], 16 * (NB1 // 2))
            for e in range(NE):
                sp.dma_start(wd_sb[:, e * MC * C:(e + 1) * MC * C].rearrange("p (c f) -> p c f", c=MC),
                             Wd[e].rearrange("(c p) f -> p c f", p=P)).then_inc(wd_in, 16)
            sp.wait_ge(lg_mm, NB1)
            sp.dma_start(bd_sb, bd.rearrange("(o e) c -> o (e c)", o=1).broadcast_to([P, NE * C])).then_inc(bd_in, 16)
            sp.wait_ge(prob_ready, 1)
            sp.dma_start(tok_dram.rearrange("(t p) r -> p t r", p=P)[:, :, C:C + 2], prob2[:, :, :]).then_inc(prob_stored, 16)
            sp.wait_ge(order_ready, 1)
            sp.dma_start(order_dram.rearrange("(p c) -> p c", p=P), tkeys[T_END][:, 0:TC]).then_inc(order_out, 16)
            sp.wait_ge(order_out, 16)
            sp.dma_start(tord[:, :].bitcast(F32), order_dram.rearrange("(c p) -> p c", p=P),
                         allow_slow_non_contiguous=True).then_inc(order_in, 16)
            sp.wait_ge(out_done, 16 * TT)

        @block.gpsimd
        def _(pool):
            pool.memset(xn[:, NT - 1, :], 0.0).then_inc(zero_x, 1)
            pool.memset(amat[:, :, :], 0.0).then_inc(zero_x, 1)
            pool.memset(ones[:, :], 1.0).then_inc(consts, 1)
            pool.memset(ident[:, :], 0.0).then_inc(pool_own, 1)
            pool.wait_ge(pool_own, 1)
            pool.affine_select(out=ident[:, :], in_=ident[:, :], compare_op=ALU.not_equal, fill=1.0, base=0,
                               pattern=[[-1, P]], channel_multiplier=1).then_inc(consts, 1)
            pool.iota(padno, pattern=[[1, PC]], base=0, channel_multiplier=PC).then_inc(consts, 1)
            pool.iota(tpadno[:, :], pattern=[[1, TPC]], base=0, channel_multiplier=TPC).then_inc(consts, 1)
            pool.iota(tokno[:, :], pattern=[[P, NT]], base=0, channel_multiplier=1).then_inc(consts, 1)
            pool.iota(sgni[:, :], pattern=[[0, 1]], base=0, channel_multiplier=1).then_inc(consts, 1)
            pool.iota(iotai[:, :], pattern=[[1, P]], base=0, channel_multiplier=0).then_inc(consts, 1)
            pool.memset(s_tab[:, NT * H:(NT + 1) * H], 0.0).then_inc(consts, 1)
            pool.memset(s_tab2[:, NT:NT + 1], 0.0).then_inc(consts, 1)
            pool.memset(hrow[:, :, :], 0.0).then_inc(consts, 1)
            def add_bias(t, j):
                pool_wait(h_ready, t + 1)
                if isinstance(t, int):
                    pool_wait(h_stored[j], 16 * (t // 2))
                else:
                    pool_wait(h_stored[j], 8 * (t - j))
                pool.tensor_tensor(hrow[:, j, 0:HR], hraw[:, j, :], bias1[:, 0:HR], ALU.add).then_inc(biased, 1)

            pool.wait_ge(bias_ready, 1)
            steps(pool, NT, 0, add_bias)

            def gathers(a, table, rows, width, used):
                def turn(i):
                    for half in range(2):
                        lo = half * (US // 2)
                        first = UG * i + half * (UG // 2)
                        pool_wait(used, first - UG // 2)
                        pool.tensor_copy(staged[:, half, :], dst_idx[:, bass.ds(US * i + lo, US // 2)]).then_inc(a.staged, 1)
                        pool_wait(a.staged, 2 * i + half + 1)
                        for c in range(lo, lo + US // 2):
                            pool.indirect_dma_start(rows[:, c, 0:width], None, table[:, :],
                                                    bass.IndirectOffsetOnAxis(ap=staged[:, half, c - lo:c - lo + 1].bitcast(U32),
                                                                              axis=0)).then_inc(a.got[c], 16)
                turn(0)
                with pool.Fori(1, NG // UG) as i:
                    turn(i)

            pool.wait_ge(sorted_, 1)
            pool.wait_ge(h_stored[0], 16 * ((NT + 1) // 2))
            pool.wait_ge(h_stored[1], 16 * (NT // 2))
            gathers(agg[0], h1_dram, got1, HR, agg[0].mm)

            def centre(p, j):
                tiles = arena[:, bass.ds(p * 2 * HD, pair(p) * HD)].rearrange("p (h d) -> p h d", d=D)
                pool.tensor_tensor(tiles, tiles, by_head(mean1[:, bass.ds(p * 2 * H, pair(p) * H)]), ALU.subtract).then_inc(centred, 1)

            for part in range(len(PARTS) - 1):
                pool.wait_ge(means, part + 1)
                for p in range(PARTS[part] // 2, (PARTS[part + 1] + 1) // 2):
                    centre(p, p % 2)
            pool.wait_ge(x1_scaled, -(-(NT + 1) * C // (2 * HD)))
            pool.memset(arena[:, 0:(NT + 1) * C], 0.0).then_inc(zeroed, 1)
            pool.wait_ge(h2_stored[0], 16 * ((NP + 1) // 2))
            pool.wait_ge(h2_stored[1], 16 * (NP // 2))
            gathers(agg[1], h2_dram, got2, HR2, agg[1].mm)

            pool.wait_ge(order_dec, 1)
            pool.wait_ge(prob_stored, 16)
            pool.wait_ge(tok_stored[0], 16 * (NB1 - NB1 // 2))
            pool.wait_ge(tok_stored[1], 16 * (NB1 // 2))
            pool.wait_ge(hr_stored[0], 16 * (NB1 - NB1 // 2))
            pool.wait_ge(hr_stored[1], 16 * (NB1 // 2))

            def tokens(b, j):
                if is_in(b, NB2):
                    pool_wait(o_ready, BT * (b - 1))
                    pool.tensor_copy(st_from[:, j, :], tok_from[:, bass.ds(BT * b, BT)]).then_inc(st_done, 1)
                    pool_wait(st_done, b + 1)
                    for q in range(BT):
                        c = BT * j + q
                        pool.indirect_dma_start(tok[:, c, :], None, tok_dram[:, :],
                                                bass.IndirectOffsetOnAxis(ap=st_from[:, j, q:q + 1].bitcast(U32), axis=0)
                                                ).then_inc(tok_in[c], 16)
                if is_in(b - 1, NB2):
                    k = 1 - j
                    pool_wait(out_done, 16 * BT * (b - 1))
                    pool.tensor_copy(st_to[:, k, :], tok_to[:, bass.ds(BT * (b - 1), BT)]).then_inc(sto_done, 1)
                    pool_wait(sto_done, b)
                    for q in range(BT):
                        pool_wait(o_ready, BT * (b - 1) + q + 1)
                        pool_wait(out_done, 16 * (BT * (b - 1) + q))
                        pool.indirect_dma_start(out[:, :], bass.IndirectOffsetOnAxis(ap=st_to[:, k, q:q + 1].bitcast(U32), axis=0),
                                                orow[:, BT * k + q, :], None, bounds_check=N - 1, oob_is_err=False
                                                ).then_inc(out_done, 16)

            steps(pool, NB2, 1, tokens)

        @block.vector
        def _(v):
            def done(ins):
                chain[0] += 1
                return ins.then_inc(dve, 1)

            def settle():
                v.wait_ge(dve, chain[0])

            asked = [0]

            def inverse_root(var_, y, t_):
                settle()
                asked[0] += 1
                done(v.tensor_copy(t_, var_))
                settle()
                v.sem_inc(sqrt_asked, 1)
                v.wait_ge(sqrt_done, asked[0])
                done(v.reciprocal(y, y))
                settle()
                done(v.tensor_tensor(t_, y, y, ALU.mult))
                settle()
                done(v.tensor_tensor(t_, t_, var_, ALU.mult))
                settle()
                done(v.tensor_scalar(t_, t_, -0.5, 1.5, ALU.mult, ALU.add))
                settle()
                done(v.tensor_tensor(y, y, t_, ALU.mult))
                settle()

            def finish_stats():
                settle()
                done(v.tensor_tensor(mean[:, :], stats[:, :, 1], stats[:, :, 4], ALU.add))
                done(v.tensor_tensor(tmp[:, :], stats[:, :, 1], stats[:, :, 4], ALU.subtract))
                done(v.tensor_tensor(var[:, :], stats[:, :, 2], stats[:, :, 5], ALU.add))
                settle()
                done(v.tensor_scalar(mean[:, :], mean[:, :], 0.5, None, ALU.mult))
                done(v.tensor_tensor(tmp[:, :], tmp[:, :], tmp[:, :], ALU.mult))
                done(v.tensor_scalar(var[:, :], var[:, :], 1.0 / C, LN_EPS, ALU.mult, ALU.add))
                settle()
                done(v.scalar_tensor_tensor(var[:, :], tmp[:, :], 0.25, var[:, :], ALU.mult, ALU.add))
                inverse_root(var[:, :], rstd[:, :], tmp[:, :])

            v.wait_ge(edges_in, 32)
            v.wait_ge(consts, 10)
            done(v.memset(zeros[:, :], 0.0))
            done(v.memset(keys[0][:, :].bitcast(I32), SURPLUS))
            done(v.tensor_copy(iota[:, :], iotai[:, :]))
            done(v.tensor_copy(eiota[:, :], iotai[:, 0:NE]))
            done(v.tensor_scalar(src_win[0:EP, :].bitcast(I32), srcdst[0:EP, 0, :], 7, None, ALU.logical_shift_right))
            settle()
            done(v.tensor_copy(src_winb[0:EP, :], src_win[0:EP, :].bitcast(I32)))
            ki = keys[0][0:EP, 0:EC].bitcast(I32)
            done(v.tensor_scalar(ki, srcdst[0:EP, 0, :], DST_BITS, ONE_TAG, ALU.logical_shift_left, ALU.bitwise_or))
            settle()
            done(v.tensor_tensor(ki, ki, srcdst[0:EP, 1, :], ALU.bitwise_or))
            for w in range(NT):
                settle()
                done(v.tensor_scalar(keys[1][0:EP, 0:EC // 2].bitcast(BF16), src_winb[0:EP, :], w + 0.5, 0.0, ALU.is_lt, ALU.add,
                                     accum_out=cnt[0:EP, w:w + 1]))
            settle()
            v.sem_inc(cnt_ready, 1)

            v.wait_ge(x_in, 32)
            for t in range(NT):
                done(v.bn_stats(stats[:, t, :], xn[:, t, :]))
            finish_stats()
            for t in range(NT):
                v.tensor_scalar(xn[:, t, :], xn[:, t, :], mean[:, t:t + 1], rstd[:, t:t + 1],
                                ALU.subtract, ALU.mult).then_inc(xn_ready, 1)
            v.wait_ge(wt_mm, 2 * KH + 2)
            v.tensor_tensor(brow2[:, :], brow2[:, :], big[0:1, 3, 0:C + 2], ALU.subtract).then_inc(br2_ready, 1)

            counted = [0]

            def pad_keys(nw, unit, pno, pnof, pwin, pwini, to, tag, step_, offset):
                done(v.memset(tot[:, 0:1], 0.0))
                counted[0] += 1
                v.wait_ge(cnt_mm, counted[0])
                done(v.tensor_copy(tot[:, 1:nw + 1], keyps[:, 0, 0:nw]))
                settle()
                done(v.tensor_tensor(padf[:, 0:nw], tot[:, 1:nw + 1], tot[:, 0:nw], ALU.subtract))
                settle()
                done(v.tensor_scalar(toti[:, 0:nw], padf[:, 0:nw], float(unit - 1), None, ALU.add))
                settle()
                sh = unit.bit_length() - 1
                done(v.tensor_scalar(toti[:, 0:nw], toti[:, 0:nw], sh, sh, ALU.logical_shift_right, ALU.logical_shift_left))
                settle()
                done(v.tensor_tensor(padf[:, 0:nw], toti[:, 0:nw], padf[:, 0:nw], ALU.subtract))
                done(v.tensor_copy(pnof, pno))
                done(v.memset(pwin, 0.0))
                settle()
                done(v.tensor_tensor_scan(padcum[:, 0:nw], padf[:, 0:nw], zeros[:, 0:nw], 0.0, ALU.add, ALU.add))
                for w in range(nw):
                    settle()
                    done(v.scalar_tensor_tensor(pwin, pnof, padcum[:, w:w + 1], pwin, ALU.is_ge, ALU.add))
                settle()
                done(v.tensor_scalar(pwini, pwin, float(step_), float(offset), ALU.mult, ALU.add))
                settle()
                done(v.tensor_scalar(to.bitcast(I32), pwini, DST_BITS, PAD_DST | tag,
                                     ALU.logical_shift_left, ALU.bitwise_or))
                settle()

            pad_keys(NT, GT * P, padno, padnof, padwin, padwini, keys[0][:, EC:SC], ONE_TAG, P, P - 1)
            done(v.tensor_scalar(sgni[:, :], sgni[:, :], 1, None, ALU.bitwise_and))
            settle()
            done(v.tensor_scalar(sgn[:, :], sgni[:, :], -2.0, 1.0, ALU.mult, ALU.add))
            settle()

            turns = [0]

            def ask_turn():
                v.sem_inc(turn_asked, 1)
                turns[0] += 1
                v.wait_ge(turned, turns[0])

            def bitonic(bufs, cur, fb):
                width = 1 << fb
                low = min(fb, 7)
                twidth = P << max(fb - 7, 0)
                parts, tparts = P, 1 << low

                def exchange(cur, bit, np_, w):
                    a = bufs[cur][0:np_, 0:w].rearrange("p (b s q) -> p b s q", s=2, q=1 << bit)
                    b = bufs[1 - cur][0:np_, 0:w].rearrange("p (b s q) -> p b s q", s=2, q=1 << bit)
                    done(v.tensor_tensor(b[:, :, 0, :], a[:, :, 0, :], a[:, :, 1, :], ALU.min))
                    done(v.tensor_tensor(b[:, :, 1, :], a[:, :, 0, :], a[:, :, 1, :], ALU.max))
                    settle()
                    return 1 - cur

                def flip(cur, np_, w, q, lo, hi):
                    part = bufs[cur][0:np_, 0:w].rearrange("p (b q) -> p b q", q=q)[:, :, lo:hi]
                    done(v.tensor_scalar(part, part, -1.0, None, ALU.mult))
                    settle()

                def turn(cur, np_, w):
                    ask_turn()
                    for h in range(-(-w // 512)):
                        n = min(512, w)
                        done(v.tensor_copy(bufs[1 - cur][0:np_, h * 512:h * 512 + n], keyps[0:np_, h, 0:n]))
                    settle()
                    return 1 - cur

                flip(cur, parts, width, 4, 2, 4)
                for k in range(1, fb + 8):
                    if 2 <= k < fb:
                        flip(cur, parts, width, 4 << (k - 1), 1 << (k - 1), 3 << (k - 1))
                    if k == fb:
                        h = width // 2
                        done(v.tensor_scalar(bufs[cur][:, 0:h], bufs[cur][:, 0:h], sgn[:, :], None, ALU.mult))
                        done(v.tensor_scalar(bufs[cur][:, h:width], bufs[cur][:, h:width], sgn[:, :], -1.0,
                                             ALU.mult, ALU.mult))
                        settle()
                    if k <= fb:
                        for d in range(k - 1, -1, -1):
                            cur = exchange(cur, d, parts, width)
                        continue
                    cur = turn(cur, tparts, twidth)
                    b = k - 1 - fb
                    if k < fb + 7:
                        flip(cur, tparts, twidth, 4 << b, 1 << b, 3 << b)
                    else:
                        flip(cur, tparts, twidth, P, P // 2, P)
                    for d in range(k - 1, fb - 1, -1):
                        cur = exchange(cur, d - fb, tparts, twidth)
                    for d in range(fb - 1, 6, -1):
                        cur = exchange(cur, d, tparts, twidth)
                    cur = turn(cur, parts, width)
                    for d in range(low - 1, -1, -1):
                        cur = exchange(cur, d, parts, width)
                return cur

            cur = bitonic(keys, 0, FB)
            assert cur == E_END
            ask_turn()
            final = keys[1 - cur]
            fo = final[:, :].rearrange("p (r b) -> p b r", b=8)
            for h in range(2):
                done(v.tensor_copy(fo[:, 4 * h:4 * h + 4, :], keyps[:, h, :].rearrange("p (b r) -> p b r", b=4)))
            settle()
            fi = final[:, 0:NTL].bitcast(I32)
            lo_i = keys[cur][:, 0:NTL].bitcast(I32)
            done(v.tensor_scalar(dst_idx[:, :], fi, PAD_DST, None, ALU.bitwise_and))
            done(v.tensor_scalar(lo_i, fi, DST_BITS, P - 1, ALU.logical_shift_right, ALU.bitwise_and))
            done(v.tensor_scalar(win_i[:, :], fi.rearrange("p (g t) -> p g t", t=GT)[:, :, 0], DST_BITS + 7, 63,
                                 ALU.logical_shift_right, ALU.bitwise_and))
            settle()
            done(v.tensor_scalar(src_lo[:, :], dst_idx[:, :], float(N) - 0.5, float(P), ALU.is_gt, ALU.mult))
            settle()
            done(v.tensor_tensor(src_lo[:, :], src_lo[:, :], lo_i, ALU.add))
            done(v.tensor_scalar(dst_idx[:, :], dst_idx[:, :], float(NT * P - 1), None, ALU.min))
            for ahead, to in ((3, win_pe), (-1, win_dve)):
                n = NG // 4 - 2
                for k in range(4):
                    of = win_i[:, 4 + ahead + k:4 + ahead + k + 4 * (n - 1) + 1:4]
                    settle()
                    if k == 0:
                        done(v.tensor_copy(to[:, 1:n + 1], of))
                    else:
                        byte = keys[cur][:, 0:n].bitcast(I32)
                        done(v.tensor_scalar(byte, of, 8 * k, None, ALU.logical_shift_left))
                        settle()
                        done(v.tensor_tensor(to[:, 1:n + 1], to[:, 1:n + 1], byte, ALU.bitwise_or))
            settle()
            v.sem_inc(sorted_, 1)

            v.wait_ge(h_mm, NT)
            v.wait_ge(wt_mm, 2 * KH + 2)
            done(v.memset(arena[:, 0:(NT + 1) * HD], 0.0))
            settle()

            def split_scores(tab, nh):
                n = (NT + 1) * nh
                parts = s_parts[:, 0:3 * n].rearrange("p (t a h) -> p t a h", a=3, h=nh)
                rest = [tab] + [s_rest[:, k, 0:n] for k in range(2)]
                for k in range(3):
                    to = parts[:, :, k, :]
                    of = rest[k].rearrange("p (t h) -> p t h", h=nh)
                    done(v.tensor_copy(to, of))
                    settle()
                    if k < 2:
                        done(v.tensor_tensor(rest[k + 1].rearrange("p (t h) -> p t h", h=nh), of, to, ALU.subtract))
                        settle()
                v.sem_inc(s_split, 1)

            v.wait_ge(s_ready, NT)
            tab = s_tab[:, 0:NT * H].rearrange("p (t h) -> p t h", h=H)
            done(v.tensor_tensor(tab, tab, bias_s[:, :].rearrange("p (o h) -> p o h", o=1).broadcast_to([P, NT, H]), ALU.add))
            settle()
            split_scores(s_tab[:, :], H)

            def aggregate(a, layer):
                nh, width, got, s_at = (H, HD, got1, HD) if layer == 0 else (1, C, got2, C + 1)

                windows = Windows(v, win_dve, -1)

                def step(g, j):
                    windows.load(g, j)
                    k = (j + 5) % UG
                    if is_in(g + 5, NG):
                        wait(v, a.mm, g - 2)
                        lo = src_lo[:, bass.ds(GT * (g + 5), GT)]
                        v.tensor_tensor(hot[:, k, :, :], iota[:, :].rearrange("p (o n) -> p o n", o=1).broadcast_to([P, GT, P]),
                                        lo.rearrange("p (u o) -> p u o", o=1).broadcast_to([P, GT, P]),
                                        ALU.is_equal).then_inc(a.hot, 1)
                    k = (j + 2) % UG
                    if is_in(g + 2, NG):
                        wait(v, a.src_mm, g + 3)
                        turn = (g + 2) // UG if isinstance(g, int) else None
                        for u in range(GT):
                            if turn is not None:
                                v.wait_ge(a.got[GT * k + u], 16 * (turn + 1))
                            else:
                                v.wait_ge(a.got[GT * k + u], GT * (g + 2 - k) + 16)
                        v.tensor_tensor(score[:, k % 4, :, 0:nh], big[:, 2 + k % 2, 0:GT * nh].rearrange("p (u h) -> p u h", u=GT),
                                        got[:, GT * k:GT * k + GT, s_at:s_at + nh], ALU.add).then_inc(a.score, 1)
                        wait(v, a.score, g + 3)
                        v.scalar_tensor_tensor(lrel[:, k % 4, :, 0:nh], score[:, k % 4, :, 0:nh], LEAK, score[:, k % 4, :, 0:nh],
                                               ALU.mult, ALU.max).then_inc(a.lrel, 1)
                    k = (j + 1) % UG
                    if is_in(g + 1, NG):
                        wait(v, a.exp, g + 2)
                        wait(v, a.mm, g)
                        if layer == 0:
                            v.tensor_tensor(
                                scaled1[:, k % 2, :, 0:HV * D].rearrange("p u (h d) -> p u h d", h=HV),
                                got[:, GT * k:GT * k + GT, 0:HV * D].rearrange("p u (h d) -> p u h d", h=HV),
                                ew[:, k % 4, :, 0:HV].rearrange("p u (h o) -> p u h o", o=1).broadcast_to([P, GT, HV, D]),
                                ALU.mult).then_inc(a.scaled, 1)
                        else:
                            v.tensor_tensor(scaled2[:, k % 2, :, :], hot[:, k, :, :],
                                            ew[:, k % 4, :, 0:1].broadcast_to([P, GT, P]), ALU.mult).then_inc(a.scaled, 1)
                    if is_in(g - 1, NG):
                        w = windows.of(g, j)
                        wait(v, a.mm, g)
                        wait(v, a.added, g - 1)
                        to = arena[:, bass.ds(w * width, width)]
                        v.tensor_tensor(to, to, big[:, (j + 1) % 2, 0:width], ALU.add).then_inc(a.added, 1)

                group_steps(v, step)
                v.wait_ge(a.added, NG)

            aggregate(agg[0], 0)

            def newton_root(var_, y, w, op, settled):
                op(v.tensor_scalar(w.bitcast(I32), var_.bitcast(I32), 1, None, ALU.logical_shift_right))
                settled()
                op(v.tensor_scalar(y.bitcast(I32), w.bitcast(I32), -1.0, float(ROOT_SEED), ALU.mult, ALU.add))
                settled()
                for _ in range(NEWTON):
                    op(v.tensor_tensor(w, y, y, ALU.mult))
                    settled()
                    op(v.tensor_tensor(w, w, var_, ALU.mult))
                    settled()
                    op(v.tensor_scalar(w, w, -0.5, 1.5, ALU.mult, ALU.add))
                    settled()
                    op(v.tensor_tensor(y, y, w, ALU.mult))
                    settled()

            def head_stats(t):
                for h in range(H):
                    ins = v.bn_stats(hstats[:, (t * H + h) * 6:(t * H + h + 1) * 6], arena[:, t * HD + h * D:t * HD + (h + 1) * D])
                done(ins)

            def finish_heads(lo, hi):
                n = slice(lo * H, hi * H)
                hs = hstats.rearrange("p (n s) -> p n s", s=6)[:, n, :]
                settle()
                done(v.tensor_tensor(mean1[:, n], hs[:, :, 1], hs[:, :, 4], ALU.add))
                done(v.tensor_tensor(tmp1[:, n], hs[:, :, 1], hs[:, :, 4], ALU.subtract))
                done(v.tensor_tensor(var1[:, n], hs[:, :, 2], hs[:, :, 5], ALU.add))
                settle()
                done(v.tensor_scalar(mean1[:, n], mean1[:, n], 0.5, None, ALU.mult))
                done(v.scalar_tensor_tensor(tmp1[:, n], tmp1[:, n], 0.25, tmp1[:, n], ALU.mult, ALU.mult))
                done(v.tensor_scalar(var1[:, n], var1[:, n], 1.0 / D, LN_EPS, ALU.mult, ALU.add))
                settle()
                v.sem_inc(means, 1)
                done(v.tensor_tensor(var1[:, n], var1[:, n], tmp1[:, n], ALU.add))
                settle()
                newton_root(var1[:, n], rstd1[:, n], tmp1[:, n], done, settle)

            def x1_pair(p, j):
                if is_in(p, NP):
                    nq = pair(p)
                    wait(v, centred, p + 1)
                    wait(v, x1t_mm, p - 1)
                    v.tensor_tensor(x1s[:, j, 0:nq * HD].rearrange("p (h d) -> p h d", d=D),
                                    arena[:, bass.ds(p * 2 * HD, nq * HD)].rearrange("p (h d) -> p h d", d=D),
                                    by_head(rstd1[:, bass.ds(p * 2 * H, nq * H)]), ALU.mult).then_inc(x1_scaled, 1)
                if isinstance(p, int) and p == 0:
                    v.wait_ge(bias2_mm, 1)
                    v.tensor_copy(bias2, keyps[:, 0, 0:C + 2]).then_inc(bias2_ready, 1)
                    v.wait_ge(bias2_ready, 1)
                if is_in(p - 1, NP):
                    nq = pair(p - 1)
                    wait(v, elu_act, p)
                    wait(v, h2_mm, p - 2)
                    v.scalar_tensor_tensor(u1[:, 1 - j, 0:nq * HD], ex1[:, 1 - j, 0:nq * HD], 1.0, re1[:, 1 - j, 0:nq * HD],
                                           ALU.min, ALU.add).then_inc(elu_u, 1)
                if is_in(p - 2, NP):
                    nq = pair(p - 2)
                    bank = (big, keyps)[j]
                    wait(v, h2_mm, p - 1)
                    v.tensor_tensor(s_tab2[:, bass.ds((p - 2) * 2, nq)], bank[:, 0:nq, C],
                                    bias2[:, C:C + 1].broadcast_to([P, nq]), ALU.add).then_inc(s2_ready, 1)
                    if isinstance(p, int):
                        wait(v, h2_stored[j], 16 * ((p - 2) // 2))
                    else:
                        v.wait_ge(h2_stored[j], 8 * (p - 2 - j))
                    v.tensor_tensor(h2row[:, 2 * j:2 * j + nq, 0:C + 2], bank[:, 0:nq, 0:C + 2],
                                    bias2.rearrange("p (o f) -> p o f", o=1).broadcast_to([P, nq, C + 2]), ALU.add).then_inc(h2_ready, 1)

            for t in range(PARTS[1]):
                head_stats(t)
            finish_heads(0, PARTS[1])
            for part in range(len(PARTS) - 1):
                lo, hi = PARTS[part:part + 2]
                end = PARTS[part + 2] if part + 2 < len(PARTS) else hi
                pairs = range(lo // 2, (hi + 1) // 2)
                at = hi
                for n, p in enumerate(pairs):
                    x1_pair(p, p % 2)
                    upto = min(end, hi + (end - hi) * (n + 1) // (len(pairs) - 1))
                    for t in range(at, upto):
                        head_stats(t)
                    at = upto
                    if n == len(pairs) - 2 and end > hi:
                        finish_heads(hi, end)
            for p in (NP, NP + 1):
                x1_pair(p, p % 2)

            v.wait_ge(zeroed, 1)
            v.wait_ge(s2_ready, NP)
            split_scores(s_tab2[:, :], 1)
            aggregate(agg[1], 1)

            for t in range(NT):
                ins = v.bn_stats(stats[:, t, :], arena[:, t * C:(t + 1) * C])
            ins.then_inc(sum_done, 1)
            v.wait_ge(sum_done, 1)
            finish_stats()
            v.wait_ge(gb_in, 32)
            done(v.memset(wg_cg, 0.0))
            done(v.memset(bg_cg[:, :], 0.0))
            settle()
            done(v.tensor_copy(wg_cg[:, :, 0:NE], wg_sb[:, :, :]))
            done(v.tensor_copy(bg_cg[0:NE, :], bg_sb[:, :]))
            settle()

            OPS = 10 + 4 * NEWTON

            def z_tiles(b, j):
                nq = last1(b)
                x2 = node[:, BT * j:BT * j + nq, 0:C]
                if isinstance(b, int):
                    wait(v, tok_stored[j], 16 * (b // 2))
                else:
                    v.wait_ge(tok_stored[j], 8 * (b - j))
                wait(v, xn2T_mm, BT * (b - 1))
                for q in range(nq):
                    t = BT * b + q
                    v.scalar_tensor_tensor(x2[:, q, :], arena[:, cols(t, C)], mean[:, cols(t, 1)], goutb,
                                           ALU.subtract, ALU.mult).then_inc(y_norm, 1)
                for q in range(nq):
                    t = BT * b + q
                    wait(v, y_norm, t + 1)
                    ins = v.scalar_tensor_tensor(x2[:, q, :], x2[:, q, :], rstd[:, cols(t, 1)], beoutb,
                                                 ALU.mult, ALU.add)
                ins.then_inc(z_ready, 1)

            def batch(b, j):
                if is_in(b, NB1):
                    nq = last1(b)
                    x2 = node[:, BT * j:BT * j + nq, 0:C]
                    wait(v, elu2_act, b + 1)
                    v.scalar_tensor_tensor(x2, expz[:, 0:nq, :], 1.0, x2, ALU.min, ALU.add).then_inc(u2_done, 1)
                    wait(v, u2_done, b + 1)
                    if isinstance(b, int):
                        v.wait_ge(xre_in[j], 16 * (b // 2 + 1))
                    else:
                        v.wait_ge(xre_in[j], 8 * (b - j) + 16)
                    v.scalar_tensor_tensor(x2, x2, -1.0, xre[:, j, 0:nq, :], ALU.add, ALU.add).then_inc(x2_done, 1)
                    wait(v, x2_done, b + 1)
                    n = [0]

                    def small_op(ins):
                        n[0] += 1
                        ins.then_inc(small, 1)

                    def small_settle():
                        wait(v, small, OPS * b + n[0])

                    for q in range(nq):
                        ins = v.bn_stats(bst[:, q, :], x2[:, q, :])
                    small_op(ins)
                    small_settle()
                    m, vr, y, w = (bsm[:, k, 0:nq] for k in range(4))
                    small_op(v.tensor_tensor(m, bst[:, 0:nq, 1], bst[:, 0:nq, 4], ALU.add))
                    small_op(v.tensor_tensor(w, bst[:, 0:nq, 1], bst[:, 0:nq, 4], ALU.subtract))
                    small_op(v.tensor_tensor(vr, bst[:, 0:nq, 2], bst[:, 0:nq, 5], ALU.add))
                    small_settle()
                    small_op(v.tensor_scalar(m, m, 0.5, None, ALU.mult))
                    small_op(v.scalar_tensor_tensor(w, w, 0.25, w, ALU.mult, ALU.mult))
                    small_op(v.tensor_scalar(vr, vr, 1.0 / C, LN_EPS, ALU.mult, ALU.add))
                    small_settle()
                    small_op(v.tensor_tensor(vr, vr, w, ALU.add))
                    small_settle()
                    newton_root(vr, y, w, small_op, small_settle)
                    assert n[0] == OPS
                    for q in range(nq):
                        v.tensor_scalar(xn2[:, BT * j + q, :], x2[:, q, :], bsm[:, 0, q:q + 1], bsm[:, 2, q:q + 1],
                                        ALU.subtract, ALU.mult).then_inc(xn2_ready, 1)
                if is_in(b + 1, NB1):
                    z_tiles(b + 1, 1 - j)
                if is_in(b - 1, NB1):
                    nq = last1(b - 1)
                    wait(v, lg_mm, b)
                    wait(v, lgt_mm, b - 1)
                    v.tensor_scalar(lgT[:, 0:nq * P], keyps[:, 0, 0:nq * P], bg_cg[:, 0:1], None, ALU.add).then_inc(lgT_ready, 1)
                    if isinstance(b, int):
                        wait(v, hr_stored[1 - j], 16 * ((b - 1) // 2))
                    else:
                        v.wait_ge(hr_stored[1 - j], 8 * (b - 1 - (1 - j)))
                    for q in range(nq):
                        wait(v, hr_mm[1], BT * (b - 1) + q + 1)
                        v.tensor_copy(hrows[:, BT * (1 - j) + q, HB:HID], big[:, 2 * (q % 2) + 1, :]).then_inc(hr_ready[1], 1)
                    flat = lg.rearrange("p t e -> p (t e)")[:, bass.ds((b - 1) * BT * NE, nq * NE)]
                    wait(v, lgt_mm, b)
                    v.tensor_reduce(flat.rearrange("p (q e) -> p q e", q=nq),
                                    keyps[:, 1, 0:nq * P].rearrange("p (q g e) -> p q e g", q=nq, e=CG)[:, :, 0:NE, :],
                                    AX.X, ALU.add).then_inc(lg_ready, 1)

            z_tiles(0, 0)
            steps(v, NB1, 1, batch, first=4, last=2)
            v.wait_ge(lg_ready, NB1)

            def each(ap):
                return ap.rearrange("p (t o) -> p t o", o=1).broadcast_to([P, NT, NE])

            done(v.tensor_reduce(lgmax[:, :], lg, AX.X, ALU.max))
            settle()
            done(v.tensor_tensor(lg, lg, each(lgmax[:, :]), ALU.subtract))
            settle()
            v.sem_inc(lexp_asked, 1)
            v.wait_ge(lexp_done, 1)
            done(v.tensor_reduce(prob[:, :], lgx, AX.X, ALU.add))
            settle()
            done(v.reciprocal(prob[:, :], prob[:, :]))
            settle()
            done(v.tensor_copy(prob2[:, :, :], prob[:, :].rearrange("p (t o) -> p t o", o=1).broadcast_to([P, NT, 2])))
            settle()
            v.sem_inc(prob_ready, 1)
            done(v.tensor_scalar(lgx, lg, 0.0, float(NE), ALU.is_lt, ALU.mult))
            settle()
            done(v.tensor_tensor(lgx, lgx, eiota[:, :].rearrange("p (o e) -> p o e", o=1).broadcast_to([P, NT, NE]), ALU.add))
            done(v.memset(pick[:, :], float(2 * NE)))
            settle()
            done(v.tensor_reduce(pick[:, 0:NT - 1], lgx[:, 0:NT - 1, :], AX.X, ALU.min))
            done(v.tensor_reduce(pick[0:LASTP, NT - 1:NT], lgx[0:LASTP, NT - 1:NT, :], AX.X, ALU.min))
            settle()
            for e in range(NE):
                done(v.tensor_scalar(tmp[:, :], pick[:, :], float(e), 0.0, ALU.is_le, ALU.add, accum_out=cnt_e[:, e:e + 1]))
                settle()
            v.sem_inc(cnt_ready, 1)
            done(v.memset(tkeys[0][:, 0:TC].bitcast(I32), T_SURPLUS))
            done(v.tensor_copy(picki[:, :], pick[:, :]))
            settle()
            done(v.tensor_scalar(picki[:, :], picki[:, :], DST_BITS, ONE_TAG, ALU.logical_shift_left, ALU.bitwise_or))
            settle()
            done(v.tensor_tensor(tkeys[0][:, 0:NT - 1].bitcast(I32), picki[:, 0:NT - 1], tokno[:, 0:NT - 1], ALU.bitwise_or))
            done(v.tensor_tensor(tkeys[0][0:LASTP, NT - 1:NT].bitcast(I32), picki[0:LASTP, NT - 1:NT],
                                 tokno[0:LASTP, NT - 1:NT], ALU.bitwise_or))
            settle()
            pad_keys(NE, P, tpadno[:, :], tpadnof[:, :], tpadwin[:, :], tpadwini[:, :], tkeys[0][:, NT:TC], ONE_TAG, 1, 0)
            cur = bitonic(tkeys, 0, TFB)
            assert cur == T_END
            v.sem_inc(order_ready, 1)
            v.wait_ge(order_in, 16)
            done(v.tensor_scalar(tok_to[:, :], tord[:, :], PAD_DST, None, ALU.bitwise_and))
            done(v.tensor_scalar(exp_i[:, :], tord[:, :], DST_BITS, 15, ALU.logical_shift_right, ALU.bitwise_and))
            settle()
            done(v.tensor_scalar(tok_from[:, :], tok_to[:, :], float(NT * P - 1), None, ALU.min))
            done(v.tensor_scalar(exp_c[:, :], exp_i[:, :], float(NE - 1), float(MC * C), ALU.min, ALU.mult))
            done(v.tensor_scalar(exp_b[:, :], exp_i[:, :], float(NE - 1), float(C), ALU.min, ALU.mult))
            settle()
            v.sem_inc(order_dec, 1)

            def output(t, c, q):
                eb = v.value_load(exp_b[0:1, cols(t, 1)], min_val=0, max_val=(NE - 1) * C)
                wait(v, y_mm, t + 1)
                wait(v, out_done, 16 * (t - 2 * BT + 1))
                v.tensor_tensor(orow[:, c, :], keyps[:, q % 2, 0:C], bd_sb[:, bass.ds(eb, C)], ALU.add).then_inc(y_biased, 1)
                wait(v, y_biased, t + 1)
                v.scalar_tensor_tensor(orow[:, c, :], orow[:, c, :], tok[:, c, C:C + 1], tok[:, c, 0:C],
                                       ALU.mult, ALU.add).then_inc(o_ready, 1)

            def expert_rows(b, j):
                for q in range(BT):
                    t = BT * b + q
                    turn_back(v, t, q, 1)
                    if is_in(t - 1, TT):
                        output(t - 1, (BT * j + q - 1) % (2 * BT), (q - 1) % BT)

            v.wait_ge(bd_in, 16)
            steps(v, NB2, 0, expert_rows)
            output(TT - 1, 2 * BT - 1, BT - 1)

        @block.scalar
        def _(act):
            act.dma_start(brow[:, 0:HD], b_heads.rearrange("h d -> (h d)").rearrange("(o n) -> o n", o=1)).then_inc(bh_in, 16)
            act.dma_start(brow2[:, 0:C], b_out.rearrange("(o n) -> o n", o=1)).then_inc(bh_in, 16)
            asked = [0]

            def root(y, v_):
                asked[0] += 1
                act.wait_ge(sqrt_asked, asked[0])
                act.activation(y, v_, ACT.Sqrt).then_inc(sqrt_done, 1)

            root(rstd[:, :], var[:, :])
            for c in range(KH):
                act.wait_ge(wt_mm, c + 1)
                act.activation(wT[:, :, c * P:(c + 1) * P], tps[:, c % 2, 0:KF * P].rearrange("p (k q) -> p k q", k=KF),
                               ACT.Copy).then_inc(wt_ready, 1)
            for c in range(KH):
                act.wait_ge(wt_mm, KH + c + 1)
                act.activation(woT[:, c, 0:C], tps[:, c % 2, 0:C], ACT.Copy).then_inc(wt_ready, 1)
            act.wait_ge(wt_mm, 2 * KH + 1)
            act.activation(wT[:, :, HD:HD + 2 * H], big[:, 1, 0:KF * 2 * H].rearrange("p (k q) -> p k q", k=KF),
                           ACT.Copy).then_inc(wt_ready, 1)
            act.activation(brow[:, HD:HD + 2 * H], big[0:1, 2, 0:2 * H], ACT.Copy).then_inc(wt_ready, 1)
            act.activation(woT[:, :, C:C + 2], big[:, 0, 0:KH * 2].rearrange("p (k q) -> p k q", k=KH),
                           ACT.Copy).then_inc(wt_ready, 1)
            act.activation(brow2[:, C:C + 2], big[0:1, 3, 0:2], ACT.Copy).then_inc(wt_ready, 1)

            act.wait_ge(wt_mm, 2 * KH + 3)
            act.activation(bias1[:, 0:HD], big[:, 0, 0:HD], ACT.Copy)
            act.activation(bias1[:, HD:HR], big[:, 1, H:2 * H], ACT.Copy).then_inc(bias_ready, 1)
            act.activation(bias_s[:, :], big[:, 1, 0:H], ACT.Copy).then_inc(wt_ready, 2)

            def rows1(t, j):
                wait(act, xt_mm, t + 1)
                act.activation(xnT[:, j, :, :], tps[:, j, 0:KF * P].rearrange("p (k q) -> p k q", k=KF),
                               ACT.Copy).then_inc(xt_ready, 1)
                wait(act, h_mm, t + 1)
                act.activation(s_tab[:, cols(t, H)], big[:, 2 * j + 1, 0:H], ACT.Copy).then_inc(s_ready, 1)
                wait(act, biased, t - 1)
                act.activation(hraw[:, j, 0:HD], big[:, 2 * j, 0:HD], ACT.Copy)
                act.activation(hraw[:, j, HD:HR], big[:, 2 * j + 1, H:2 * H], ACT.Copy).then_inc(h_ready, 1)

            act.wait_ge(consts, 10)
            steps(act, NT, 0, rows1)

            def weights(a, layer):
                nh = H if layer == 0 else 1

                def step(g, j):
                    if is_in(g + 4, NG):
                        wait(act, a.hotT_mm, g + 5)
                        wait(act, a.src_mm, g + 3)
                        act.activation(hotT[:, j % 2, :, :], tps[:, j % 2, 0:GT * P].rearrange("p (u q) -> p u q", u=GT),
                                       ACT.Copy).then_inc(a.hotT, 1)
                    if is_in(g + 2, NG):
                        k = (j + 2) % 4
                        wait(act, a.lrel, g + 3)
                        wait(act, a.scaled, g - 1)
                        act.activation(ew[:, k, :, 0:nh], lrel[:, k, :, 0:nh], ACT.Exp, scale=-1.0).then_inc(a.exp, 1)
                    if layer == 0 and is_in(g + 1, NG):
                        k = (j + 1) % UG
                        wait(act, a.exp, g + 2)
                        wait(act, a.mm, g)
                        for u in range(GT):
                            for h in range(HV, H):
                                ins = act.activation(scaled1[:, k % 2, u, h * D:(h + 1) * D], got1[:, GT * k + u, h * D:(h + 1) * D],
                                                     ACT.Copy, scale=ew[:, k % 4, u, h:h + 1])
                        ins.then_inc(a.scaled_act, 1)

                group_steps(act, step)

            weights(agg[0], 0)

            def elu1(p, j):
                nq = pair(p)
                wait(act, x1t_mm, p + 1)
                wait(act, elu_u, p - 1)
                for c in range(KH):
                    z = (tps[:, 0:nq, c * P:(c + 1) * P], big[:, 2:2 + nq, c * P:(c + 1) * P])[j]
                    for to, func in ((ex1, ACT.Exp), (re1, ACT.Relu)):
                        ins = act.activation(to[:, j, 0:nq * HD].rearrange("p (q w) -> p q w", q=nq)[:, :, c * P:(c + 1) * P], z,
                                             func, bias=becol[:, c:c + 1], scale=gcol[:, c:c + 1])
                ins.then_inc(elu_act, 1)

            steps(act, NP, 0, elu1)

            weights(agg[1], 1)

            def elu2(b, j):
                wait(act, z_ready, b + 1)
                wait(act, u2_done, b)
                x2 = node[:, BT * j:BT * j + last1(b), 0:C]
                act.activation(expz[:, 0:last1(b), :], x2, ACT.Exp).then_inc(exp2_done, 1)
                wait(act, exp2_done, b + 1)
                act.activation(x2, x2, ACT.Relu).then_inc(elu2_act, 1)

            def xn2T_copies(b, j):
                for q in range(last1(b)):
                    wait(act, xn2T_mm, BT * b + q + 1)
                    if q == 0:
                        wait(act, up_mm, MC * (b - 1))
                    act.activation(xT[j][:, :, q * P:(q + 1) * P], tps[:, q % 2, 0:KF * P].rearrange("p (k q) -> p k q", k=KF),
                                   ACT.Copy).then_inc(xn2T_ready, 1)

            def nodes(b, j):
                nq = last1(b)
                if is_in(b + 1, NB1):
                    elu2(b + 1, 1 - j)
                wait(act, hr_mm[1], BT * b)
                for c in range(MC):
                    wait(act, up_mm, MC * b + c + 1)
                    act.activation(hT[:, c, 0:nq * P], big[:, c % 4, 0:nq * P], ACT.Gelu, bias=b1c[:, c:c + 1]).then_inc(up_ready, 1)
                if is_in(b + 1, NB1):
                    xn2T_copies(b + 1, 1 - j)
                if isinstance(b, int):
                    wait(act, hr_stored[j], 16 * (b // 2))
                else:
                    act.wait_ge(hr_stored[j], 8 * (b - j))
                for q in range(nq):
                    wait(act, hr_mm[0], BT * b + q + 1)
                    act.activation(hrows[:, BT * j + q, 0:HB], big[:, 2 * (q % 2), :], ACT.Copy).then_inc(hr_ready[0], 1)

            root(rstd[:, :], var[:, :])
            elu2(0, 0)
            xn2T_copies(0, 0)
            steps(act, NB1, 0, nodes, last=2)
            act.wait_ge(lexp_asked, 1)
            act.activation(lgx, lg, ACT.Exp).then_inc(lexp_done, 1)

            def expert_rows(b, j):
                for q in range(BT):
                    turn_back(act, BT * b + q, q, 0)

            steps(act, NB2, 0, expert_rows)

        @block.tensor
        def _(pe):
            pe.wait_ge(consts, 10)
            pe.wait_ge(cnt_ready, 1)
            pe.matmul(keyps[:, 0, 0:NT], ones[0:EP, :], cnt[0:EP, :], start=True, stop=True).then_inc(cnt_mm, 1)
            pe.wait_ge(w_in, 16 * (2 + 7 + 2 * H + 2))
            for c in range(2 * KH):
                if c >= 2:
                    pe.wait_ge(wt_ready, c - 1)
                for k in range(KF):
                    raw = wraw[:, c, k * P:(k + 1) * P] if c < KH else woraw[:, k, (c - KH) * P:(c - KH + 1) * P]
                    last = pe.transpose(tps[:, c % 2, k * P:(k + 1) * P], raw, ident[:, :])
                last.then_inc(wt_mm, 1)
            for k in range(KF):
                for c in range(KH):
                    pe.matmul(big[:, 1, k * 2 * H:(k + 1) * 2 * H], wraw[:, c, k * P:(k + 1) * P], amat[:, c, :],
                              start=(c == 0), stop=(c == KH - 1))
            for c in range(KH):
                pe.matmul(big[0:1, 2, 0:2 * H], bcol[:, c:c + 1], amat[:, c, :], start=(c == 0), stop=(c == KH - 1))
            for c in range(KH):
                for m in range(KF):
                    pe.matmul(big[:, 0, 2 * c:2 * c + 2], woraw[:, m, c * P:(c + 1) * P], a2[:, m, :],
                              start=(m == 0), stop=(m == KF - 1))
            for m in range(KF):
                last = pe.matmul(big[0:1, 3, 0:2], bocol[:, m:m + 1], a2[:, m, :], start=(m == 0), stop=(m == KF - 1))
            last.then_inc(wt_mm, 1)
            pe.wait_ge(wt_ready, 2 * KH + 4)
            pe.wait_ge(bh_in, 32)
            for c in range(KH):
                last = pe.matmul(big[0:1, 3, 0:C + 2], ones[:, 0:1], woT[:, c, :], start=(c == 0), stop=(c == KH - 1))
            last.then_inc(wt_mm, 1)
            pe.matmul(big[:, 0, 0:HD], ones[0:1, :], brow[:, 0:HD], start=True, stop=True)
            pe.matmul(big[:, 1, 0:2 * H], ones[0:1, :], brow[:, HD:HD + 2 * H], start=True, stop=True).then_inc(wt_mm, 1)

            def turn_x(t, j):
                wait(pe, xn_ready, t + 1)
                wait(pe, xt_ready, t - 1)
                for k in range(KF):
                    last = pe.transpose(tps[:, j, k * P:(k + 1) * P], xn[:, t, k * P:(k + 1) * P], ident[:, :])
                last.then_inc(xt_mm, 1)

            def h1(t, j):
                wait(pe, xt_ready, t + 1)
                wait(pe, h_ready, t - 1)
                for lo, n, bank in ((0, HD, 2 * j), (HD, 2 * H, 2 * j + 1)):
                    for k in range(KF):
                        last = pe.matmul(big[:, bank, 0:n], xnT[:, j, k, :], wT[:, k, lo:lo + n], start=(k == 0), stop=(k == KF - 1))
                last.then_inc(h_mm, 1)

            pe.wait_ge(br2_ready, 1)
            pe.wait_ge(wt_ready, 2 * KH + 6)

            turns = 0
            before = NT - 2 * len(E_TURNS)
            for t in range(NT):
                turn_x(t, t % 2)
                h1(t, t % 2)
                if t >= before and (t - before) % 2 == 0:
                    c = E_TURNS[turns]
                    turns += 1
                    pe.wait_ge(turn_asked, turns)
                    for b in range(SC // P):
                        last = pe.transpose(keyps[:, b // 4, (b % 4) * P:(b % 4 + 1) * P], keys[c][:, b * P:(b + 1) * P],
                                            ident[:, :])
                    last.then_inc(turned, 1)
            assert turns == len(E_TURNS)

            def sums_of(a, layer):
                nh, width, got, tab = (H, HD, got1, s_parts) if layer == 0 else (1, C, got2, s_parts)
                pe.wait_ge(s_split, layer + 1)

                windows = Windows(pe, win_pe, 3)

                def step(g, j):
                    windows.load(g, j)
                    if is_in(g + 4, NG):
                        k = (j + 4) % UG
                        wait(pe, a.hot, g + 5)
                        wait(pe, a.hotT, g + 3)
                        for u in range(GT):
                            last = pe.transpose(tps[:, k % 2, u * P:(u + 1) * P], hot[:, k, u, :], ident[:, :])
                        last.then_inc(a.hotT_mm, 1)
                    if is_in(g + 3, NG):
                        k = (j + 3) % UG
                        w = windows.of(g, j)
                        wait(pe, a.hotT, g + 4)
                        wait(pe, a.score, g + 2)
                        for u in range(GT):
                            for part in range(3):
                                last = pe.matmul(big[:, 2 + k % 2, u * nh:(u + 1) * nh], hotT[:, k % 2, u, :],
                                                 tab[:, bass.ds(w * (3 * nh) + part * nh, nh)], start=(part == 0), stop=(part == 2))
                        last.then_inc(a.src_mm, 1)
                    if is_in(g, NG):
                        wait(pe, a.scaled, g + 1)
                        if layer == 0:
                            wait(pe, a.scaled_act, g + 1)
                        wait(pe, a.added, g - 1)
                        for u in range(GT):
                            if layer == 0:
                                lhs, rhs = hot[:, j, u, :], scaled1[:, j % 2, u, :]
                            else:
                                lhs, rhs = scaled2[:, j % 2, u, :], got[:, GT * j + u, 0:C]
                            last = pe.matmul(big[:, j % 2, 0:width], lhs, rhs, start=(u == 0), stop=(u == GT - 1))
                        last.then_inc(a.mm, 1)

                group_steps(pe, step)

            sums_of(agg[0], 0)

            def h2(p, j):
                if is_in(p, NP):
                    wait(pe, x1_scaled, p + 1)
                    wait(pe, elu_act, p - 1)
                    for q in range(pair(p)):
                        for c in range(KH):
                            at = q * HD + c * P
                            last = pe.transpose((tps[:, q, c * P:(c + 1) * P], big[:, 2 + q, c * P:(c + 1) * P])[j],
                                                x1s[:, j, at:at + P], ident[:, :])
                    last.then_inc(x1t_mm, 1)
                if isinstance(p, int) and p == 0:
                    pe.matmul(keyps[:, 0, 0:C + 2], ones[0:1, :], brow2[:, :], start=True, stop=True).then_inc(bias2_mm, 1)
                if is_in(p - 1, NP):
                    k = 1 - j
                    nq = pair(p - 1)
                    wait(pe, elu_u, p)
                    if isinstance(p, int) and p == 1:
                        pe.wait_ge(bias2_ready, 1)
                    wait(pe, h2_ready, p - 2)
                    for q in range(nq):
                        for c in range(KH):
                            at = q * HD + c * P
                            last = pe.matmul((big, keyps)[k][:, q, 0:C + 2], u1[:, k, at:at + P], woT[:, c, :],
                                             start=(c == 0), stop=(c == KH - 1))
                    last.then_inc(h2_mm, 1)

            steps(pe, NP, 1, h2, first=4)
            sums_of(agg[1], 1)

            pe.wait_ge(w1_in, 16)

            def xn2_turns(b, j):
                for q in range(last1(b)):
                    wait(pe, xn2_ready, BT * b + q + 1)
                    wait(pe, xn2T_ready, BT * b + q - 1)
                    for k in range(KF):
                        last = pe.transpose(tps[:, q % 2, k * P:(k + 1) * P], xn2[:, BT * j + q, k * P:(k + 1) * P], ident[:, :])
                    last.then_inc(xn2T_mm, 1)

            def logit_batch(b, j):
                nq = last1(b)
                wait(pe, xn2T_ready, BT * b + nq)
                for c in range(MC):
                    wait(pe, up_ready, MC * b + c - 3)
                    if c < 4:
                        wait(pe, hr_ready[c % 2], BT * (b - 1) + 3 + c // 2)
                    for k in range(KF):
                        last = pe.matmul(big[:, c % 4, 0:nq * P], w1_sb[:, k, c * P:(c + 1) * P], xT[j][:, k, 0:nq * P],
                                         start=(k == 0), stop=(k == KF - 1))
                    last.then_inc(up_mm, 1)
                if is_in(b + 1, NB1):
                    xn2_turns(b + 1, 1 - j)
                wait(pe, up_ready, MC * (b + 1))
                wait(pe, lgT_ready, b)
                for c in range(MC):
                    lo = c % 4 * CG
                    last = pe.matmul(keyps[lo:lo + CG, 0, 0:nq * P], wg_cg[:, c, :], hT[:, c, 0:nq * P],
                                     start=(c < 4), stop=(c >= MC - 4), tile_position=(0, lo))
                last.then_inc(lg_mm, 1)
                for q in range(nq):
                    for h in range(2):
                        wait(pe, hr_ready[h], BT * b + q - 1)
                        for c in range(MC // 2):
                            last = pe.transpose(big[:, 2 * (q % 2) + h, c * P:(c + 1) * P], hT[:, h * MC // 2 + c, q * P:(q + 1) * P], ident[:, :])
                        last.then_inc(hr_mm[h], 1)

            def logit_turn(b, j):
                wait(pe, lgT_ready, b + 1)
                wait(pe, lg_ready, b)
                for q in range(last1(b)):
                    last = pe.transpose(keyps[:, 1, q * P:(q + 1) * P], lgT[:, q * P:(q + 1) * P], ident[:, :])
                last.then_inc(lgt_mm, 1)

            def logit_both(b, j):
                logit_batch(b, j)
                logit_turn(b, j)

            xn2_turns(0, 0)
            steps(pe, NB1, 0, logit_both, last=2)
            pe.wait_ge(cnt_ready, 2)
            pe.matmul(keyps[:, 0, 0:NE], ones[:, :], cnt_e[:, :], start=True, stop=True).then_inc(cnt_mm, 1)
            for n, c in enumerate(T_TURNS):
                turns += 1
                pe.wait_ge(turn_asked, turns)
                if n % 2 == 0:
                    pe.transpose(keyps[0:TC, 0, 0:P], tkeys[c][:, 0:TC], ident[:, :]).then_inc(turned, 1)
                else:
                    pe.transpose(keyps[:, 0, 0:TC], tkeys[c][0:TC, :], ident[0:TC, 0:TC]).then_inc(turned, 1)

            pe.wait_ge(wd_in, 16 * NE)
            pe.wait_ge(order_dec, 1)

            def turn_rows(b, j, q):
                if isinstance(b, int):
                    pe.wait_ge(tok_in[BT * j + q], 16 * (b // 2 + 1))
                else:
                    pe.wait_ge(tok_in[BT * j + q], 8 * (b - j) + 16)
                for h in range(2):
                    wait(pe, et_ready[h], BT * b + q - 1)
                    for c in range(MC // 2):
                        lo = C + 2 + h * HB + c * P
                        last = pe.transpose(big[:, 2 * (q % 2) + h, c * P:(c + 1) * P], tok[:, BT * j + q, lo:lo + P], ident[:, :])
                    last.then_inc(et_mm[h], 1)

            def expert_tile(t, q):
                e = pe.value_load(exp_c[0:1, cols(t, 1)], min_val=0, max_val=(NE - 1) * MC * C)
                wait(pe, y_biased, t - 1)
                for h in range(2):
                    wait(pe, et_ready[h], t + 1)
                for c in range(MC):
                    last = pe.matmul(keyps[:, q % 2, 0:C], hT[:, c, q * P:(q + 1) * P], wd_sb[:, bass.ds(e + c * C, C)],
                                     start=(c == 0), stop=(c == MC - 1))
                last.then_inc(y_mm, 1)

            def expert_batch(b, j):
                for q in range(BT):
                    turn_rows(b, j, q)
                    if is_in(BT * b + q - 1, TT):
                        expert_tile(BT * b + q - 1, (q - 1) % BT)

            steps(pe, NB2, 0, expert_batch)
            expert_tile(TT - 1, BT - 1)


_INS = ['x', 'src', 'dst', 'L0_gnn_W_heads', 'L0_gnn_b_heads', 'L0_gnn_a_heads', 'L0_gnn_g_heads', 'L0_gnn_beta_heads',
        'L0_gnn_W_out', 'L0_gnn_b_out', 'L0_gnn_a_out', 'L0_gnn_g_out', 'L0_gnn_beta_out',
        'L0_ffn_W1', 'L0_ffn_b1', 'L0_ffn_Wg', 'L0_ffn_bg', 'L0_ffn_Wd', 'L0_ffn_bd']
_OUTS = [((6250, 256), 'float32')]


def kernel(**inputs):
    import numpy as _np
    import concourse.bacc as _bacc
    from concourse import mybir as _mybir
    from concourse.bass_utils import run_bass_kernel_spmd as _run

    nc = _bacc.Bacc("TRN2", target_bir_lowering=False, num_devices=1)
    arrays, args = {}, []
    for name in _INS:
        a = _np.ascontiguousarray(inputs[name])
        arrays[f"in_{name}_dram"] = a
        args.append(nc.dram_tensor(f"in_{name}_dram", a.shape, _mybir.dt.from_np(a.dtype), kind="ExternalInput").ap())
    for i, (shape, dtype) in enumerate(_OUTS):
        dt = _mybir.dt.from_np(_np.dtype(dtype))
        args.append(nc.dram_tensor(f"out_{i}_dram", shape, dt, kind="ExternalOutput").ap())
    build(nc, *args)
    r = _run(nc, [arrays], core_ids=[0])
    return r.results[0]["out_0_dram"]
```
